# Optimizing a Trainium2 kernel written in Bass

```python
import numpy as np
import jax
import jax.numpy as jnp

def _softmax(x, axis=-1):
    return jax.nn.softmax(x, axis=axis)

def _gelu(x):
    return jax.nn.gelu(x, approximate=True)

def _silu(x):
    return jax.nn.silu(x)

def _sigmoid(x):
    return jax.nn.sigmoid(x)

def _layernorm(x, axis=-1, eps=1e-05):
    m = jnp.mean(x, axis=axis, keepdims=True)
    v = jnp.var(x, axis=axis, keepdims=True)
    return (x - m) / jnp.sqrt(v + eps)

def _scatter_add(tgt, idx, src, axis=0):
    return tgt.at[idx].add(src)

def _segment_sum(src, seg, n):
    return jax.ops.segment_sum(src, seg, n)
kernel_name = 'mk_vit_tower_d2_tok_img768_r4_2d0731'

def setup_inputs(seed: int=0):
    np.random.seed(seed)
    _w = jnp.asarray

    def _rec_inputs():
        import jax
        import jax.numpy as jnp
        _rk = jax.random.key(seed)
        x = -0.000356955 + 1 * jax.random.normal(jax.random.fold_in(_rk, 1), (64, 3, 112, 112), jnp.float32)
        return x
    x = _rec_inputs()

    def _L0_tok_setup():
        import jax, jax.numpy as jnp
        import numpy as np
        EPS = 1e-05

        def _layernorm(x, gamma, beta):
            mu = jnp.mean(x, axis=-1, keepdims=True)
            var = jnp.mean(jnp.square(x - mu), axis=-1, keepdims=True)
            return (x - mu) * jax.lax.rsqrt(var + EPS) * gamma + beta
        key = jax.random.key(seed)
        ks = jax.random.split(key, 6)
        B, C, H, P, D = (128, 3, 224, 16, 192)
        patch_dim = C * P * P
        x = jax.random.normal(ks[0], (B, C, H, H), dtype=jnp.float32)
        ln1_g = jnp.ones((patch_dim,), jnp.float32)
        ln1_b = jnp.zeros((patch_dim,), jnp.float32)
        W = jax.random.normal(ks[1], (patch_dim, D), dtype=jnp.float32) * (1.0 / np.sqrt(patch_dim))
        b = jax.random.normal(ks[2], (D,), dtype=jnp.float32) * 0.01
        ln2_g = jnp.ones((D,), jnp.float32)
        ln2_b = jnp.zeros((D,), jnp.float32)
        return {'x': x, 'ln1_g': ln1_g, 'ln1_b': ln1_b, 'W': W, 'b': b, 'ln2_g': ln2_g, 'ln2_b': ln2_b}
    _L0_tok_all = _L0_tok_setup()
    _L0_tok_in = {k: v for k, v in _L0_tok_all.items() if k in ('ln1_g', 'ln1_b', 'W', 'b', 'ln2_g', 'ln2_b')}
    del _L0_tok_all

    def _L0_attn_setup():
        import jax, jax.numpy as jnp
        import numpy as np
        DIM = 192
        GP_NUM = 49
        key = jax.random.key(seed)
        ks = jax.random.split(key, 7)
        b, n, d = (16, 256, DIM)
        s = d ** (-0.5)
        x = jax.random.normal(ks[0], (b, n, d), dtype=jnp.float32)
        W_qkv = jax.random.normal(ks[1], (d, 3 * d), dtype=jnp.float32) * s
        b_qkv = jnp.zeros((3 * d,), dtype=jnp.float32)
        W_proj = jax.random.normal(ks[2], (d, d), dtype=jnp.float32) * s
        b_proj = jnp.zeros((d,), dtype=jnp.float32)
        W_gp = jax.random.normal(ks[3], (d, GP_NUM), dtype=jnp.float32) * s
        alpha = jnp.zeros((1,), dtype=jnp.float32)
        return {'x': x, 'W_qkv': W_qkv, 'b_qkv': b_qkv, 'W_proj': W_proj, 'b_proj': b_proj, 'W_gp': W_gp, 'alpha': alpha}
    _L0_attn_all = _L0_attn_setup()
    _L0_attn_in = {k: v for k, v in _L0_attn_all.items() if k in ('W_qkv', 'b_qkv', 'W_proj', 'b_proj', 'W_gp', 'alpha')}
    del _L0_attn_all

    def _L0_ffn_setup():
        import jax, jax.numpy as jnp
        import numpy as np
        B, S, D = (2, 256, 192)
        NF, NR, R, DS, K = (128, 128, 128, 64, 4)

        @jax.checkpoint
        def feature_fn(x, neurons, weights):
            all_h = jnp.einsum('bsd,ndr->bsnr', x, neurons)
            return jnp.einsum('bsnr,bsn->bsr', all_h, weights)

        @jax.checkpoint
        def restore_fn(h, neurons, weights):
            all_out = jnp.einsum('bsr,nrd->bsnd', h, neurons)
            return jnp.einsum('bsnd,bsn->bsd', all_out, weights)

        def topk_sparsify(weights, k):
            topk_vals, topk_idx = jax.lax.top_k(weights, k)
            N = weights.shape[-1]
            one_hot_mask = jax.nn.one_hot(topk_idx, N, dtype=weights.dtype)
            sparse = (one_hot_mask * topk_vals[..., jnp.newaxis]).sum(axis=-2)
            sparse = sparse / (sparse.sum(axis=-1, keepdims=True) + 1e-08)
            return (sparse, topk_idx)
        key = jax.random.key(seed)
        ks = jax.random.split(key, 8)
        x = jax.random.normal(ks[0], (B, S, D), jnp.float32)
        f_know = jax.random.normal(ks[1], (NF, D, R), jnp.float32) * 0.02
        r_know = jax.random.normal(ks[2], (NR, R, D), jnp.float32) * 0.02
        W_fk = jax.random.normal(ks[3], (D, DS), jnp.float32) * 0.02
        b_fk = jnp.zeros((DS,), jnp.float32)
        W_rk = jax.random.normal(ks[4], (D, DS), jnp.float32) * 0.02
        b_rk = jnp.zeros((DS,), jnp.float32)
        emb_fk = jax.random.normal(ks[5], (NF, DS), jnp.float32) * 0.02
        emb_rk = jax.random.normal(ks[6], (NR, DS), jnp.float32) * 0.02
        return {'x': x, 'f_know': f_know, 'r_know': r_know, 'W_fk': W_fk, 'b_fk': b_fk, 'W_rk': W_rk, 'b_rk': b_rk, 'emb_fk': emb_fk, 'emb_rk': emb_rk}
    _L0_ffn_all = _L0_ffn_setup()
    _L0_ffn_in = {k: v for k, v in _L0_ffn_all.items() if k in ('f_know', 'r_know', 'W_fk', 'b_fk', 'W_rk', 'b_rk', 'emb_fk', 'emb_rk')}
    del _L0_ffn_all

    def _L1_attn_setup():
        import jax, jax.numpy as jnp
        import numpy as np
        DIM = 192
        NUM_HEADS = 12
        HEAD_DIM = DIM // NUM_HEADS
        SPARSITY_RATIO = 0.5
        key = jax.random.key(seed)
        ks = jax.random.split(key, 6)
        B, N = (4, 256)
        x = jax.random.normal(ks[0], (B, N, DIM), dtype=jnp.float32)
        s = 1.0 / np.sqrt(DIM)
        qkv_w = jax.random.uniform(ks[1], (3 * DIM, DIM), jnp.float32, -s, s)
        qkv_b = jax.random.uniform(ks[2], (3 * DIM,), jnp.float32, -s, s)
        proj_w = jax.random.uniform(ks[3], (DIM, DIM), jnp.float32, -s, s)
        proj_b = jax.random.uniform(ks[4], (DIM,), jnp.float32, -s, s)
        temperature = jnp.ones((1,), jnp.float32) * 0.1
        return {'x': x, 'qkv_w': qkv_w, 'qkv_b': qkv_b, 'proj_w': proj_w, 'proj_b': proj_b, 'temperature': temperature}
    _L1_attn_all = _L1_attn_setup()
    _L1_attn_in = {k: v for k, v in _L1_attn_all.items() if k in ('qkv_w', 'qkv_b', 'proj_w', 'proj_b', 'temperature')}
    del _L1_attn_all

    def _L1_ffn_setup():
        import jax, jax.numpy as jnp
        import numpy as np
        CAPACITY_FACTOR = 1.25
        key = jax.random.key(seed)
        ks = jax.random.split(key, 5)
        B, S, D, F, E = (8, 512, 192, 768, 8)
        return {'x': jax.random.normal(ks[0], (B, S, D), jnp.float32), 'switch_w': jax.random.normal(ks[1], (D, E), jnp.float32) * 0.02, 'switch_b': jnp.zeros((E,), jnp.float32), 'w1': jax.random.normal(ks[2], (E, D, F), jnp.float32) * 0.02, 'b1': jnp.zeros((E, F), jnp.float32), 'w2': jax.random.normal(ks[3], (E, F, D), jnp.float32) * 0.02, 'b2': jnp.zeros((E, D), jnp.float32)}
    _L1_ffn_all = _L1_ffn_setup()
    _L1_ffn_in = {k: v for k, v in _L1_ffn_all.items() if k in ('switch_w', 'switch_b', 'w1', 'b1', 'w2', 'b2')}
    del _L1_ffn_all
    return {'x': x, 'L0_tok_ln1_g': _L0_tok_in['ln1_g'], 'L0_tok_ln1_b': _L0_tok_in['ln1_b'], 'L0_tok_W': _L0_tok_in['W'], 'L0_tok_b': _L0_tok_in['b'], 'L0_tok_ln2_g': _L0_tok_in['ln2_g'], 'L0_tok_ln2_b': _L0_tok_in['ln2_b'], 'L0_attn_W_qkv': _L0_attn_in['W_qkv'], 'L0_attn_b_qkv': _L0_attn_in['b_qkv'], 'L0_attn_W_proj': _L0_attn_in['W_proj'], 'L0_attn_b_proj': _L0_attn_in['b_proj'], 'L0_attn_W_gp': _L0_attn_in['W_gp'], 'L0_attn_alpha': _L0_attn_in['alpha'], 'L0_ffn_f_know': _L0_ffn_in['f_know'], 'L0_ffn_r_know': _L0_ffn_in['r_know'], 'L0_ffn_W_fk': _L0_ffn_in['W_fk'], 'L0_ffn_b_fk': _L0_ffn_in['b_fk'], 'L0_ffn_W_rk': _L0_ffn_in['W_rk'], 'L0_ffn_b_rk': _L0_ffn_in['b_rk'], 'L0_ffn_emb_fk': _L0_ffn_in['emb_fk'], 'L0_ffn_emb_rk': _L0_ffn_in['emb_rk'], 'L1_attn_qkv_w': _L1_attn_in['qkv_w'], 'L1_attn_qkv_b': _L1_attn_in['qkv_b'], 'L1_attn_proj_w': _L1_attn_in['proj_w'], 'L1_attn_proj_b': _L1_attn_in['proj_b'], 'L1_attn_temperature': _L1_attn_in['temperature'], 'L1_ffn_switch_w': _L1_ffn_in['switch_w'], 'L1_ffn_switch_b': _L1_ffn_in['switch_b'], 'L1_ffn_w1': _L1_ffn_in['w1'], 'L1_ffn_b1': _L1_ffn_in['b1'], 'L1_ffn_w2': _L1_ffn_in['w2'], 'L1_ffn_b2': _L1_ffn_in['b2']}

def reference(x, L0_tok_ln1_g, L0_tok_ln1_b, L0_tok_W, L0_tok_b, L0_tok_ln2_g, L0_tok_ln2_b, L0_attn_W_qkv, L0_attn_b_qkv, L0_attn_W_proj, L0_attn_b_proj, L0_attn_W_gp, L0_attn_alpha, L0_ffn_f_know, L0_ffn_r_know, L0_ffn_W_fk, L0_ffn_b_fk, L0_ffn_W_rk, L0_ffn_b_rk, L0_ffn_emb_fk, L0_ffn_emb_rk, L1_attn_qkv_w, L1_attn_qkv_b, L1_attn_proj_w, L1_attn_proj_b, L1_attn_temperature, L1_ffn_switch_w, L1_ffn_switch_b, L1_ffn_w1, L1_ffn_b1, L1_ffn_w2, L1_ffn_b2):
    import jax
    import jax.numpy as jnp

    def _L0_tok_ref(x, ln1_g, ln1_b, W, b, ln2_g, ln2_b):
        import jax, jax.numpy as jnp
        import numpy as np
        EPS = 1e-05

        def _layernorm(x, gamma, beta):
            mu = jnp.mean(x, axis=-1, keepdims=True)
            var = jnp.mean(jnp.square(x - mu), axis=-1, keepdims=True)
            return (x - mu) * jax.lax.rsqrt(var + EPS) * gamma + beta
        B, C, H, Wd = x.shape
        P = 16
        h, w = (H // P, Wd // P)
        patches = x.reshape(B, C, h, P, w, P)
        patches = patches.transpose(0, 2, 4, 3, 5, 1)
        patches = patches.reshape(B, h * w, P * P * C)
        y = _layernorm(patches, ln1_g, ln1_b)
        y = jnp.einsum('bnp,pd->bnd', y, W) + b
        return _layernorm(y, ln2_g, ln2_b)

    def _L0_attn_ref(x, W_qkv, b_qkv, W_proj, b_proj, W_gp, alpha):
        import jax, jax.numpy as jnp
        import numpy as np
        DIM = 192
        GP_NUM = 49
        d = x.shape[-1]
        scale = d ** (-0.5)
        qkv = x @ W_qkv + b_qkv
        q, k, v = jnp.split(qkv, 3, axis=-1)
        scores = jnp.einsum('bnd,bmd->bnm', q, k) * scale
        attn = jax.nn.softmax(scores, axis=-1)
        gw = jax.nn.softmax(q @ W_gp, axis=-1)
        group = jnp.einsum('bng,bmg->bnm', gw, gw)
        a = jax.nn.sigmoid(alpha)
        weights = attn * (a + (1.0 - a) * group)
        out = jnp.einsum('bnm,bmd->bnd', weights, v)
        return out @ W_proj + b_proj

    def _L0_ffn_ref(x, f_know, r_know, W_fk, b_fk, W_rk, b_rk, emb_fk, emb_rk):
        import jax, jax.numpy as jnp
        import numpy as np
        B, S, D = (2, 256, 192)
        NF, NR, R, DS, K = (128, 128, 128, 64, 4)

        @jax.checkpoint
        def feature_fn(x, neurons, weights):
            all_h = jnp.einsum('bsd,ndr->bsnr', x, neurons)
            return jnp.einsum('bsnr,bsn->bsr', all_h, weights)

        @jax.checkpoint
        def restore_fn(h, neurons, weights):
            all_out = jnp.einsum('bsr,nrd->bsnd', h, neurons)
            return jnp.einsum('bsnd,bsn->bsd', all_out, weights)

        def topk_sparsify(weights, k):
            topk_vals, topk_idx = jax.lax.top_k(weights, k)
            N = weights.shape[-1]
            one_hot_mask = jax.nn.one_hot(topk_idx, N, dtype=weights.dtype)
            sparse = (one_hot_mask * topk_vals[..., jnp.newaxis]).sum(axis=-2)
            sparse = sparse / (sparse.sum(axis=-1, keepdims=True) + 1e-08)
            return (sparse, topk_idx)
        emb_fk_n = emb_fk / (jnp.linalg.norm(emb_fk, axis=-1, keepdims=True) + 1e-08)
        emb_rk_n = emb_rk / (jnp.linalg.norm(emb_rk, axis=-1, keepdims=True) + 1e-08)
        logits_fk = jnp.einsum('bsd,nd->bsn', x @ W_fk + b_fk, emb_fk_n)
        logits_rk = jnp.einsum('bsd,nd->bsn', x @ W_rk + b_rk, emb_rk_n)
        w_fk, _ = topk_sparsify(jax.nn.softmax(logits_fk, axis=-1), K)
        w_rk, _ = topk_sparsify(jax.nn.softmax(logits_rk, axis=-1), K)
        h = feature_fn(x, f_know, w_fk)
        out = restore_fn(h, r_know, w_rk)
        return out

    def _L1_attn_ref(x, qkv_w, qkv_b, proj_w, proj_b, temperature):
        import jax, jax.numpy as jnp
        import numpy as np
        DIM = 192
        NUM_HEADS = 12
        HEAD_DIM = DIM // NUM_HEADS
        SPARSITY_RATIO = 0.5
        B, N, C = x.shape
        scale = HEAD_DIM ** (-0.5)
        k_keep = max(1, int(N * SPARSITY_RATIO))
        qkv = (x @ qkv_w.T + qkv_b).reshape(B, N, 3, NUM_HEADS, HEAD_DIM)
        qkv = jnp.transpose(qkv, (2, 0, 3, 1, 4))
        q, k, v = (qkv[0], qkv[1], qkv[2])
        temp = jnp.clip(temperature, 0.01, None)
        q = q / temp
        scores = jnp.einsum('bhnd,bhmd->bhnm', q, k) * scale
        thresh = jax.lax.top_k(scores, k_keep)[0][..., -1:]
        scores = jnp.where(scores >= thresh, scores, -jnp.inf)
        probs = jax.nn.softmax(scores, axis=-1)
        out = jnp.einsum('bhnm,bhmd->bhnd', probs, v)
        out = jnp.transpose(out, (0, 2, 1, 3)).reshape(B, N, C)
        return out @ proj_w.T + proj_b

    def _L1_ffn_ref(x, switch_w, switch_b, w1, b1, w2, b2):
        import jax, jax.numpy as jnp
        import numpy as np
        CAPACITY_FACTOR = 1.25
        B, S, D = x.shape
        E = w1.shape[0]
        xf = x.reshape(-1, D)
        N = xf.shape[0]
        capacity = int(CAPACITY_FACTOR * N / E)
        probs = jax.nn.softmax(xf @ switch_w + switch_b, axis=-1)
        prob_max = jnp.max(probs, axis=-1)
        routes = jnp.argmax(probs, axis=-1)
        sort_idx = jnp.lexsort((-prob_max, routes))
        counts = jnp.bincount(routes, length=E)
        starts = jnp.concatenate([jnp.zeros((1,), counts.dtype), jnp.cumsum(counts)[:-1]])
        rank_sorted = jnp.arange(N) - starts[routes[sort_idx]]
        rank = jnp.zeros((N,), jnp.int32).at[sort_idx].set(rank_sorted.astype(jnp.int32))
        keep = rank < capacity
        dest_e = jnp.where(keep, routes, E)
        dest_c = jnp.where(keep, rank, 0)
        buf = jnp.zeros((E + 1, capacity, D), xf.dtype).at[dest_e, dest_c].set(xf)
        h = jax.nn.gelu(jnp.einsum('ecd,edf->ecf', buf[:E], w1) + b1[:, None, :], approximate=False)
        o = jnp.einsum('ecf,efd->ecd', h, w2) + b2[:, None, :]
        y_exp = o[routes, dest_c]
        y = jnp.where(keep[:, None], y_exp, xf)
        out = y * prob_max[:, None]
        return out.reshape(B, S, D)
    h = _L0_tok_ref(x, L0_tok_ln1_g, L0_tok_ln1_b, L0_tok_W, L0_tok_b, L0_tok_ln2_g, L0_tok_ln2_b)
    h = h + _L0_attn_ref(_layernorm(h, axis=-1), L0_attn_W_qkv, L0_attn_b_qkv, L0_attn_W_proj, L0_attn_b_proj, L0_attn_W_gp, L0_attn_alpha)
    h = h + _L0_ffn_ref(_layernorm(h, axis=-1), L0_ffn_f_know, L0_ffn_r_know, L0_ffn_W_fk, L0_ffn_b_fk, L0_ffn_W_rk, L0_ffn_b_rk, L0_ffn_emb_fk, L0_ffn_emb_rk)
    h = h + _L1_attn_ref(_layernorm(h, axis=-1), L1_attn_qkv_w, L1_attn_qkv_b, L1_attn_proj_w, L1_attn_proj_b, L1_attn_temperature)
    h = h + _L1_ffn_ref(_layernorm(h, axis=-1), L1_ffn_switch_w, L1_ffn_switch_b, L1_ffn_w1, L1_ffn_b1, L1_ffn_w2, L1_ffn_b2)
    return h

_drawn_inputs = setup_inputs


def setup_inputs(seed=0):
    import zlib

    import numpy as np

    out = dict(_drawn_inputs(seed))
    spreads = {'L0_tok_ln1_g': (1.0, 0.2),
     'L0_tok_ln1_b': (0.0, 0.1),
     'L0_tok_ln2_g': (1.0, 0.2),
     'L0_tok_ln2_b': (0.0, 0.1),
     'L0_attn_b_qkv': (0.0, 0.1),
     'L0_attn_b_proj': (0.0, 0.1),
     'L0_ffn_b_fk': (0.0, 0.444),
     'L0_ffn_b_rk': (0.0, 0.428),
     'L1_ffn_switch_b': (0.0, 0.1),
     'L1_ffn_b1': (0.0, 0.8),
     'L1_ffn_b2': (0.0, 0.488)}
    factors = {'L0_tok_b': 3.793,
     'L0_attn_W_gp': 8.0,
     'L0_ffn_f_know': 2.805,
     'L0_ffn_r_know': 2.684,
     'L0_ffn_W_fk': 2.699,
     'L0_ffn_W_rk': 2.702,
     'L0_ffn_emb_fk': 2.721,
     'L0_ffn_emb_rk': 2.748,
     'L1_ffn_w1': 4.341,
     'L1_ffn_w2': 3.99}
    for name, (base, spread) in spreads.items():
        noise = np.random.default_rng([zlib.crc32(name.encode()), seed]).standard_normal(out[name].shape)
        drawn = base * np.exp(spread * noise) if base else spread * noise
        out[name] = jnp.asarray(drawn.astype(out[name].dtype))
    for name, factor in factors.items():
        out[name] = (out[name] * factor).astype(out[name].dtype)
    return out
```

```python
from contextlib import ExitStack

import concourse.bass as bass
from concourse import mybir

ALU = mybir.AluOpType
ACT = mybir.ActivationFunctionType
AX = mybir.AxisListType
F32 = mybir.dt.float32
I32 = mybir.dt.int32
U32 = mybir.dt.uint32

P = 128
IMAGES = 64
SEQ = 49
TOKENS = IMAGES * SEQ
TILES = -(-TOKENS // P)
PADDED = TILES * P
LAST = TOKENS - (TILES - 1) * P
GROUP = 5
TURNS = TILES // GROUP
D = 192
DH = D // 2
PATCH = 768
PCH = PATCH // P
PAIRS = IMAGES // 2
SLOT = 64
COLS = (IMAGES + 2) * SLOT
EPS = 1e-5


EXPERTS = 8
HIDDEN = 768
CAPACITY = int(1.25 * TOKENS / EXPERTS)
EXPERT_SLOTS = -(-CAPACITY // P) * P
MOE_SLOTS = EXPERTS * EXPERT_SLOTS
ROUNDS = 7
HEADS = 12
HEAD = D // HEADS
LOWEST, HIGHEST = -3.0e38, 3.0e38
R2 = 64
NEURONS = 128
NT_RING = 12
X_CHUNKS = 3
SLOT_TILES = -(-(4 * PADDED // P + NEURONS - 1) // NT_RING) * NT_RING


class Program:

    def __init__(self, nc, ctx):
        self.nc, self.ctx = nc, ctx
        self.of_stage, self.cleared = [], []
        self.software = {name: [nc.alloc_semaphore(f"{name}{i}") for i in range(n)] for name, n in (
            ("scatter0_sent", 1), ("nt0_stored", X_CHUNKS), ("comb0_gathered", GROUP), ("comb0_sent", 1),
            ("nt1_stored", X_CHUNKS), ("comb1_gathered", GROUP), ("comb1_sent", 1), ("moe_sent", 1), ("ex_stored", 2),
            ("fin_gathered", GROUP))}

    def sb(self, name, shape, dt=F32):
        return self.ctx.enter_context(self.nc.sbuf_tensor(name, shape, dt))

    def bank(self, name):
        return self.ctx.enter_context(self.nc.psum_tensor(name, [P, 512], F32))

    def lasting(self, name):
        return self.nc.alloc_semaphore(name)

    def sem(self, name):
        self.of_stage.append(self.nc.alloc_semaphore(name))
        return self.of_stage[-1]

    def stage(self, build, *args):
        self.of_stage = []
        build(self.nc, self, *args)
        for sem in self.cleared:
            self.nc.release_semaphore(sem)
        for sem in self.of_stage:
            self.nc.gpsimd.sem_clear(sem)
        self.cleared = self.of_stage


def row_to_all(dram_row, n, parts=P):
    return dram_row.rearrange("(a n) -> a n", a=1).broadcast_to([parts, n])


def load_constants(nc, p, m, a):
    s = m.sems
    for n in ("c_tok", "c_rows", "c_attn0", "c_ffn0", "c_attn1", "c_moe", "c_masks", "c_fill", "c_fill_moe", "c_ident", "out_stored"):
        s[n] = p.lasting(n)
    s["c_x"] = [p.lasting(f"c_x{g}") for g in range(TURNS)]
    with nc.Block() as block:

        @block.sync
        def _(sp):
            for g in range(TURNS):
                t0 = g * GROUP
                n = GROUP if g < TURNS - 1 else GROUP - 1
                sp.dma_start(m.x_all[:, t0:t0 + n, :],
                             a["x"][t0 * P:(t0 + n) * P, :].rearrange("(t q) d -> q t d", q=P)).then_inc(s["c_x"][g], 16)
            for half in range(2):
                sp.dma_start(m.x_all[half * LAST:(half + 1) * LAST, TILES - 1, :],
                             a["x"][(TILES - 1) * P:TOKENS, :]).then_inc(s["c_x"][TURNS - 1], 16)

        @block.scalar
        def _(act):
            act.dma_start(m.w_tok[:, :, :], a["L0_tok_W"].rearrange("(c q) d -> q c d", q=P)).then_inc(s["c_tok"], 16)
            act.dma_start(m.g1[:, :], a["L0_tok_ln1_g"]).then_inc(s["c_tok"], 16)
            act.dma_start(m.b1[:, :], a["L0_tok_ln1_b"]).then_inc(s["c_tok"], 16)
            for name, dst in (("L0_tok_b", m.r_btok), ("L0_tok_ln2_g", m.r_g2), ("L0_tok_ln2_b", m.r_b2)):
                act.dma_start(dst[:, :], row_to_all(a[name], D)).then_inc(s["c_rows"], 16)

        @block.gpsimd
        def _(pool):
            pool.memset(m.ident[:, :], 0.0).then_inc(s["c_ident"], 1)
            pool.memset(m.minus_half[:, :], -0.5)
            pool.memset(m.plus_half[:, :], 0.5)
            pool.memset(m.ones[:, :], 1.0)
            pool.memset(m.zeros[:, :], 0.0).then_inc(s["c_ident"], 1)
            pool.wait_ge(s["c_ident"], 2)
            pool.affine_select(out=m.ident[:, :], in_=m.ident[:, :], compare_op=ALU.not_equal, fill=1.0,
                               base=0, pattern=[[-1, P]], channel_multiplier=1).then_inc(s["c_ident"], 1)


def load_later(sp, m, a):
    s = m.sems
    half = lambda w: w.rearrange("(h q) n -> q h n", h=2)
    for dst, src in ((m.w_qkv0[:, :, :], half(a["L0_attn_W_qkv"])), (m.w_gp[:, :, :], half(a["L0_attn_W_gp"])),
                     (m.w_proj0[:, :, :], half(a["L0_attn_W_proj"])), (m.b_qk0[:, :], a["L0_attn_b_qkv_cols"]),
                     (m.alpha[:, :], row_to_all(a["L0_attn_alpha"], 1)),
                     (m.r_bv0[:, :], row_to_all(a["L0_attn_b_qkv"][2 * D:3 * D], D)),
                     (m.r_bproj0[:, :], row_to_all(a["L0_attn_b_proj"], D))):
        sp.dma_start(dst, src).then_inc(s["c_attn0"], 16)
        m.n_attn0 += 16
    sp.dma_start(m.pair_row[:, :], a["c_pair_row"]).then_inc(s["c_masks"], 16)
    sp.dma_start(m.pair_bar[:, :], a["c_pair_bar"]).then_inc(s["c_masks"], 16)
    for dst, src in ((m.iota[:, :], row_to_all(a["c_iota"], 2 * P)), (m.upto[:, :], a["c_upto"]),
                     (m.w_route[:, :, 0:R2], a["L0_ffn_W_fk"].rearrange("(h q) n -> q h n", h=2)),
                     (m.w_route[:, :, R2:2 * R2], a["L0_ffn_W_rk"].rearrange("(h q) n -> q h n", h=2)),
                     (m.b_route[0:R2, :], a["L0_ffn_b_fk"].rearrange("(q a) -> q a", a=1)),
                     (m.b_route[R2:2 * R2, :], a["L0_ffn_b_rk"].rearrange("(q a) -> q a", a=1)),
                     (m.emb[:, 0:R2], a["L0_ffn_emb_fk"]), (m.emb[:, R2:2 * R2], a["L0_ffn_emb_rk"])):
        sp.dma_start(dst, src).then_inc(s["c_ffn0"], 16)
        m.n_ffn0 += 16
    for dst, src in ((m.w_switch[:, :, :], a["L1_ffn_switch_w"].rearrange("(h q) n -> q h n", h=2)),
                     (m.r_switch[:, :], row_to_all(a["L1_ffn_switch_b"], EXPERTS)),
                     (m.b_up[:, :, :], a["L1_ffn_b1"]), (m.group_ones[:, :], a["c_group_ones"]),
                     (m.threshold[:, :], a["c_threshold"]), (m.slot_base[:, :], a["c_slot_base"]),
                     (m.own_row[:, :], a["c_own_row"])):
        sp.dma_start(dst, src).then_inc(s["c_moe"], 16)
        m.n_moe += 16
    for dst, src in ((m.w_qkv1[:, :, :], half(a["L1_attn_qkv_w"])), (m.w_proj1[:, :, :], half(a["L1_attn_proj_w"])),
                     (m.b_qk1[:, :], a["L1_attn_qkv_b"][:, 0:4]), (m.b_v1[:, :], a["L1_attn_qkv_b"][:, 4:6]),
                     (m.r_bproj1[:, :], row_to_all(a["L1_attn_proj_b"], D)),
                     (m.score_scale[:, :], row_to_all(a["L1_attn_temperature"], 1)),
                     (m.head_mask[:, :], a["c_head_mask"])):
        sp.dma_start(dst, src).then_inc(s["c_attn1"], 16)
        m.n_attn1 += 16

    sp.wait_ge(s["c_ident"], 2)
    for g in range(TURNS):
        sp.wait_ge(s["c_x"][g], 16 if g < TURNS - 1 else 48)
    sp.wait_ge(s["c_rows"], 48)
    for dram, n in ((m.fk_in, D), (m.rk_in, NEURONS)):
        sp.dma_start(dram.rearrange("(t q) d -> q t d", q=P),
                     m.zeros[:, 0:n].unsqueeze(1).broadcast_to([P, SLOT_TILES, n])).then_inc(s["c_fill"], 16)
    sp.dma_start(m.moe_in[0:MOE_SLOTS, :].rearrange("(t q) d -> q t d", q=P),
                 m.zeros[:, 0:D].unsqueeze(1).broadcast_to([P, MOE_SLOTS // P, D])).then_inc(s["c_fill_moe"], 16)


def tiles(t0, n=1):
    return bass.ds(t0, n)


def one(ap):
    return ap.rearrange("q a n -> q (a n)")


def rstd_of_variance(pool, m, mv, rstd, now, n, sem, before):
    pool.tensor_scalar(rstd[:, now], mv[:, now, 1], EPS, None, ALU.add).then_inc(sem, 1)
    pool.wait_ge(sem, before + 1)
    pool.tensor_tensor(rstd[:, now], rstd[:, now], m.minus_half[:, 0:n], ALU.pow).then_inc(sem, 1)
    pool.wait_ge(sem, before + 2)


def row_statistics(dve, m, mv, g, rows_ready, part, aggregated, stats, passed):
    bn = m.bn[:, 64:64 + GROUP * 6].rearrange("q (j n) -> q j n", j=GROUP)
    dve.wait_ge(*rows_ready).then_inc(passed, 1)
    for j in range(GROUP):
        ins = dve.bn_stats(bn[:, j, :], m.h[:, tiles(g * GROUP + j), :])
    ins.then_inc(part, 1)
    dve.wait_ge(part, g + 1).then_inc(passed, 1)
    for j in range(GROUP):
        ins = dve.bn_aggr(m.mv_group[:, j, :], bn[:, j, :])
    ins.then_inc(aggregated, 1)
    dve.wait_ge(aggregated, g + 1)
    dve.tensor_copy(mv[:, tiles(g * GROUP, GROUP), :], m.mv_group[:, :, :]).then_inc(stats, 1)
    dve.wait_ge(stats, g + 1)


def patch_tokens(nc, p, m, a):
    s = m.sems
    folded, bias_ready, stats_part, stats_ready, rstd_step, shift_ready, xn_ready, turned, xt_ready, y_ready, \
        y_biased, y_part, y_stats, aggregated, y_aggregated, passed = [p.sem("tok_" + n) for n in (
            "folded", "bias_ready", "stats_part", "stats_ready", "rstd_step", "shift_ready", "xn_ready", "turned",
            "xt_ready", "y_ready", "y_biased", "y_part", "y_stats", "aggregated", "y_aggregated", "passed")]
    xt = m.xt_patches
    bn = m.bn[:, 0:GROUP * 12].rearrange("q (j n) -> q j n", j=GROUP)

    def xt_ps(j, lo, hi):
        bank = m.bank[2 * (j % 2) + lo // 4]
        return bank[:, (lo % 4) * P:(lo % 4 + hi - lo) * P]

    def y_ps(j):
        return m.bank[4 + j % 4][:, 0:D]

    with nc.Block() as block:

        @block.sync
        def _(sp):
            load_later(sp, m, a)

        @block.vector
        def _(dve):
            def patch_stats(g):
                for j in range(GROUP):
                    for h in range(2):
                        ins = dve.bn_stats(bn[:, j, 6 * h:6 * h + 6],
                                           m.x_all[:, tiles(g * GROUP + j), h * 384:(h + 1) * 384])
                ins.then_inc(stats_part, 1)
                dve.wait_ge(stats_part, g + 1).then_inc(passed, 1)
                for j in range(GROUP):
                    ins = dve.bn_aggr(m.mv_group[:, j, :], bn[:, j, :])
                ins.then_inc(aggregated, 1)
                dve.wait_ge(aggregated, g + 1)
                dve.tensor_copy(m.mv[:, tiles(g * GROUP, GROUP), :], m.mv_group[:, :, :]).then_inc(stats_ready, 1)
                dve.wait_ge(stats_ready, g + 1).then_inc(passed, 1)

            def token_rows(g):
                for j in range(GROUP):
                    dve.wait_ge(y_ready, g * GROUP + j + 1)
                    dve.tensor_tensor(one(m.h[:, tiles(g * GROUP + j), :]), y_ps(j), m.r_btok[:, :],
                                      ALU.add).then_inc(y_biased, 1)
                row_statistics(dve, m, m.mv2, g, (y_biased, g * GROUP + GROUP), y_part, y_aggregated, y_stats, passed)

            dve.wait_ge(s["c_x"][0], 16)
            patch_stats(0)

            dve.wait_ge(s["c_tok"], 48)
            dve.wait_ge(s["c_rows"], 48)
            dve.wait_ge(bias_ready, 1)
            dve.tensor_tensor(m.r_btok[:, :], m.r_btok[:, :], m.bank[7][:, 0:D], ALU.add)
            for c in range(PCH):
                ins = dve.tensor_scalar(m.w_tok[:, c, :], m.w_tok[:, c, :], m.g1[:, c:c + 1], None, ALU.mult)
            ins.then_inc(folded, 1)

            AHEAD = 3
            for g in range(1, AHEAD):
                dve.wait_ge(s["c_x"][g], 16)
                patch_stats(g)
            for g in range(AHEAD, TURNS):
                dve.wait_ge(s["c_x"][g], 16 if g < TURNS - 1 else 48)
            with dve.Fori(0, TURNS - AHEAD) as g:
                token_rows(g)
                patch_stats(g + AHEAD)
            for g in range(TURNS - AHEAD, TURNS):
                token_rows(g)

        @block.gpsimd
        def _(pool):
            for g in range(TURNS):
                now = slice(g * GROUP, (g + 1) * GROUP)
                pool.wait_ge(stats_ready, g + 1)
                rstd_of_variance(pool, m, m.mv, m.rstd, now, GROUP, rstd_step, 2 * g)
                pool.tensor_tensor(m.shift[:, now], m.mv[:, now, 0], m.rstd[:, now], ALU.mult).then_inc(shift_ready, 1)
                pool.wait_ge(shift_ready, 2 * g + 1)
                pool.tensor_scalar(m.shift[:, now], m.shift[:, now], -1.0, None, ALU.mult).then_inc(shift_ready, 1)

        @block.scalar
        def _(act):
            def normalise(g, j):
                act.wait_ge(shift_ready, 2 * g + 2)
                act.activation(m.xn_patches[:, j, :], one(m.x_all[:, tiles(g * GROUP + j), :]), ACT.Identity, bias=m.shift[:, tiles(g * GROUP + j)],
                               scale=m.rstd[:, tiles(g * GROUP + j)]).then_inc(xn_ready, 1)

            def lift(g, j, before):
                act.wait_ge(turned, g * GROUP + j + 1)
                if before is not None:
                    act.wait_ge(y_ready, before + j + 1)
                act.activation(xt[:, j, 0:4 * P], xt_ps(j, 0, 4), ACT.Copy)
                act.activation(xt[:, j, 4 * P:6 * P], xt_ps(j, 4, 6), ACT.Copy).then_inc(xt_ready, 1)

            for j in range(GROUP):
                normalise(0, j)
            for j in range(GROUP):
                lift(0, j, None)
                normalise(1, j)
            with act.Fori(0, TURNS - 2) as g:
                for j in range(GROUP):
                    lift(g + 1, j, g * GROUP)
                    normalise(g + 2, j)
            for j in range(GROUP):
                lift(TURNS - 1, j, (TURNS - 2) * GROUP)

        @block.tensor
        def _(pe):
            pe.wait_ge(s["c_tok"], 48)
            for c in range(PCH):
                mm = pe.matmul(m.bank[7][:, 0:D], m.b1[:, c:c + 1].broadcast_to([P, P]), m.w_tok[:, c, :],
                               start=(c == 0), stop=(c == PCH - 1))
            mm.then_inc(bias_ready, 1)

            def turn(g, j):
                pe.wait_ge(xn_ready, g * GROUP + j + 1)
                pe.wait_ge(xt_ready, g * GROUP + (j - 1 if j >= 2 else 0))
                for c in range(PCH):
                    mm = pe.transpose(xt_ps(j, c, c + 1), m.xn_patches[:, j, c * P:(c + 1) * P],
                                      m.ident[:, :])
                mm.then_inc(turned, 1)

            def project(g, j):
                pe.wait_ge(xt_ready, g * GROUP + j + 1)
                pe.wait_ge(y_biased, g * GROUP + j // 4)
                for c in range(PCH):
                    mm = pe.matmul(y_ps(j), xt[:, j, c * P:(c + 1) * P], m.w_tok[:, c, :],
                                   start=(c == 0), stop=(c == PCH - 1))
                mm.then_inc(y_ready, 1)

            pe.wait_ge(s["c_ident"], 3)
            pe.wait_ge(folded, 1)
            turn(0, 0)
            with pe.Fori(0, TURNS - 1) as g:
                for j in range(GROUP):
                    turn(g + (j + 1) // GROUP, (j + 1) % GROUP)
                    project(g, j)
            for j in range(GROUP):
                if j + 1 < GROUP:
                    turn(TURNS - 1, j + 1)
                project(TURNS - 1, j)


def token_norm(nc, p, m):
    s = m.sems
    rstd_step, centred, scaled, shifted, part, aggregated, stats, passed = [p.sem("tn_" + n) for n in (
        "rstd_step", "centred", "scaled", "shifted", "part", "aggregated", "stats", "passed")]

    with nc.Block() as block:

        @block.gpsimd
        def _(pool):
            rstd_of_variance(pool, m, m.mv2, m.rstd, slice(0, TILES), TILES, rstd_step, 0)

        @block.vector
        def _(dve):
            gamma = m.r_g2[:, :].unsqueeze(1).broadcast_to([P, GROUP, D])
            beta = m.r_b2[:, :].unsqueeze(1).broadcast_to([P, GROUP, D])
            dve.wait_ge(rstd_step, 2)
            with dve.Fori(0, TURNS) as g:
                rows = m.h[:, tiles(g * GROUP, GROUP), :]
                for j in range(GROUP):
                    t = tiles(g * GROUP + j)
                    ins = dve.tensor_scalar(one(m.h[:, t, :]), one(m.h[:, t, :]), one(m.mv2[:, t, 0:1]),
                                            m.rstd[:, t], ALU.subtract, ALU.mult)
                ins.then_inc(centred, 1)
                dve.wait_ge(centred, g + 1)
                dve.tensor_tensor(rows, rows, gamma, ALU.mult).then_inc(scaled, 1)
                dve.wait_ge(scaled, g + 1)
                dve.tensor_tensor(rows, rows, beta, ALU.add).then_inc(shifted, 1)
                row_statistics(dve, m, m.mv, g, (shifted, g + 1), part, aggregated, stats, passed)


def norm_and_turn(nc, p, m, name, xn, xt):
    rstd_step, xn_ready, turned, lifted = [p.sem(f"{name}_{n}") for n in ("rstd_step", "xn_ready", "turned", "lifted")]

    with nc.Block() as block:

        @block.gpsimd
        def _(pool):
            rstd_of_variance(pool, m, m.mv, m.rstd, slice(0, TILES), TILES, rstd_step, 0)

        @block.vector
        def _(dve):
            dve.wait_ge(rstd_step, 2)
            with dve.Fori(0, TURNS) as g:
                for j in range(GROUP):
                    now = tiles(g * GROUP + j)
                    dve.tensor_scalar(one(xn[:, now, :]), one(m.h[:, now, :]), one(m.mv[:, now, 0:1]), m.rstd[:, now],
                                      ALU.subtract, ALU.mult).then_inc(xn_ready, 1)

        @block.tensor
        def _(pe):
            for t in range(TILES):
                pe.wait_ge(xn_ready, t + 1)
                if t >= GROUP:
                    pe.wait_ge(lifted, t - GROUP + 1)
                for c in range(2):
                    mm = pe.transpose(m.bank[t % GROUP][0:DH, c * P:(c + 1) * P], xn[:, t, c * DH:(c + 1) * DH],
                                      m.ident[:, :])
                mm.then_inc(turned, 1)

        @block.scalar
        def _(act):
            with act.Fori(0, TURNS) as g:
                for j in range(GROUP):
                    act.wait_ge(turned, g * GROUP + j + 1)
                    act.activation(xt[:, :, bass.ds((g * GROUP + j) * P, P)],
                                   m.bank[j][0:DH, 0:2 * P].rearrange("q (c n) -> q c n", c=2),
                                   ACT.Copy).then_inc(lifted, 1)


def project_qk(nc, p, m, name, w, bias, weights_loaded):
    ready, q_out, k_out, x_out = [p.sem(f"{name}_{n}") for n in ("ready", "q_out", "k_out", "x_out")]
    PER = 8
    N = PER * SEQ

    def by_image(x, h, c):
        return x[:, h, bass.ds((c * PER + 1) * SLOT, PER * SLOT)].rearrange("q (i k) -> q i k", k=SLOT)[:, :, 0:SEQ]

    with nc.Block() as block:

        @block.tensor
        def _(pe):
            pe.wait_ge(*weights_loaded)
            with pe.Fori(0, IMAGES // PER) as c:
                for o in range(4):
                    pe.wait_ge(q_out if o < 2 else k_out, 2 * c)
                    for h in range(2):
                        mm = pe.matmul(m.bank[o][0:DH, 0:N], w[:, h, o * DH:(o + 1) * DH],
                                       m.xt[:, h, bass.ds(c * N, N)], start=(h == 0), stop=(h == 1))
                    mm.then_inc(ready, 1)

        @block.scalar
        def _(act):
            act.wait_ge(*weights_loaded)
            with act.Fori(0, IMAGES // PER) as c:
                for o in range(2):
                    act.wait_ge(ready, 4 * c + o + 1)
                    act.activation(by_image(m.qt, o, c), m.bank[o][0:DH, 0:N].rearrange("q (i k) -> q i k", k=SEQ),
                                   ACT.Identity, bias=bias[:, o:o + 1]).then_inc(q_out, 1)

        @block.vector
        def _(dve):
            dve.wait_ge(*weights_loaded)
            for x in (m.qt, m.kt, m.xs):
                dve.memset(x[:, :, :].rearrange("q h (i k) -> q h i k", k=SLOT)[:, :, :, SEQ:SLOT], 0.0)
            with dve.Fori(0, IMAGES // PER) as c:
                for o in range(2):
                    dve.wait_ge(ready, 4 * c + o + 3)
                    dve.tensor_scalar(by_image(m.kt, o, c), m.bank[2 + o][0:DH, 0:N].rearrange("q (i k) -> q i k", k=SEQ),
                                      bias[:, 2 + o:3 + o], None, ALU.add).then_inc(k_out, 1)

        @block.gpsimd
        def _(pool):
            with pool.Fori(0, IMAGES // PER) as c:
                for h in range(2):
                    pool.tensor_copy(by_image(m.xs, h, c),
                                     m.xt[:, h, bass.ds(c * N, N)].rearrange("q (i k) -> q i k", k=SEQ)).then_inc(x_out, 1)


def pair_columns(x, h, i):
    return x[:, h, (2 * i + 1) * SLOT:(2 * i + 3) * SLOT]


def group_attention(nc, p, m):
    s = m.sems
    names = ("scores_ready", "row_max", "shift_ready", "v_out", "group_exp", "score_exp", "group_sum", "group_weights",
             "groups_turned", "groups_out", "group_ready", "mixed", "sum_inverse", "weights_ready", "weights_turned",
             "weights_out", "heads_ready", "heads_out", "gate", "v_ready")
    (scores_ready, row_max, shift_ready, v_out, group_exp, score_exp, group_sum, group_weights, groups_turned,
     groups_out, group_ready, mixed, sum_inverse, weights_ready, weights_turned, weights_out, heads_ready,
     heads_out, gate, v_ready) = [p.sem("a0_" + n) for n in names]
    SCALE = float(D) ** -0.5
    with ExitStack() as mem:
        sb = lambda n, shape: mem.enter_context(nc.sbuf_tensor("a0_" + n, shape, F32))
        v = sb("v", [P, 2, D])
        probs = sb("probs", [P, 2, P])
        weights = sb("weights", [P, P])
        weights_t = sb("weights_t", [P, P])
        mix = sb("mix", [P, P])
        ge = sb("ge", [P, 2, SEQ])
        gw = sb("gw", [P, 2, SEQ])
        gw_t = sb("gw_t", [SEQ, P])
        peak = sb("peak", [P, 2, 2])
        shift = sb("shift", [P, 2, 2])
        total = sb("total", [P, 2, 2])
        inverse = sb("inverse", [P, 2, 2])
        a_col = sb("a_col", [P, 3])
        S, GL, V, GT, G, WT, O = [m.bank[0], m.bank[1]], m.bank[2], m.bank[3], m.bank[4], m.bank[5], m.bank[6], m.bank[7]

        with nc.Block() as block:

            @block.tensor
            def _(pe):
                def scores(i):
                    if i >= 2:
                        pe.wait_ge(score_exp, i - 1)
                    if i >= 1:
                        pe.wait_ge(group_exp, i)
                    for h in range(2):
                        pe.matmul(S[i % 2][:, 0:P], pair_columns(m.qt, h, i), pair_columns(m.kt, h, i),
                                  start=(h == 0), stop=False)
                    pe.matmul(S[i % 2][:, 0:P], m.pair_row[:, :], m.pair_bar[:, :], start=False, stop=True)
                    for h in range(2):
                        mm = pe.matmul(GL[:, 0:SEQ], pair_columns(m.qt, h, i), m.w_gp[:, h, :], start=(h == 0), stop=(h == 1))
                    mm.then_inc(scores_ready, 1)

                def values(i):
                    if i:
                        pe.wait_ge(v_out, i)
                    for h in range(2):
                        mm = pe.matmul(V[:, 0:D], pair_columns(m.xs, h, i), m.w_qkv0[:, h, 2 * D:3 * D],
                                       start=(h == 0), stop=(h == 1))
                    mm.then_inc(v_ready, 1)

                def turn_groups(i):
                    pe.wait_ge(group_weights, i + 1)
                    if i:
                        pe.wait_ge(groups_out, i)
                    pe.transpose(GT[0:SEQ, 0:P], gw[:, i % 2, :], m.ident[:, :]).then_inc(groups_turned, 1)

                def group(i):
                    pe.wait_ge(groups_out, i + 1)
                    if i:
                        pe.wait_ge(mixed, i)
                    pe.matmul(G[:, 0:P], gw_t[:, :], gw_t[:, :], start=True, stop=True).then_inc(group_ready, 1)

                def turn_weights(i):
                    pe.wait_ge(weights_ready, i + 1)
                    if i:
                        pe.wait_ge(weights_out, i)
                    pe.transpose(WT[:, 0:P], weights[:, :], m.ident[:, :]).then_inc(weights_turned, 1)

                def heads(i):
                    pe.wait_ge(weights_out, i + 1)
                    if i:
                        pe.wait_ge(heads_out, i)
                    for h in range(2):
                        mm = pe.matmul(O[0:DH, h * P:(h + 1) * P], v[:, i % 2, h * DH:(h + 1) * DH], weights_t[:, :],
                                       start=True, stop=True)
                    mm.then_inc(heads_ready, 1)

                pe.wait_ge(s["c_attn0"], m.n_attn0)
                pe.wait_ge(s["c_masks"], 32)
                scores(0)
                values(0)
                turn_groups(0)
                for i in range(PAIRS):
                    group(i)
                    if i + 1 < PAIRS:
                        scores(i + 1)
                    turn_weights(i)
                    if i + 1 < PAIRS:
                        values(i + 1)
                        turn_groups(i + 1)
                    heads(i)

            def over_pairs(eng, before, body, ahead):
                before()
                with eng.Fori(0, PAIRS // 2 - 1) as g:
                    for u in range(2):
                        body(2 * g + u, u, lambda: ahead(2 * g + u + 1, 1 - u))
                body(PAIRS - 2, 0, lambda: ahead(PAIRS - 1, 1))
                body(PAIRS - 1, 1, lambda: None)

            @block.vector
            def _(dve):
                dve.wait_ge(gate, 1)
                dve.tensor_scalar(a_col[:, 1:2], a_col[:, 0:1], 1.0, None, ALU.add).then_inc(gate, 1)
                dve.wait_ge(gate, 2)
                dve.reciprocal(a_col[:, 0:1], a_col[:, 1:2]).then_inc(gate, 1)
                dve.wait_ge(gate, 3)
                dve.tensor_scalar(a_col[:, 1:2], a_col[:, 0:1], -1.0, 1.0, ALU.mult, ALU.add).then_inc(gate, 1)
                dve.wait_ge(gate, 4)

                def maxima(i, u, first=False):
                    dve.wait_ge(scores_ready, i + 1)
                    dve.reduce_max(peak[:, u, 0:1], S[u][:, 0:P], AX.X)
                    dve.reduce_max(peak[:, u, 1:2], GL[:, 0:SEQ], AX.X).then_inc(row_max, 1)
                    dve.wait_ge(row_max, i + 1)
                    dve.tensor_scalar(shift[:, u, 0:1], peak[:, u, 0:1], -SCALE, None, ALU.mult)
                    dve.tensor_scalar(shift[:, u, 1:2], peak[:, u, 1:2], -1.0, None, ALU.mult).then_inc(shift_ready, 1)
                    dve.wait_ge(group_exp, i + 1)
                    dve.reciprocal(inverse[:, u, 1:2], total[:, u, 1:2]).then_inc(group_sum, 1)
                    dve.wait_ge(group_sum, i + 1)
                    dve.tensor_scalar(gw[:, u, :], ge[:, u, :], inverse[:, u, 1:2], None, ALU.mult).then_inc(group_weights, 1)
                    dve.wait_ge(v_ready, i + 1)
                    if not first:
                        dve.wait_ge(heads_ready, i - 1)
                    dve.tensor_tensor(v[:, u, :], V[:, 0:D], m.r_bv0[:, :], ALU.add).then_inc(v_out, 1)

                def mix_in(i, u, ahead):
                    dve.wait_ge(group_ready, i + 1)
                    dve.tensor_scalar(mix[:, :], G[:, 0:P], a_col[:, 1:2], a_col[:, 0:1], ALU.mult, ALU.add)\
                        .then_inc(mixed, 1)
                    dve.wait_ge(score_exp, i + 1)
                    dve.reciprocal(inverse[:, u, 0:1], total[:, u, 0:1]).then_inc(sum_inverse, 1)
                    dve.wait_ge(sum_inverse, i + 1)
                    dve.wait_ge(mixed, i + 1)
                    dve.wait_ge(weights_turned, i)
                    dve.scalar_tensor_tensor(weights[:, :], mix[:, :], inverse[:, u, 0:1], probs[:, u, :], ALU.mult,
                                             ALU.mult).then_inc(weights_ready, 1)
                    ahead()

                over_pairs(dve, lambda: maxima(0, 0, True), mix_in, maxima)

            @block.scalar
            def _(act):
                act.wait_ge(s["c_attn0"], m.n_attn0)
                act.activation(a_col[:, 0:1], m.alpha[:, :], ACT.Exp, scale=-1.0).then_inc(gate, 1)

                def exps(i, u):
                    act.wait_ge(shift_ready, i + 1)
                    act.activation(ge[:, u, :], GL[:, 0:SEQ], ACT.Exp, bias=shift[:, u, 1:2],
                                   accum_out=total[:, u, 1:2]).then_inc(group_exp, 1)
                    act.activation(probs[:, u, :], S[u][:, 0:P], ACT.Exp, bias=shift[:, u, 0:1], scale=SCALE,
                                   accum_out=total[:, u, 0:1]).then_inc(score_exp, 1)

                def lift_groups(i, u):
                    act.wait_ge(groups_turned, i + 1)
                    act.wait_ge(group_ready, i)
                    act.activation(gw_t[:, :], GT[0:SEQ, 0:P], ACT.Copy).then_inc(groups_out, 1)

                def body(i, u, ahead):
                    act.wait_ge(weights_turned, i + 1)
                    act.wait_ge(heads_ready, i)
                    act.activation(weights_t[:, :], WT[:, 0:P], ACT.Copy).then_inc(weights_out, 1)
                    ahead()
                    for x in pending:
                        lift_groups(*x)
                    pending.clear()
                    act.wait_ge(heads_ready, i + 1)
                    src = O[0:DH, 0:2 * P].rearrange("q (h a k) -> q h a k", h=2, a=2)
                    dst = m.at[:, :, bass.ds(i * 2 * SEQ, 2 * SEQ)].rearrange("q h (a k) -> q h a k", a=2)
                    for h in range(2):
                        ins = act.activation(dst[:, h], src[:, h, :, 0:SEQ], ACT.Copy)
                    ins.then_inc(heads_out, 1)

                def ahead(i, u):
                    exps(i, u)
                    pending.append((i, u))

                pending = []

                def both(i, u, nxt):
                    body(i, u, nxt)

                def before():
                    exps(0, 0)
                    lift_groups(0, 0)

                over_pairs(act, before, both, ahead)


def output_projection(nc, p, m, name, w, r_bias):
    ready, with_bias, added, part, aggregated, stats, passed = [p.sem(f"{name}_{n}") for n in (
        "ready", "with_bias", "added", "part", "aggregated", "stats", "passed")]

    with nc.Block() as block:

        @block.tensor
        def _(pe):
            for t in range(TILES):
                if t >= GROUP:
                    pe.wait_ge(added, t - GROUP + 1)
                for h in range(2):
                    mm = pe.matmul(m.bank[t % GROUP][:, 0:D], m.at[:, h, t * P:(t + 1) * P], w[:, h, :],
                                   start=(h == 0), stop=(h == 1))
                mm.then_inc(ready, 1)

        @block.gpsimd
        def _(pool):
            with pool.Fori(0, TURNS) as g:
                rows = m.h[:, tiles(g * GROUP, GROUP), :]
                pool.tensor_tensor(rows, rows, r_bias[:, :].unsqueeze(1).broadcast_to([P, GROUP, D]), ALU.add)\
                    .then_inc(with_bias, 1)

        @block.vector
        def _(dve):
            with dve.Fori(0, TURNS) as g:
                dve.wait_ge(with_bias, g + 1)
                for j in range(GROUP):
                    dve.wait_ge(ready, g * GROUP + j + 1)
                    row = one(m.h[:, tiles(g * GROUP + j), :])
                    dve.tensor_tensor(row, row, m.bank[j][:, 0:D], ALU.add).then_inc(added, 1)
                row_statistics(dve, m, m.mv, g, (added, g * GROUP + GROUP), part, aggregated, stats, passed)


def over_tiles(eng, tile):
    with eng.Fori(0, TILES // 2) as g:
        for b in range(2):
            tile(g, b)
    tile(TILES // 2, 0)


def embeddings(nc, p, m):
    s = m.sems
    step, pstep, turned = [p.sem("emb_" + n) for n in ("step", "pstep", "turned")]
    norm = m.bn[:, 64:66]

    with nc.Block() as block:

        @block.vector
        def _(dve):
            dve.wait_ge(s["c_ffn0"], m.n_ffn0)
            for r in range(2):
                ins = dve.tensor_tensor_reduce(m.squares[:, r * R2:(r + 1) * R2], m.emb[:, r * R2:(r + 1) * R2],
                                               m.emb[:, r * R2:(r + 1) * R2], 1.0, 0.0, ALU.mult, ALU.add,
                                               norm[:, r:r + 1])
            ins.then_inc(step, 1)
            dve.wait_ge(pstep, 2)
            dve.reciprocal(norm, norm).then_inc(step, 1)
            dve.wait_ge(step, 2)
            for r in range(2):
                ins = dve.tensor_scalar(m.emb[:, r * R2:(r + 1) * R2], m.emb[:, r * R2:(r + 1) * R2], norm[:, r:r + 1],
                                        None, ALU.mult)
            ins.then_inc(step, 1)
            dve.wait_ge(turned, 1)
            dve.tensor_copy(m.emb_t[:, :], m.bank[0][:, 0:P])

        @block.gpsimd
        def _(pool):
            pool.wait_ge(step, 1)
            pool.tensor_tensor(norm, norm, m.plus_half[:, 0:2], ALU.pow).then_inc(pstep, 1)
            pool.wait_ge(pstep, 1)
            pool.tensor_scalar(norm, norm, 1e-8, None, ALU.add).then_inc(pstep, 1)

        @block.tensor
        def _(pe):
            pe.wait_ge(step, 3)
            pe.transpose(m.bank[0][:, 0:P], m.emb[:, :], m.ident[:, :]).then_inc(turned, 1)


def route(nc, p, m):
    (z_ready, z_out, logits_ready, top, index, shifted, exp_done, mark, four_set, hot, hot_turned, hot_out, less, e4, dsum,
     denom, inverse, passed) = [p.sem("route_" + n) for n in (
         "z_ready", "z_out", "logits_ready", "top", "index", "shifted", "exp_done", "mark", "four_set", "hot",
         "hot_turned", "hot_out", "less", "e4", "dsum", "denom", "inverse", "passed")]
    N = PADDED // 8
    with ExitStack() as mem:
        sb = lambda n, shape, dt=F32: mem.enter_context(nc.sbuf_tensor("route_" + n, shape, dt))
        top8 = sb("top8", [P, 2, 2, 8])
        index8 = sb("index8", [P, 2, 2, 8], U32)
        scratch = sb("scratch", [P, 2, 2, P])
        shift = sb("shift", [P, TILES, 2])
        total = sb("total", [P, TILES, 2])
        sum4 = sb("sum4", [P, TILES, 2])
        onehot = sb("onehot", [P, 2, 2, P])
        marked = sb("marked", [P, 2, P])
        four = sb("four", [P, 2, 2, 8])
        zt = m.zt

        with nc.Block() as block:

            @block.tensor
            def _(pe):
                with pe.Fori(0, 4) as c:
                    for b in range(2):
                        pe.wait_ge(z_out, 2 * c)
                        for h in range(2):
                            mm = pe.matmul(m.bank[b][:, 0:N], m.w_route[:, h, :], m.xt[:, h, bass.ds((2 * c + b) * N, N)],
                                           start=(h == 0), stop=(h == 1))
                        mm.then_inc(z_ready, 1)
                pe.wait_ge(z_out, 8)

                def turn(t):
                    for r in range(2):
                        pe.wait_ge(hot, 2 * t + r + 1)
                        if t >= 2:
                            pe.wait_ge(hot_out, 2 * (t - 2) + r + 1)
                        pe.transpose(m.bank[4 + 2 * r + t % 2][:, 0:P], onehot[:, t % 2, r, :], m.ident[:, :])\
                            .then_inc(hot_turned, 1)
                for t in range(TILES):
                    for r in range(2):
                        if t >= 2:
                            pe.wait_ge(exp_done, 2 * (t - 2) + r + 1)
                        q = slice(r * R2, (r + 1) * R2)
                        pe.matmul(m.bank[2 * (t % 2) + r][:, 0:P], zt[q, t * P:(t + 1) * P], m.emb_t[q, :],
                                  start=True, stop=True).then_inc(logits_ready, 1)
                    if t:
                        turn(t - 1)
                turn(TILES - 1)

            @block.scalar
            def _(act):
                with act.Fori(0, 4) as c:
                    for b in range(2):
                        act.wait_ge(z_ready, 2 * c + b + 1)
                        act.activation(zt[:, bass.ds((2 * c + b) * N, N)], m.bank[b][:, 0:N], ACT.Identity,
                                       bias=m.b_route[:, :]).then_inc(z_out, 1)

                def tile(g, b):
                    t = 2 * g + b
                    for r in range(2):
                        act.wait_ge(shifted, t + 1)
                        act.wait_ge(exp_done, 4 * g)
                        act.activation(scratch[:, b, r, :], m.bank[2 * b + r][:, 0:P], ACT.Exp,
                                       bias=one(shift[:, tiles(t), r:r + 1]),
                                       accum_out=one(total[:, tiles(t), r:r + 1])).then_inc(exp_done, 1)
                    for r in range(2):
                        act.wait_ge(hot_turned, 2 * t + r + 1)
                        act.activation(m.chosen[r][:, bass.ds(t * P, P)], m.bank[4 + 2 * r + b][:, 0:P],
                                       ACT.Copy).then_inc(hot_out, 1)

                over_tiles(act, tile)
                act.wait_ge(less, TILES)
                act.activation(m.w4[:, :, :, :], m.w4[:, :, :, :], ACT.Exp).then_inc(e4, 1)

            @block.vector
            def _(dve):
                dve.memset(four[:, :, :, :], LOWEST).then_inc(four_set, 1)
                dve.wait_ge(four_set, 1)

                def tile(g, b):
                    t = 2 * g + b
                    for r in range(2):
                        dve.wait_ge(logits_ready, 2 * t + r + 1).then_inc(passed, 1)
                        ins = dve.max(top8[:, b, r, :], m.bank[2 * b + r][:, 0:P])
                    ins.then_inc(top, 1)
                    dve.wait_ge(top, t + 1).then_inc(passed, 1)
                    for r in range(2):
                        ins = dve.max_index(index8[:, b, r, :], top8[:, b, r, :], m.bank[2 * b + r][:, 0:P])
                    ins.then_inc(index, 1)
                    dve.tensor_copy(four[:, b, :, 0:4], top8[:, b, :, 0:4]).then_inc(four_set, 1)
                    dve.tensor_tensor(m.w4[:, tiles(t), :, :].rearrange("q a r k -> q (a r) k"), top8[:, b, :, 0:4],
                                      top8[:, b, :, 0:1].broadcast_to([P, 2, 4]), ALU.subtract).then_inc(less, 1)
                    dve.wait_ge(four_set, t + 2).then_inc(passed, 1)
                    for r in range(2):
                        ins = dve.match_replace(marked[:, r, :], four[:, b, r, :], m.bank[2 * b + r][:, 0:P], HIGHEST)
                    ins.then_inc(mark, 1)
                    dve.tensor_scalar(one(shift[:, tiles(t), :]), top8[:, b, :, 0], -1.0, None, ALU.mult).then_inc(shifted, 1)
                    dve.wait_ge(index, t + 1)
                    dve.tensor_copy(m.index4[:, tiles(t), :, :].rearrange("q a r k -> q (a r) k"),
                                    index8[:, b, :, 0:4])
                    dve.wait_ge(mark, t + 1)
                    dve.wait_ge(hot_turned, 4 * g)
                    for r in range(2):
                        ins = dve.tensor_scalar(onehot[:, b, r, :], marked[:, r, :], HIGHEST, None, ALU.is_equal)\
                            .then_inc(hot, 1)

                over_tiles(dve, tile)

                dve.wait_ge(e4, 1)
                dve.reduce_sum(sum4[:, :, :], m.w4[:, :, :, :], AX.X).then_inc(dsum, 1)
                dve.wait_ge(dsum, 1)
                dve.scalar_tensor_tensor(sum4[:, :, :], total[:, :, :], 1e-8, sum4[:, :, :], ALU.mult,
                                         ALU.add).then_inc(denom, 1)
                dve.wait_ge(denom, 1)
                dve.reciprocal(sum4[:, :, :], sum4[:, :, :]).then_inc(inverse, 1)
                dve.wait_ge(inverse, 1)
                dve.tensor_tensor(m.w4[:, :, :, :], m.w4[:, :, :, :],
                                  sum4[:, :, :].unsqueeze(3).broadcast_to([P, TILES, 2, 4]), ALU.mult)


def assign_slots(nc, p, m):
    names = ("counted", "masked", "step", "incl_ready", "owner_ready", "turned", "zmax", "slots_out", "w_step", "passed")
    counted, masked, step, incl_ready, owner_ready, turned, zmax, slots_out, w_step, passed = \
        [p.sem("slots_" + n) for n in names]
    with ExitStack() as mem:
        sb = lambda n, shape, dt=F32: mem.enter_context(nc.sbuf_tensor("slots_" + n, shape, dt))
        cum = m.cum
        tiles_f = sb("tiles_f", [P, 2])
        tiles_i = sb("tiles_i", [P, 2], I32)
        incl = sb("incl", [P, 2])
        base = sb("base", [P, 2])
        begun = sb("begun", [P, 2, SLOT_TILES])
        z8 = sb("z8", [P, 2 * GROUP, 8])
        rank = sb("rank", [P, TILES * 2, 4])
        pairs4 = sb("pairs4", [P, TILES * 2, 4, 4])
        w_new = sb("w_new", [P, TILES * 2, 4])

        with nc.Block() as block:

            @block.vector
            def _(dve):
                n = [0]

                def then(ins):
                    ins.then_inc(step, 1)
                    n[0] += 1
                    dve.wait_ge(step, n[0])

                for r in range(2):
                    ins = dve.tensor_tensor_scan(cum[r][:, :], m.chosen[r][:, :], m.chosen[r][:, :], 0.0, ALU.add, ALU.max)
                then(ins)
                for r in range(2):
                    ins = dve.tensor_scalar(tiles_f[:, r:r + 1], cum[r][:, PADDED - 1:PADDED], float(P - 1), None, ALU.add)
                then(ins)
                then(dve.tensor_copy(tiles_i[:, :], tiles_f[:, :]))
                then(dve.tensor_scalar(tiles_i[:, :], tiles_i[:, :], P.bit_length() - 1, None, ALU.arith_shift_right))
                dve.tensor_copy(tiles_f[:, :], tiles_i[:, :]).then_inc(counted, 1)
                dve.wait_ge(incl_ready, 1)
                then(dve.tensor_copy(incl[:, :], m.bank[0][:, 0:2]))
                then(dve.tensor_tensor(base[:, :], incl[:, :], tiles_f[:, :], ALU.subtract))
                then(dve.tensor_scalar(base[:, :], base[:, :], float(P), None, ALU.mult))
                for r in range(2):
                    ins = dve.tensor_scalar(begun[:, r, :], m.iota[:, 0:SLOT_TILES], incl[:, r:r + 1], None, ALU.is_ge)
                then(ins)
                for r in range(2):
                    dve.scalar_tensor_tensor(cum[r][:, :], cum[r][:, :], base[:, r:r + 1], m.chosen[r][:, :], ALU.add,
                                             ALU.mult).then_inc(masked, 1)
                dve.wait_ge(owner_ready, 1)
                dve.tensor_scalar(m.owner[0:1, :], m.bank[1][0:1, 0:2 * SLOT_TILES], float(P - 1), None, ALU.min)

                idx = m.index4[:, :, :, :].rearrange("q t r k -> q (t r) k")
                w = m.w4[:, :, :, :].rearrange("q t r k -> q (t r) k")
                G4 = [P, TILES * 2, 4, 4]
                then(dve.tensor_tensor(pairs4[:, :, :, :], idx.unsqueeze(2).broadcast_to(G4),
                                       idx.unsqueeze(3).broadcast_to(G4), ALU.is_gt))
                then(dve.reduce_sum(rank[:, :, :], pairs4[:, :, :, :], AX.X))
                at = m.iota[:, 0:4].unsqueeze(1).unsqueeze(3).broadcast_to(G4)
                then(dve.tensor_tensor(pairs4[:, :, :, :], rank[:, :, :].unsqueeze(2).broadcast_to(G4), at, ALU.is_equal))
                then(dve.tensor_tensor(pairs4[:, :, :, :], pairs4[:, :, :, :], w.unsqueeze(2).broadcast_to(G4), ALU.mult))
                dve.reduce_sum(w_new[:, :, :], pairs4[:, :, :, :], AX.X).then_inc(w_step, 1)
                dve.wait_ge(w_step, 1)
                dve.tensor_copy(w, w_new[:, :, :])

                with dve.Fori(0, TURNS) as g:
                    for j in range(GROUP):
                        for r in range(2):
                            t = g * GROUP + j
                            q = 2 * j + r
                            dve.wait_ge(turned, 2 * t + r + 1).then_inc(passed, 1)
                            dve.max(z8[:, q, :], m.bank[2 + q % 5][:, 0:P]).then_inc(zmax, 1)
                    dve.wait_ge(zmax, 2 * GROUP * (g + 1))
                    now = m.slots[:, tiles(g * GROUP, GROUP), :, :].rearrange("q t r k -> q (t r) k")
                    dve.tensor_scalar(now, z8[:, :, 0:4], -1.0, None, ALU.add).then_inc(slots_out, 1)
                    dve.wait_ge(slots_out, g + 1)

            @block.tensor
            def _(pe):
                pe.wait_ge(counted, 1)
                pe.matmul(m.bank[0][:, 0:2], m.upto[:, :], tiles_f[:, :], start=True, stop=True).then_inc(incl_ready, 1)
                pe.wait_ge(step, 8)
                pe.matmul(m.bank[1][0:1, 0:2 * SLOT_TILES], m.ones[:, 0:1], begun[:, :, :].rearrange("q r n -> q (r n)"),
                          start=True, stop=True).then_inc(owner_ready, 1)
                pe.wait_ge(masked, 2)
                for t in range(TILES):
                    for r in range(2):
                        q = 2 * t + r
                        if q >= 5:
                            pe.wait_ge(zmax, q - 4)
                        pe.transpose(m.bank[2 + q % 5][:, 0:P], cum[r][:, t * P:(t + 1) * P], m.ident[:, :])\
                            .then_inc(turned, 1)


def scatter_rows(nc, p, m, r, src, dst, filled):
    sent, = p.software[f"scatter{r}_sent"]
    with nc.Block() as block:

        @block.gpsimd
        def _(pool):
            pool.wait_ge(filled[0], filled[1])
            for t in range(TILES):
                for k in range(4):
                    pool.indirect_dma_start(out=dst, out_offset=bass.IndirectOffsetOnAxis(
                        ap=m.slots[:, t, r, k:k + 1], axis=0), in_=src[:, t, :], in_offset=None).then_inc(sent, 16)
            pool.wait_ge(sent, 16 * 4 * TILES)


def neuron_tiles(nc, p, m, r, slots_in, weights, slots_out, kh, kp, n):
    x_ready = [p.sem(f"nt{r}_x_ready{i}") for i in range(X_CHUNKS)]
    w_ready = [p.sem(f"nt{r}_w_ready{i}") for i in range(NT_RING)]
    turned, xt_out, o_ready, o_out = [p.sem(f"nt{r}_" + n) for n in ("turned", "xt_out", "o_ready", "o_out")]
    stored = p.software[f"nt{r}_stored"]
    K = kh * kp
    TURN = NT_RING
    PER = TURN // X_CHUNKS
    LOOPS = SLOT_TILES // TURN
    area = m.after_hidden()
    x = area(P, TURN * K).rearrange("q (t n) -> q t n", t=TURN)
    w = area(kp, TURN * kh * n).rearrange("q (t h n) -> q t h n", t=TURN, h=kh)
    xt = area(kp, TURN * kh * P).rearrange("q (t n) -> q t n", t=TURN)
    o = area(P, TURN * n).rearrange("q (t n) -> q t n", t=TURN)
    chunk = lambda dram, g, c: dram[bass.ds((g * TURN + c * PER) * P, PER * P), :].rearrange("(t q) d -> q t d", q=P)

    def turns(eng, turn):
        turn(0, None)
        with eng.Fori(0, LOOPS - 1) as g:
            turn(g + 1, g * TURN)

    with nc.Block() as block:

        @block.sync
        def _(sp):
            def turn(g, before):
                _, owners = nc.values_load_multi_w_load_instructions(
                    m.owner[0:1, bass.ds(r * SLOT_TILES + g * TURN, TURN)], engines=[mybir.EngineType.SP],
                    min_val=0, max_val=P - 1, skip_runtime_bounds_check_because="assign_slots clips owners")
                for j in range(TURN):
                    if j % PER == 0:
                        if before is not None:
                            sp.wait_ge(turned, before + j + PER)
                        sp.dma_start(x[:, j:j + PER, :], chunk(slots_in, g, j // PER)).then_inc(x_ready[j // PER], 16)
                    if before is not None:
                        sp.wait_ge(o_ready, before + j + 1)
                    sp.dma_start(w[:, j, :, :].rearrange("q h n -> q (h n)"), weights[bass.ds(owners[j], 1), :, :].rearrange("e q n -> q (e n)"))\
                        .then_inc(w_ready[j], 16)

            turns(sp, turn)

        @block.gpsimd
        def _(pool):
            with pool.Fori(0, LOOPS) as g:
                for c in range(X_CHUNKS):
                    pool.wait_ge(o_out, g * TURN + (c + 1) * PER)
                    pool.dma_start(chunk(slots_out, g, c), o[:, c * PER:(c + 1) * PER, :]).then_inc(stored[c], 16)
            for c in range(X_CHUNKS):
                pool.wait_ge(stored[c], 16 * LOOPS)

        @block.tensor
        def _(pe):
            AHEAD = 3

            def turn(g, j, first=False):
                pe.wait_ge(x_ready[j // PER], 16 * g + 16)
                if not first:
                    pe.wait_ge(xt_out, g * TURN + j - 3)
                for h in range(kh):
                    mm = pe.transpose(m.bank[j % 4][0:kp, h * P:(h + 1) * P], x[:, j, h * kp:(h + 1) * kp], m.ident[:, :])
                mm.then_inc(turned, 1)

            def product(g, j, first=False):
                pe.wait_ge(xt_out, g * TURN + j + 1)
                pe.wait_ge(w_ready[j], 16 * g + 16)
                if not first:
                    pe.wait_ge(o_out, g * TURN + j - 3)
                for h in range(kh):
                    mm = pe.matmul(m.bank[4 + j % 4][:, 0:n], xt[:, j, h * P:(h + 1) * P], w[:, j, h, :],
                                   start=(h == 0), stop=(h == kh - 1))
                mm.then_inc(o_ready, 1)

            for j in range(AHEAD):
                turn(0, j, True)
            for j in range(TURN):
                t = j + AHEAD
                turn(t // TURN, t % TURN, t < 4)
                product(0, j, j < 4)
            with pe.Fori(0, LOOPS - 2) as g:
                for j in range(TURN):
                    turn(g + (1 + (j + AHEAD) // TURN), (j + AHEAD) % TURN)
                    product(g + 1, j)
            for j in range(TURN):
                if j + AHEAD < TURN:
                    turn(LOOPS - 1, j + AHEAD)
                product(LOOPS - 1, j)

        @block.scalar
        def _(act):
            def turn(g, before):
                for j in range(TURN):
                    act.wait_ge(turned, g * TURN + j + 1)
                    if before is not None:
                        act.wait_ge(o_ready, before + j + 1)
                    act.activation(xt[:, j, :], m.bank[j % 4][0:kp, 0:kh * P], ACT.Copy).then_inc(xt_out, 1)

            turns(act, turn)

        @block.vector
        def _(dve):
            def turn(g, before):
                for j in range(TURN):
                    if j % PER == 0 and before is not None:
                        dve.wait_ge(stored[j // PER], 16 * g)
                    dve.wait_ge(o_ready, g * TURN + j + 1)
                    dve.tensor_copy(o[:, j, :], m.bank[4 + j % 4][:, 0:n]).then_inc(o_out, 1)

            turns(dve, turn)


def combine(nc, p, m, r, slots_out, n, dst, scatter_to=None, filled=None):
    gathered = p.software[f"comb{r}_gathered"]
    sent, = p.software[f"comb{r}_sent"]
    step, summed, part, aggregated, stats, passed = [p.sem(f"comb{r}_" + n) for n in (
        "step", "summed", "part", "aggregated", "stats", "passed")]
    if True:
        rows = m.after_hidden()(P, GROUP * 4 * n).rearrange("q (j k n) -> q j k n", j=GROUP, k=4)

        with nc.Block() as block:

            @block.gpsimd
            def _(pool):
                LAG = 3

                def scatter(t):
                    pool.wait_ge(summed, t + 1)
                    for k in range(4):
                        pool.indirect_dma_start(out=scatter_to, out_offset=bass.IndirectOffsetOnAxis(
                            ap=m.slots[:, t, 1, k:k + 1], axis=0), in_=dst[:, t, :], in_offset=None).then_inc(sent, 16)
                if scatter_to is not None:
                    pool.wait_ge(filled[0], filled[1])
                for t in range(TILES):
                    if t >= GROUP:
                        pool.wait_ge(summed, t - GROUP + 1)
                    for k in range(4):
                        pool.indirect_dma_start(out=rows[:, t % GROUP, k, :], out_offset=None, in_=slots_out,
                                                in_offset=bass.IndirectOffsetOnAxis(ap=m.slots[:, t, r, k:k + 1], axis=0))\
                            .then_inc(gathered[t % GROUP], 16)
                    if scatter_to is not None and t >= LAG:
                        scatter(t - LAG)
                if scatter_to is not None:
                    for t in range(TILES - LAG, TILES):
                        scatter(t)
                    pool.wait_ge(sent, 16 * 4 * TILES)

            @block.vector
            def _(dve):
                with dve.Fori(0, TURNS) as g:
                    for j in range(GROUP):
                        t = g * GROUP + j
                        out = one(dst[:, tiles(t), :])
                        dve.wait_ge(gathered[j], 64 * g + 64)
                        for k in range(4):
                            w = m.w4[:, tiles(t), r, k:k + 1].rearrange("q a k -> q (a k)")
                            if k == 0 and scatter_to is not None:
                                ins = dve.tensor_scalar(out, rows[:, j, k, :], w, None, ALU.mult)
                            else:
                                ins = dve.scalar_tensor_tensor(out, rows[:, j, k, :], w, out, ALU.mult, ALU.add)
                            if k < 3:
                                ins.then_inc(step, 1)
                                dve.wait_ge(step, 3 * t + k + 1)
                            else:
                                ins.then_inc(summed, 1)
                    if scatter_to is None:
                        row_statistics(dve, m, m.mv, g, (summed, g * GROUP + GROUP), part, aggregated, stats, passed)


def projection_bias(nc, p, m):
    s = m.sems
    ready, scaled = [p.sem("pb_" + n) for n in ("ready", "scaled")]
    with nc.Block() as block:

        @block.tensor
        def _(pe):
            pe.wait_ge(s["c_attn1"], m.n_attn1)
            for h in range(2):
                mm = pe.matmul(m.bank[0][:, 0:D], m.b_v1[:, h:h + 1].broadcast_to([DH, P]), m.w_proj1[:, h, :],
                               start=(h == 0), stop=(h == 1))
            mm.then_inc(ready, 1)

        @block.vector
        def _(dve):
            dve.wait_ge(s["c_attn1"], m.n_attn1)
            dve.tensor_scalar(m.score_scale[:, :], m.score_scale[:, :], 0.01, None, ALU.max).then_inc(scaled, 1)
            dve.wait_ge(scaled, 1)
            dve.reciprocal(m.score_scale[:, :], m.score_scale[:, :]).then_inc(scaled, 1)
            dve.wait_ge(scaled, 2)
            dve.tensor_scalar(m.score_scale[:, :], m.score_scale[:, :], float(HEAD) ** -0.5, None, ALU.mult)
            dve.wait_ge(ready, 1)
            dve.tensor_tensor(m.r_bproj1[:, :], m.r_bproj1[:, :], m.bank[0][:, 0:D], ALU.add)


def sparse_attention(nc, p, m):
    s = m.sems
    names = ("k_blocks", "scores_ready", "top1", "rest1", "top2", "rest2", "top3", "shift_ready", "mask_ready",
             "exp_ready", "kept_ready", "v_ready", "v_blocks", "probs_turned", "probs_out", "heads_ready", "inverse",
             "heads_scaled", "heads_turned", "heads_out", "cleared", "v_cleared", "scores_out", "passed")
    (k_blocks, scores_ready, top1, rest1, top2, rest2, top3, shift_ready, mask_ready, exp_ready, kept_ready, v_ready,
     v_blocks, probs_turned, probs_out, heads_ready, inverse_ready, heads_scaled, heads_turned, heads_out,
     cleared, v_cleared, scores_out, passed) = [p.sem("a1_" + n) for n in names]
    NH, HB = HEADS, HEADS // 2
    VC = 2 * HEAD + 2
    KEYS = HB * SEQ
    xn = m.xn[:, :, :].rearrange("q t d -> q (t d)")
    at = [0]

    def area(parts, n):
        at[0] += n
        assert at[0] <= TILES * D
        return xn[0:parts, at[0] - n:at[0]]

    with ExitStack() as mem:
        sb = lambda n, shape, dt=F32: mem.enter_context(nc.sbuf_tensor("a1_" + n, shape, dt))
        kb = sb("kb", [DH, 2, 2, 2, KEYS])
        work = area(P, NH * SEQ).rearrange("q (h k) -> q h k", h=NH)
        ex = [area(P, NH * SEQ).rearrange("q (h k) -> q h k", h=NH) for _ in range(2)]
        sc = [area(P, NH * SEQ).rearrange("q (h k) -> q h k", h=NH) for _ in range(2)]
        mask = [area(P, KEYS).bitcast(mybir.dt.bfloat16).rearrange("q (h k) -> q h k", h=NH) for _ in range(2)]
        kept = [area(P, NH * SLOT).rearrange("q (h k) -> q h k", h=NH), sb("kept", [P, NH, SLOT])]
        pt = m.spare[:, 0:HB * P].rearrange("q (j n) -> q j n", j=HB)
        vb = sb("vb", [P, 2, 2, HB, VC])
        top_a, top_b, top_c = [area(P, NH * 8).rearrange("q (h k) -> q h k", h=NH) for _ in range(3)]
        shift = sb("shift", [P, 2, NH])
        inverse = area(P, NH)
        o = area(P, D)
        S = [(m.bank[0], m.bank[1]), (m.bank[2], m.bank[3])]
        PT, V, O = (m.bank[4], m.bank[5]), m.bank[6], m.bank[7]

        def score(u, h):
            return sc[u][:, h, :]

        with nc.Block() as block:

            @block.tensor
            def _(pe):
                def columns(x, c, i, b):
                    return x[:, c, (2 * i + 1 + b) * SLOT:(2 * i + 2 + b) * SLOT]

                def scores(i):
                    pe.wait_ge(k_blocks, i + 1)
                    if i >= 2:
                        pe.wait_ge(scores_out, i - 1)
                    for c in range(2):
                        for b in range(2):
                            mm = pe.matmul(S[i % 2][c][b * SLOT:(b + 1) * SLOT, 0:KEYS], columns(m.qt, c, i, b),
                                           kb[:, i % 2, b, c, :], start=True, stop=True)
                    mm.then_inc(scores_ready, 1)

                def values(i):
                    if i:
                        pe.wait_ge(v_blocks, i)
                    wv = m.w_qkv1[:, :, 2 * D:3 * D]
                    for c in range(2):
                        pe.matmul(V[:, 0:D], pair_columns(m.xs, c, i), wv[:, c, :], start=(c == 0), stop=(c == 1))
                    for b in range(2):
                        q = slice((1 - b) * SLOT, (2 - b) * SLOT)
                        for c in range(2):
                            mm = pe.matmul(V[q, D:2 * D], columns(m.xs, c, i, b), wv[:, c, :], start=(c == 0), stop=(c == 1))
                    mm.then_inc(v_ready, 1)

                def turn_probs(i):
                    pe.wait_ge(kept_ready, i + 1)
                    if i:
                        pe.wait_ge(probs_out, i)
                    for j in range(HB):
                        mm = pe.transpose(PT[j // 4][:, (j % 4) * P:(j % 4 + 1) * P],
                                          kept[i % 2][:, 2 * j:2 * j + 2, :].rearrange("q h k -> q (h k)"), m.ident[:, :])
                    mm.then_inc(probs_turned, 1)

                def heads(i):
                    pe.wait_ge(probs_out, i + 1)
                    pe.wait_ge(v_blocks, i + 1)
                    if i:
                        pe.wait_ge(heads_out, i)
                    for j in range(HB):
                        for b in range(2):
                            q = slice(b * SLOT, (b + 1) * SLOT)
                            mm = pe.matmul(O[q, j * VC:(j + 1) * VC], pt[:, j, q], vb[:, i % 2, b, j, :], start=True, stop=True)
                    mm.then_inc(heads_ready, 1)

                def turn_heads(i):
                    pe.wait_ge(heads_scaled, i + 1)
                    for c in range(2):
                        mm = pe.transpose(O[0:DH, c * P:(c + 1) * P], o[:, c * DH:(c + 1) * DH], m.ident[:, :])
                    mm.then_inc(heads_turned, 1)

                scores(0)
                for i in range(PAIRS + 2):
                    if 1 <= i <= PAIRS:
                        turn_probs(i - 1)
                    if i >= 2:
                        turn_heads(i - 2)
                    if i + 1 < PAIRS:
                        scores(i + 1)
                    if 1 <= i <= PAIRS:
                        heads(i - 1)
                    if i < PAIRS:
                        values(i)

            @block.gpsimd
            def _(pool):
                for x in kept:
                    pool.memset(x[:, :, :], 0.0).then_inc(cleared, 1)
                pool.wait_ge(cleared, 2)

                def blocks(i, u, first=False):
                    if not first:
                        pool.wait_ge(scores_ready, i - 1)
                    for b in range(2):
                        for c in range(2):
                            k = m.kt[:, c, bass.ds((2 * i + 1 + b) * SLOT, SEQ)]
                            ins = pool.tensor_tensor(kb[:, u, b, c, :].rearrange("q (h k) -> q h k", h=HB),
                                                     k.unsqueeze(1).broadcast_to([DH, HB, SEQ]),
                                                     m.head_mask[:, :].unsqueeze(2).broadcast_to([DH, HB, SEQ]), ALU.mult)
                    ins.then_inc(k_blocks, 1)

                def keep(i, u, first=False):
                    pool.wait_ge(mask_ready, i + 1)
                    pool.wait_ge(exp_ready, i + 1)
                    if not first:
                        pool.wait_ge(probs_turned, i - 1)
                    pool.tensor_tensor(kept[u][:, :, 0:SEQ], ex[u], mask[u], ALU.mult).then_inc(kept_ready, 1)

                blocks(0, 0, True)
                blocks(1, 1, True)
                for i in range(2):
                    blocks(i + 2, i)
                    keep(i, i, True)
                with pool.Fori(0, PAIRS // 2 - 2) as g:
                    for u in range(2):
                        i = 2 * g + 2 + u
                        blocks(i + 2, u)
                        keep(i, u)
                keep(PAIRS - 2, 0)
                keep(PAIRS - 1, 1)

            @block.vector
            def _(dve):
                def select(i, u):
                    half = [range(n * HB, (n + 1) * HB) for n in range(2)]

                    def largest(top, x, n, done):
                        for h in half[n]:
                            ins = dve.max(top[:, h, :], x(h))
                        ins.then_inc(done, 1)

                    def without(top, x, n, done):
                        for h in half[n]:
                            ins = dve.match_replace(work[:, h, :], top[:, h, :], x(h), LOWEST)
                        ins.then_inc(done, 1)

                    given = lambda h: score(u, h)
                    rest = lambda h: work[:, h, :]
                    dve.wait_ge(scores_out, i + 1).then_inc(passed, 1)
                    largest(top_a, given, 0, top1)
                    largest(top_a, given, 1, top1)
                    dve.wait_ge(top1, 2 * i + 1).then_inc(passed, 1)
                    without(top_a, given, 0, rest1)
                    dve.wait_ge(top1, 2 * i + 2)
                    dve.tensor_scalar(shift[:, u, :], top_a[:, :, 0], m.score_scale[:, 0:1], -1.0, ALU.mult,
                                      ALU.mult).then_inc(shift_ready, 1)
                    without(top_a, given, 1, rest1)
                    for n in range(2):
                        dve.wait_ge(rest1, 2 * i + n + 1).then_inc(passed, 1)
                        largest(top_b, rest, n, top2)
                    for n in range(2):
                        dve.wait_ge(top2, 2 * i + n + 1).then_inc(passed, 1)
                        without(top_b, rest, n, rest2)
                    for n in range(2):
                        dve.wait_ge(rest2, 2 * i + n + 1).then_inc(passed, 1)
                        largest(top_c, rest, n, top3)
                    dve.wait_ge(top3, 2 * i + 2)
                    if not (isinstance(i, int) and i == 0):
                        dve.wait_ge(kept_ready, i - 1)
                    dve.tensor_tensor(mask[u], sc[u], top_c[:, :, 7:8].broadcast_to([P, NH, SEQ]), ALU.is_ge)\
                        .then_inc(mask_ready, 1)

                def scale(i):
                    dve.wait_ge(heads_ready, i + 1)
                    got = O[:, 0:HB * VC].rearrange("q (j c) -> q j c", j=HB)
                    dve.reciprocal(inverse[:, :].rearrange("q (j e) -> q j e", e=2), got[:, :, 2 * HEAD:VC])\
                        .then_inc(inverse_ready, 1)
                    dve.wait_ge(inverse_ready, i + 1)
                    dve.wait_ge(heads_turned, i)
                    inv = inverse[:, :].rearrange("q (j e) -> q j e", e=2)
                    out = o[:, :].rearrange("q (j e d) -> q j e d", j=HB, e=2)
                    for e in range(2):
                        ins = dve.tensor_tensor(out[:, :, e, :], got[:, :, e * HEAD:(e + 1) * HEAD],
                                                inv[:, :, e:e + 1].broadcast_to([P, HB, HEAD]), ALU.mult)
                    ins.then_inc(heads_scaled, 1)

                select(0, 0)
                with dve.Fori(0, PAIRS // 2 - 1) as g:
                    for k in range(2):
                        i = 2 * g + 1 + k
                        select(i, 1 - k)
                        scale(i - 1)
                select(PAIRS - 1, 1)
                scale(PAIRS - 2)
                scale(PAIRS - 1)

            @block.scalar
            def _(act):
                act.activation(vb[:, :, :, :, :].rearrange("q a b j c -> q (a b j c)"),
                               m.zeros[:, 0:1].broadcast_to([P, 4 * HB * VC]), ACT.Copy).then_inc(v_cleared, 1)
                act.wait_ge(v_cleared, 1)
                flat = vb[:, :, :, :, :].rearrange("q a b j c -> q (a b j) c")
                for e in range(2):
                    q = slice(e * SLOT, (e + 1) * SLOT)
                    act.activation(flat[q, :, 2 * HEAD + e], m.ones[q, 0:1].broadcast_to([SLOT, 4 * HB]), ACT.Copy)

                def lift_scores(i, u):
                    act.wait_ge(scores_ready, i + 1)
                    for c in range(2):
                        ins = act.activation(sc[u][:, c * HB:(c + 1) * HB, :],
                                             S[u][c][:, 0:KEYS].rearrange("q (h k) -> q h k", h=HB), ACT.Copy)
                    ins.then_inc(scores_out, 1)

                def exps(i, u):
                    act.wait_ge(shift_ready, i + 1)
                    if not (isinstance(i, int) and i == 0):
                        act.wait_ge(kept_ready, i - 1)
                    for h in range(NH):
                        ins = act.activation(ex[u][:, h, :], score(u, h), ACT.Exp, bias=shift[:, u, h:h + 1],
                                             scale=m.score_scale[:, 0:1])
                    ins.then_inc(exp_ready, 1)

                def spread_values(i, u):
                    act.wait_ge(v_ready, i + 1)
                    if not (isinstance(i, int) and i == 0):
                        act.wait_ge(heads_ready, i - 1)
                    for e in range(2):
                        for b in range(2):
                            q = slice(e * SLOT, (e + 1) * SLOT)
                            src = V[q, (e != b) * D:(e != b) * D + D].rearrange("q (j e d) -> q j e d", j=HB, e=2)
                            ins = act.activation(vb[q, u, b, :, e * HEAD:(e + 1) * HEAD], src[:, :, e, :], ACT.Copy)
                    ins.then_inc(v_blocks, 1)

                def lift_probs(i):
                    act.wait_ge(probs_turned, i + 1)
                    act.wait_ge(heads_ready, i)
                    act.activation(pt[:, 0:4, :], PT[0][:, :].rearrange("q (j n) -> q j n", j=4), ACT.Copy)
                    act.activation(pt[:, 4:6, :], PT[1][:, 0:2 * P].rearrange("q (j n) -> q j n", j=2), ACT.Copy)\
                        .then_inc(probs_out, 1)

                def lift_heads(i):
                    act.wait_ge(heads_turned, i + 1)
                    src = O[0:DH, 0:2 * P].rearrange("q (h a k) -> q h a k", h=2, a=2)
                    dst = m.at[:, :, bass.ds(i * 2 * SEQ, 2 * SEQ)].rearrange("q h (a k) -> q h a k", a=2)
                    for h in range(2):
                        ins = act.activation(dst[:, h], src[:, h, :, 0:SEQ], ACT.Copy)
                    ins.then_inc(heads_out, 1)

                def pair(i, u, lag=2, last=False):
                    if lag >= 1:
                        lift_probs(i - 1)
                    if lag >= 2:
                        lift_heads(i - 2)
                    exps(i, u)
                    if not last:
                        lift_scores(i + 1, 1 - u)
                    spread_values(i, u)

                lift_scores(0, 0)
                pair(0, 0, lag=0)
                pair(1, 1, lag=1)
                with act.Fori(0, PAIRS // 2 - 2) as g:
                    for k in range(2):
                        pair(2 * g + 2 + k, k)
                pair(PAIRS - 2, 0)
                pair(PAIRS - 1, 1, last=True)
                lift_probs(PAIRS - 1)
                lift_heads(PAIRS - 2)
                lift_heads(PAIRS - 1)


def route_experts(nc, p, m):
    s = m.sems
    names = ("logits_ready", "step", "less", "exp_ready", "spread", "turned", "rows_out", "enough", "over_ready",
             "valued", "back_turned", "back_out")
    logits_ready, step, less, exp_ready, spread, turned, rows_out, enough, over_ready, valued, back_turned, \
        back_out = [p.sem("moe_" + n) for n in names]
    at = [0]

    def area(n):
        at[0] += n
        assert at[0] <= 6 * COLS
        return m.arena[:, at[0] - n:at[0]]

    E = EXPERTS
    C = P // E
    by_expert = lambda x: x.rearrange("q (t e) -> q t e", e=E)
    logits, probs, equal, first = [by_expert(area(TILES * E)) for _ in range(4)]
    low, total, route = [area(TILES) for _ in range(3)]
    spread_q = area(TILES * P).rearrange("q (t e c) -> q t e c", t=TILES, e=E)
    rows, above, level, run = [area(PADDED) for _ in range(4)]
    lo, thr, count, over, room, level_at, part = [area(1) for _ in range(7)]
    value = area(TILES)
    BANKS = -(-TILES // 4)
    T8 = [P, TILES, E]

    with nc.Block() as block:

        @block.tensor
        def _(pe):
            pe.wait_ge(s["c_moe"], m.n_moe)
            for t in range(TILES):
                for h in range(2):
                    mm = pe.matmul(m.bank[7][:, t * E:(t + 1) * E], m.xt[:, h, t * P:(t + 1) * P], m.w_switch[:, h, :],
                                   start=(h == 0), stop=(h == 1))
            mm.then_inc(logits_ready, 1)
            pe.wait_ge(spread, 1)
            for t in range(TILES):
                mm = pe.transpose(m.bank[t // 4][:, (t % 4) * P:(t % 4 + 1) * P],
                                  spread_q[:, t, :, :].rearrange("q e c -> q (e c)"), m.ident[:, :])
                mm.then_inc(turned, 1)
            for n in range(ROUNDS):
                pe.wait_ge(enough, n + 1)
                pe.matmul(m.bank[7][:, 0:1], m.group_ones[:, :], over, start=True, stop=True).then_inc(over_ready, 1)
            pe.wait_ge(valued, 1)
            for t in range(TILES):
                mm = pe.transpose(m.bank[t // 4][:, (t % 4) * P:(t % 4 + 1) * P], level[:, t * P:(t + 1) * P], m.ident[:, :])
            mm.then_inc(back_turned, 1)

        @block.scalar
        def _(act):
            act.wait_ge(less, 1)
            act.activation(probs, probs, ACT.Exp).then_inc(exp_ready, 1)
            for b in range(BANKS):
                n = min(4, TILES - 4 * b) * P
                act.wait_ge(turned, min(4 * b + 4, TILES))
                act.activation(rows[:, 4 * b * P:4 * b * P + n], m.bank[b][:, 0:n], ACT.Copy).then_inc(rows_out, 1)

        @block.vector
        def _(dve):
            n = [0]

            def then(ins):
                ins.then_inc(step, 1)
                n[0] += 1
                dve.wait_ge(step, n[0])

            dve.wait_ge(s["c_moe"], m.n_moe)
            dve.wait_ge(logits_ready, 1)
            then(dve.tensor_tensor(logits, m.bank[7][:, 0:TILES * E].rearrange("q (t e) -> q t e", e=E),
                                   m.r_switch[:, :].unsqueeze(1).broadcast_to(T8), ALU.add))
            then(dve.reduce_max(low, logits, AX.X))
            dve.tensor_tensor(probs, logits, low.unsqueeze(2).broadcast_to(T8), ALU.subtract).then_inc(less, 1)
            dve.wait_ge(exp_ready, 1)
            then(dve.reduce_sum(total, probs, AX.X))
            then(dve.reciprocal(total, total))
            then(dve.tensor_tensor(probs, probs, total.unsqueeze(2).broadcast_to(T8), ALU.mult))
            then(dve.reduce_max(m.prob_max[:, :], probs, AX.X))
            best = m.prob_max[:, :].unsqueeze(2).broadcast_to(T8)
            expert = m.iota[:, 0:E].unsqueeze(1).broadcast_to(T8)
            then(dve.tensor_tensor(equal, probs, best, ALU.is_lt))
            then(dve.scalar_tensor_tensor(first, equal, float(E), expert, ALU.mult, ALU.add))
            then(dve.tensor_reduce(route, first, AX.X, ALU.min))
            then(dve.tensor_tensor(equal, expert, route.unsqueeze(2).broadcast_to(T8), ALU.is_equal))
            then(dve.tensor_tensor(equal, equal, best, ALU.mult))
            half = spread_q.rearrange("q t e c -> q (t e) c")
            dve.tensor_copy(half, equal.rearrange("q t e -> q (t e)").unsqueeze(2).broadcast_to([P, TILES * E, C]))\
                .then_inc(spread, 1)

            dve.wait_ge(rows_out, BANKS)
            now = slice(0, TOKENS)
            then(dve.memset(lo, 0.0))
            width = 2.0
            for r in range(ROUNDS):
                width /= C
                then(dve.scalar_tensor_tensor(thr, m.threshold[:, 0:1], width, lo, ALU.mult, ALU.add))
                then(dve.tensor_scalar(above[:, now], rows[:, now], thr, None, ALU.is_ge, ALU.add, accum_out=count))
                dve.tensor_scalar(over, count, float(CAPACITY), None, ALU.is_ge).then_inc(enough, 1)
                dve.wait_ge(over_ready, r + 1)
                then(dve.tensor_scalar(part, m.bank[7][:, 0:1], -1.0, width, ALU.add, ALU.mult))
                then(dve.tensor_tensor(lo, lo, part, ALU.add))
            then(dve.tensor_scalar(above[:, now], rows[:, now], lo, None, ALU.is_gt, ALU.add, accum_out=count))
            then(dve.tensor_scalar(room, count, -1.0, float(CAPACITY), ALU.mult, ALU.add))
            then(dve.tensor_scalar(level_at, lo, 0.0, None, ALU.is_equal))
            then(dve.tensor_tensor(level_at, lo, level_at, ALU.subtract))
            then(dve.tensor_scalar(level[:, now], rows[:, now], level_at, None, ALU.is_equal))
            then(dve.tensor_tensor_scan(run[:, now], level[:, now], level[:, now], 0.0, ALU.add, ALU.max))
            then(dve.scalar_tensor_tensor(level[:, now], run[:, now], room, level[:, now], ALU.is_le, ALU.mult))
            then(dve.tensor_tensor(above[:, now], above[:, now], level[:, now], ALU.add))
            then(dve.tensor_tensor_scan(run[:, now], above[:, now], above[:, now], 0.0, ALU.add, ALU.max))
            dve.scalar_tensor_tensor(level[:, now], run[:, now], m.slot_base[:, 0:1], above[:, now], ALU.add, ALU.mult)
            dve.memset(level[:, TOKENS:PADDED], 0.0).then_inc(valued, 1)
            dve.wait_ge(back_turned, 1)
            for b in range(BANKS):
                k = min(4, TILES - 4 * b)
                src = m.bank[b][:, 0:k * P].rearrange("q (t e c) -> q t e c", t=k, e=E)[:, :, :, 0]
                ins = dve.reduce_max(value[:, 4 * b:4 * b + k], src, AX.X)
            then(ins)
            then(dve.tensor_scalar(route, value, 0.0, None, ALU.is_equal))
            then(dve.tensor_tensor(low, value, route, ALU.add))
            then(dve.tensor_scalar(m.moe_row[:, :], low, -1.0, None, ALU.add))
            then(dve.tensor_tensor(low, route, m.own_row[:, :], ALU.mult))
            then(dve.tensor_tensor(value, value, low, ALU.add))
            then(dve.tensor_scalar(m.moe_slot[:, :], value, -1.0, None, ALU.add))
            then(dve.tensor_tensor(m.scale_xn[:, :], m.prob_max[:, :], route, ALU.mult))
            dve.tensor_tensor(m.scale_out[:, :], m.prob_max[:, :], m.scale_xn[:, :], ALU.subtract)


def scatter_to_experts(nc, p, m):
    sent, = p.software["moe_sent"]
    with nc.Block() as block:

        @block.gpsimd
        def _(pool):
            pool.wait_ge(m.sems["c_fill_moe"], 16)
            for t in range(TILES):
                pool.indirect_dma_start(out=m.moe_in, out_offset=bass.IndirectOffsetOnAxis(
                    ap=m.moe_slot[:, t:t + 1], axis=0), in_=m.xn[:, t, :], in_offset=None).then_inc(sent, 16)
            pool.wait_ge(sent, 16 * TILES)


def experts(nc, p, m, a):
    s = m.sems
    x_ready, w_ready = [[p.sem(f"ex_{n}{u}") for u in range(2)] for n in ("x_ready", "w_ready")]
    stored = p.software["ex_stored"]
    bias_ready = p.sem("ex_bias_ready")
    turned, xt_out, h_ready, h_out, o_ready, o_out = [p.sem("ex_" + n) for n in (
        "turned", "xt_out", "h_ready", "h_out", "o_ready", "o_out")]
    at = [0]

    def area(parts, n):
        at[0] += n
        assert at[0] <= 6 * COLS
        return m.arena[0:parts, at[0] - n:at[0]]

    ST = EXPERT_SLOTS // P
    FC = HIDDEN // P
    x = area(P, 2 * ST * D).rearrange("q (u t d) -> q u t d", u=2, t=ST)
    xt = area(DH, 2 * 2 * EXPERT_SLOTS).rearrange("q (u h n) -> q u h n", u=2, h=2)
    w1 = area(DH, 2 * 2 * HIDDEN).rearrange("q (u h n) -> q u h n", u=2, h=2)
    w2 = area(P, 2 * FC * D).rearrange("q (u f n) -> q u f n", u=2, f=FC)
    hid = area(P, FC * EXPERT_SLOTS).rearrange("q (f n) -> q f n", f=FC)
    o = area(P, 2 * ST * D).rearrange("q (u t d) -> q u t d", u=2, t=ST)
    r_down = area(P, EXPERTS * D)
    w1_dram = a["L1_ffn_w1"].rearrange("e (h q) n -> q e h n", h=2)
    w2_dram = a["L1_ffn_w2"].rearrange("e (f q) n -> q e f n", q=P)
    slots = lambda dram, e: dram[bass.ds(e * EXPERT_SLOTS, EXPERT_SLOTS), :].rearrange("(t q) d -> q t d", q=P)

    def weights_of(dram, e):
        return dram[:, bass.ds(e, 1), :, :].rearrange("q e h n -> q (e h) n")

    with nc.Block() as block:

        @block.sync
        def _(sp):
            sp.dma_start(r_down, row_to_all(a["L1_ffn_b2"].rearrange("e d -> (e d)"), EXPERTS * D)).then_inc(bias_ready, 16)
            with sp.Fori(0, EXPERTS // 2) as g:
                for u in range(2):
                    e = 2 * g + u
                    sp.wait_ge(turned, 2 * ST * g)
                    sp.dma_start(x[:, u, :, :], slots(m.moe_in, e)).then_inc(x_ready[u], 16)
                    sp.wait_ge(h_ready, 2 * FC * g)
                    sp.dma_start(w1[:, u, :, :], weights_of(w1_dram, e)).then_inc(w_ready[u], 16)
                    sp.wait_ge(o_ready, 2 * ST * g)
                    sp.dma_start(w2[:, u, :, :], weights_of(w2_dram, e)).then_inc(w_ready[u], 16)

        @block.gpsimd
        def _(pool):
            with pool.Fori(0, EXPERTS // 2) as g:
                for u in range(2):
                    pool.wait_ge(o_out, ST * (2 * g + u + 1))
                    pool.dma_start(slots(m.moe_out, 2 * g + u), o[:, u, :, :]).then_inc(stored[u], 16)
            for u in range(2):
                pool.wait_ge(stored[u], 16 * (EXPERTS // 2))

        @block.tensor
        def _(pe):
            def turn(g, u):
                e = 2 * g + u
                pe.wait_ge(x_ready[u], 16 * g + 16)
                for t in range(ST):
                    pe.wait_ge(xt_out, ST * e)
                    for h in range(2):
                        mm = pe.transpose(m.bank[h][0:DH, t * P:(t + 1) * P], x[:, u, t, h * DH:(h + 1) * DH], m.ident[:, :])
                    mm.then_inc(turned, 1)

            def up(g, u):
                e = 2 * g + u
                pe.wait_ge(xt_out, ST * (e + 1))
                pe.wait_ge(w_ready[u], 32 * g + 32)
                for f in range(FC):
                    pe.wait_ge(h_out, FC * e + (f - 1 if f >= 2 else 0))
                    for h in range(2):
                        mm = pe.matmul(m.bank[2 + f % 2][:, :], w1[:, u, h, f * P:(f + 1) * P], xt[:, u, h, :],
                                       start=(h == 0), stop=(h == 1))
                    mm.then_inc(h_ready, 1)

            def down(g, u):
                e = 2 * g + u
                pe.wait_ge(h_out, FC * (e + 1))
                pe.wait_ge(o_out, ST * e)
                for t in range(ST):
                    for f in range(FC):
                        mm = pe.matmul(m.bank[4 + t][:, 0:D], hid[:, f, t * P:(t + 1) * P], w2[:, u, f, :],
                                       start=(f == 0), stop=(f == FC - 1))
                    mm.then_inc(o_ready, 1)

            turn(0, 0)
            with pe.Fori(0, EXPERTS // 2 - 1) as g:
                for u in range(2):
                    up(g, u)
                    turn(g + u, 1 - u)
                    down(g, u)
            up(EXPERTS // 2 - 1, 0)
            turn(EXPERTS // 2 - 1, 1)
            down(EXPERTS // 2 - 1, 0)
            up(EXPERTS // 2 - 1, 1)
            down(EXPERTS // 2 - 1, 1)

        @block.scalar
        def _(act):
            with act.Fori(0, EXPERTS // 2) as g:
                for u in range(2):
                    e = 2 * g + u
                    act.wait_ge(o_ready, ST * e)
                    for f in range(FC):
                        act.wait_ge(h_ready, FC * e + f + 1)
                        act.activation(hid[:, f, :], m.bank[2 + f % 2][:, :], ACT.Gelu,
                                       bias=m.b_up[:, bass.ds(e, 1), f]).then_inc(h_out, 1)

        @block.vector
        def _(dve):
            def lift_x(e, u):
                dve.wait_ge(turned, ST * (e + 1))
                for h in range(2):
                    ins = dve.tensor_copy(xt[:, u, h, :], m.bank[h][0:DH, :])
                ins.then_inc(xt_out, ST)

            def rows(g, u):
                dve.wait_ge(stored[u], 16 * g)
                for t in range(ST):
                    dve.wait_ge(o_ready, ST * (2 * g + u) + t + 1)
                    dve.tensor_tensor(o[:, u, t, :], m.bank[4 + t][:, 0:D], r_down[:, bass.ds((2 * g + u) * D, D)],
                                      ALU.add).then_inc(o_out, 1)

            dve.wait_ge(bias_ready, 16)
            lift_x(0, 0)
            with dve.Fori(0, EXPERTS // 2 - 1) as g:
                for u in range(2):
                    lift_x(2 * g + u + 1, 1 - u)
                    rows(g, u)
            lift_x(EXPERTS - 1, 1)
            rows(EXPERTS // 2 - 1, 0)
            rows(EXPERTS // 2 - 1, 1)


def finish(nc, p, m, out):
    gathered = p.software["fin_gathered"]
    first, second = [p.sem("fin_" + n) for n in ("first", "second")]
    stored = m.sems["out_stored"]
    rows = m.arena[:, 0:GROUP * D].rearrange("q (j d) -> q j d", j=GROUP)
    with nc.Block() as block:

        @block.gpsimd
        def _(pool):
            for t in range(TILES):
                if t >= GROUP:
                    pool.wait_ge(second, t - GROUP + 1)
                pool.indirect_dma_start(out=rows[:, t % GROUP, :], out_offset=None, in_=m.moe_out,
                                        in_offset=bass.IndirectOffsetOnAxis(ap=m.moe_row[:, t:t + 1], axis=0))\
                    .then_inc(gathered[t % GROUP], 16)

        @block.vector
        def _(dve):
            with dve.Fori(0, TURNS) as g:
                for j in range(GROUP):
                    t = g * GROUP + j
                    h = one(m.h[:, tiles(t), :])
                    dve.scalar_tensor_tensor(h, one(m.xn[:, tiles(t), :]), m.scale_xn[:, tiles(t)], h, ALU.mult,
                                             ALU.add).then_inc(first, 1)
                for j in range(GROUP):
                    t = g * GROUP + j
                    h = one(m.h[:, tiles(t), :])
                    dve.wait_ge(gathered[j], 16 * g + 16)
                    dve.wait_ge(first, g * GROUP + GROUP)
                    dve.scalar_tensor_tensor(h, rows[:, j, :], m.scale_out[:, tiles(t)], h, ALU.mult,
                                             ALU.add).then_inc(second, 1)

        @block.sync
        def _(sp):
            with sp.Fori(0, TURNS - 1) as g:
                sp.wait_ge(second, g * GROUP + GROUP)
                sp.dma_start(out[bass.ds(g * GROUP * P, GROUP * P), :].rearrange("(j q) d -> q j d", q=P),
                             m.h[:, tiles(g * GROUP, GROUP), :]).then_inc(stored, 16)
            sp.wait_ge(second, TILES)
            t0 = (TURNS - 1) * GROUP
            sp.dma_start(out[t0 * P:(TILES - 1) * P, :].rearrange("(j q) d -> q j d", q=P),
                         m.h[:, t0:TILES - 1, :]).then_inc(stored, 16)
            sp.dma_start(out[(TILES - 1) * P:TOKENS, :], m.h[0:LAST, TILES - 1, :]).then_inc(stored, 16)
            sp.wait_ge(stored, 16 * (TURNS + 1))


class Memory:

    def after_hidden(self):
        at = [PADDED]

        def area(parts, n):
            at[0] += n
            assert at[0] <= 6 * COLS
            return self.arena[0:parts, at[0] - n:at[0]]
        return area



def build(nc, a, out):
    with ExitStack() as ctx:
        p = Program(nc, ctx)
        m = Memory()
        m.sems = {}
        m.bank = [p.bank(f"bank{i}") for i in range(8)]
        m.h = p.sb("h", [P, TILES, D])
        m.xn = p.sb("xn", [P, TILES, D])
        m.xn_patches = m.xn[:, :, :].rearrange("q t d -> q (t d)")[:, 0:GROUP * PATCH].rearrange("q (j d) -> q j d", j=GROUP)
        m.xt = p.sb("xt", [DH, 2, PADDED])
        m.arena = p.sb("arena", [P, 6 * COLS])
        m.x_all = m.arena[:, 0:TILES * PATCH].rearrange("q (t d) -> q t d", t=TILES)
        m.mv = p.sb("mv", [P, TILES, 2])
        m.mv2 = p.sb("mv2", [P, TILES, 2])
        m.rstd = p.sb("rstd", [P, TILES])
        m.shift = p.sb("shift", [P, TILES])
        m.bn = p.sb("bn", [P, 128])
        m.mv_group = p.sb("mv_group", [P, GROUP, 2])
        m.minus_half = p.sb("minus_half", [P, TILES])
        m.ident = p.sb("ident", [P, P])
        m.g1 = p.sb("g1", [P, PCH])
        m.b1 = p.sb("b1", [P, PCH])
        m.r_btok = p.sb("r_btok", [P, D])
        m.r_g2 = p.sb("r_g2", [P, D])
        m.r_b2 = p.sb("r_b2", [P, D])
        m.n_attn0 = 0
        m.qt, m.kt, m.xs = [m.arena[0:DH, i * 2 * COLS:(i + 1) * 2 * COLS].rearrange("q (h n) -> q h n", h=2)
                            for i in range(3)]
        m.at = m.xt
        m.pair_row = p.sb("pair_row", [2, P])
        m.pair_bar = p.sb("pair_bar", [2, P])
        m.spare = p.sb("spare", [P, 6 * D])
        m.w_qkv0 = m.spare[0:DH, :].rearrange("q (h n) -> q h n", h=2)
        m.w_gp = p.sb("w_gp", [DH, 2, SEQ])
        m.w_proj0 = p.sb("w_proj0", [DH, 2, D])
        m.b_qk0 = p.sb("b_qk0", [DH, 4])
        m.alpha = p.sb("alpha", [P, 1])
        m.r_bv0 = p.sb("r_bv0", [P, D])
        m.r_bproj0 = p.sb("r_bproj0", [P, D])
        m.n_moe = 0
        m.w_switch = p.sb("w_switch", [DH, 2, EXPERTS])
        m.r_switch = p.sb("r_switch", [P, EXPERTS])
        m.b_up = p.sb("b_up", [P, EXPERTS, HIDDEN // P])
        m.group_ones = p.sb("group_ones", [P, P])
        m.threshold, m.slot_base = [p.sb(n, [P, 1]) for n in ("threshold", "slot_base")]
        m.own_row = p.sb('own_row', [P, TILES])
        m.prob_max, m.scale_xn, m.scale_out = [p.sb(n, [P, TILES]) for n in ("prob_max", "scale_xn", "scale_out")]
        m.moe_slot = p.sb("moe_slot", [P, TILES], U32)
        m.moe_row = p.sb("moe_row", [P, TILES], U32)
        m.moe_in = nc.dram_tensor("moe_in", [MOE_SLOTS + 1 + PADDED, D], F32).ap()
        m.moe_out = nc.dram_tensor("moe_out", [MOE_SLOTS, D], F32).ap()
        m.n_attn1 = 0
        m.w_qkv1 = p.sb("w_qkv1", [DH, 2, 3 * D])
        m.w_proj1 = p.sb("w_proj1", [DH, 2, D])
        m.b_qk1 = p.sb("b_qk1", [DH, 4])
        m.b_v1 = p.sb("b_v1", [DH, 2])
        m.r_bproj1 = p.sb("r_bproj1", [P, D])
        m.score_scale = p.sb("score_scale", [P, 1])
        m.head_mask = p.sb("head_mask", [DH, HEADS // 2])
        m.n_ffn0 = 0
        m.plus_half = p.sb("plus_half", [P, 2])
        m.ones = p.sb("ones", [P, 2])
        m.zeros = p.sb("zeros", [P, D])
        m.iota = p.sb("iota", [P, 2 * P])
        m.upto = p.sb("upto", [P, P])
        m.w_route = p.sb("w_route", [DH, 2, 2 * R2])
        m.b_route = p.sb("b_route", [2 * R2, 1])
        m.emb = p.sb("emb", [P, 2 * R2])
        m.squares = p.sb("squares", [P, 2 * R2])
        m.emb_t = p.sb("emb_t", [2 * R2, NEURONS])
        m.w4 = p.sb("w4", [P, TILES, 2, 4])
        m.index4 = p.sb("index4", [P, TILES, 2, 4])
        m.slots = p.sb("slots", [P, TILES, 2, 4], U32)
        m.owner = p.sb("owner", [1, 2 * SLOT_TILES], I32)
        m.zt = m.arena[:, 0:PADDED]
        m.chosen = [m.arena[:, (1 + r) * PADDED:(2 + r) * PADDED] for r in range(2)]
        m.cum = [m.arena[:, (3 + r) * PADDED:(4 + r) * PADDED] for r in range(2)]
        m.hidden = m.arena[:, 0:PADDED].rearrange("q (t n) -> q t n", t=TILES)
        m.fk_in = nc.dram_tensor("fk_in", [SLOT_TILES * P, D], F32).ap()
        m.fk_out = nc.dram_tensor("fk_out", [SLOT_TILES * P, NEURONS], F32).ap()
        m.rk_in = nc.dram_tensor("rk_in", [SLOT_TILES * P, NEURONS], F32).ap()
        m.rk_out = nc.dram_tensor("rk_out", [SLOT_TILES * P, D], F32).ap()
        n = TILES * PATCH
        m.xt_patches = m.arena[:, n:n + GROUP * PATCH].rearrange("q (j d) -> q j d", j=GROUP)
        n += GROUP * PATCH
        m.w_tok = m.arena[:, n:n + PCH * D].rearrange("q (c d) -> q c d", c=PCH)
        p.stage(load_constants, m, a)
        p.stage(patch_tokens, m, a)
        p.stage(token_norm, m)
        p.stage(norm_and_turn, m, "n0", m.xn, m.xt)
        p.stage(project_qk, m, "qk0", m.w_qkv0, m.b_qk0, (m.sems["c_attn0"], m.n_attn0))
        p.stage(group_attention, m)
        p.stage(output_projection, m, "proj0", m.w_proj0, m.r_bproj0)
        p.stage(norm_and_turn, m, "n1", m.xn, m.xt)
        p.stage(embeddings, m)
        p.stage(route, m)
        p.stage(assign_slots, m)
        filled = (m.sems["c_fill"], 32)
        p.stage(scatter_rows, m, 0, m.xn, m.fk_in, filled)
        p.stage(neuron_tiles, m, 0, m.fk_in, a["L0_ffn_f_know"], m.fk_out, 2, DH, NEURONS)
        p.stage(combine, m, 0, m.fk_out, NEURONS, m.hidden, m.rk_in, filled)
        p.stage(neuron_tiles, m, 1, m.rk_in, a["L0_ffn_r_know"], m.rk_out, 1, P, D)
        p.stage(combine, m, 1, m.rk_out, D, m.h)
        p.stage(projection_bias, m)
        p.stage(norm_and_turn, m, "n2", m.xn, m.xt)
        p.stage(project_qk, m, "qk1", m.w_qkv1, m.b_qk1, (m.sems["c_attn1"], m.n_attn1))
        p.stage(sparse_attention, m)
        p.stage(output_projection, m, "proj1", m.w_proj1, m.r_bproj1)
        p.stage(norm_and_turn, m, "n3", m.xn, m.xt)
        p.stage(route_experts, m)
        p.stage(scatter_to_experts, m)
        p.stage(experts, m, a)
        p.stage(finish, m, out)


def _layouts(inputs):
    import numpy as np

    a = {n: np.ascontiguousarray(v) for n, v in inputs.items()}
    grid, side = 7, 16
    patches = a["x"].reshape(IMAGES, 3, grid, side, grid, side).transpose(0, 2, 4, 3, 5, 1)
    a["x"] = patches.reshape(TOKENS, PATCH)
    for n in ("L0_tok_ln1_g", "L0_tok_ln1_b"):
        a[n] = a[n].reshape(PCH, P).T
    a["L0_attn_b_qkv_cols"] = a["L0_attn_b_qkv"][:2 * D].reshape(4, DH).T
    a["L1_attn_qkv_w"], a["L1_attn_proj_w"] = a["L1_attn_qkv_w"].T, a["L1_attn_proj_w"].T
    a["L1_attn_qkv_b"] = a["L1_attn_qkv_b"].reshape(6, DH).T
    a["L0_ffn_f_know"] = a["L0_ffn_f_know"].reshape(NEURONS, 2, DH, NEURONS).transpose(0, 2, 1, 3).reshape(NEURONS, DH, 2 * NEURONS)
    a["L1_ffn_b1"] = a["L1_ffn_b1"].reshape(EXPERTS, HIDDEN // P, P).transpose(2, 0, 1)

    q = np.arange(P)
    columns = np.stack([q < SLOT, q >= SLOT])
    a["c_pair_row"] = columns.astype(np.float32)
    a["c_pair_bar"] = np.where(columns & (q % SLOT < SEQ), 0.0, -1e30).astype(np.float32)
    a["c_iota"] = np.arange(2 * P).astype(np.float32)
    a["c_upto"] = np.triu(np.ones((P, P), np.float32))
    a["c_head_mask"] = (np.arange(DH)[:, None] // HEAD == np.arange(HEADS // 2)).astype(np.float32)
    per_expert = P // EXPERTS
    a["c_group_ones"] = (q[:, None] // per_expert == q // per_expert).astype(np.float32)
    a["c_threshold"] = (q % per_expert).astype(np.float32)[:, None]
    a["c_slot_base"] = (q // per_expert * EXPERT_SLOTS).astype(np.float32)[:, None]
    a["c_own_row"] = (MOE_SLOTS + 1 + q[:, None] + P * np.arange(TILES)).astype(np.float32)
    return {n: np.ascontiguousarray(v) for n, v in a.items()}


def kernel(**inputs):
    import numpy as np
    import concourse.bacc as bacc
    from concourse.bass_utils import run_bass_kernel_spmd

    nc = bacc.Bacc("TRN2", target_bir_lowering=False, num_devices=1)
    arrays = _layouts(inputs)
    a = {n: nc.dram_tensor(n, v.shape, mybir.dt.from_np(v.dtype), kind="ExternalInput").ap() for n, v in arrays.items()}
    out = nc.dram_tensor("out", (TOKENS, D), F32, kind="ExternalOutput").ap()
    build(nc, a, out)
    r = run_bass_kernel_spmd(nc, [arrays], core_ids=[0])
    return r.results[0]["out"].reshape(IMAGES, SEQ, D)
```

```python
from contextlib import ExitStack

import concourse.bass as bass
from concourse import mybir

ALU = mybir.AluOpType
ACT = mybir.ActivationFunctionType
AX = mybir.AxisListType
F32 = mybir.dt.float32
I32 = mybir.dt.int32
U32 = mybir.dt.uint32

P = 128
IMAGES = 64
SEQ = 49
TOKENS = IMAGES * SEQ
TILES = -(-TOKENS // P)
PADDED = TILES * P
LAST = TOKENS - (TILES - 1) * P
GROUP = 5
TURNS = TILES // GROUP
D = 192
DH = D // 2
PATCH = 768
PCH = PATCH // P
PAIRS = IMAGES // 2
SLOT = 64
COLS = (IMAGES + 2) * SLOT
EPS = 1e-5
EXPERTS = 8
HIDDEN = 768
CAPACITY = int(1.25 * TOKENS / EXPERTS)
EXPERT_SLOTS = -(-CAPACITY // P) * P
MOE_SLOTS = EXPERTS * EXPERT_SLOTS
ROUNDS = 7
HEADS = 12
HEAD = D // HEADS
LOWEST, HIGHEST = -3.0e38, 3.0e38
R2 = 64
NEURONS = 128
NT_RING = 12
X_CHUNKS = 3
SLOT_TILES = -(-(4 * PADDED // P + NEURONS - 1) // NT_RING) * NT_RING


class Program:

    def __init__(self, nc, ctx):
        self.nc, self.ctx = nc, ctx
        self.of_stage, self.cleared = [], []
        self.software = {name: [nc.alloc_semaphore(f"{name}{i}") for i in range(n)] for name, n in (
            ("scatter0_sent", 1), ("nt0_stored", X_CHUNKS), ("comb0_gathered", GROUP), ("comb0_sent", 1),
            ("nt1_stored", X_CHUNKS), ("comb1_gathered", GROUP), ("comb1_sent", 1), ("moe_sent", 1), ("ex_stored", 2),
            ("fin_gathered", GROUP))}

    def sb(self, name, shape, dt=F32):
        return self.ctx.enter_context(self.nc.sbuf_tensor(name, shape, dt))

    def bank(self, name):
        return self.ctx.enter_context(self.nc.psum_tensor(name, [P, 512], F32))

    def lasting(self, name):
        return self.nc.alloc_semaphore(name)

    def sem(self, name):
        self.of_stage.append(self.nc.alloc_semaphore(name))
        return self.of_stage[-1]

    def stage(self, build, *args):
        self.of_stage = []
        build(self.nc, self, *args)
        for sem in self.cleared:
            self.nc.release_semaphore(sem)
        for sem in self.of_stage:
            self.nc.gpsimd.sem_clear(sem)
        self.cleared = self.of_stage


def row_to_all(dram_row, n, parts=P):
    return dram_row.rearrange("(a n) -> a n", a=1).broadcast_to([parts, n])


def load_constants(nc, p, m, a):
    s = m.sems
    for n in ("c_tok", "c_rows", "c_attn0", "c_ffn0", "c_attn1", "c_moe", "c_masks", "c_fill", "c_fill_moe", "c_ident", "out_stored"):
        s[n] = p.lasting(n)
    s["c_x"] = [p.lasting(f"c_x{g}") for g in range(TURNS)]
    with nc.Block() as block:

        @block.sync
        def _(sp):
            sp.dma_start(m.w_tok[:, :, :], a["L0_tok_W"].rearrange("(c q) d -> q c d", q=P)).then_inc(s["c_tok"], 16)
            sp.dma_start(m.g1[:, :], a["L0_tok_ln1_g"]).then_inc(s["c_tok"], 16)
            sp.dma_start(m.b1[:, :], a["L0_tok_ln1_b"]).then_inc(s["c_tok"], 16)
            for g in range(TURNS):
                t0 = g * GROUP
                n = GROUP if g < TURNS - 1 else GROUP - 1
                sp.dma_start(m.x_all[:, t0:t0 + n, :],
                             a["x"][t0 * P:(t0 + n) * P, :].rearrange("(t q) d -> q t d", q=P)).then_inc(s["c_x"][g], 16)
            for half in range(2):
                sp.dma_start(m.x_all[half * LAST:(half + 1) * LAST, TILES - 1, :],
                             a["x"][(TILES - 1) * P:TOKENS, :]).then_inc(s["c_x"][TURNS - 1], 16)

        @block.scalar
        def _(act):
            for name, dst in (("L0_tok_b", m.r_btok), ("L0_tok_ln2_g", m.r_g2), ("L0_tok_ln2_b", m.r_b2)):
                act.dma_start(dst[:, :], row_to_all(a[name], D)).then_inc(s["c_rows"], 16)

        @block.gpsimd
        def _(pool):
            pool.memset(m.ident[:, :], 0.0).then_inc(s["c_ident"], 1)
            pool.memset(m.minus_half[:, :], -0.5)
            pool.memset(m.plus_half[:, :], 0.5)
            pool.memset(m.ones[:, :], 1.0)
            pool.memset(m.zeros[:, :], 0.0).then_inc(s["c_ident"], 1)
            pool.wait_ge(s["c_ident"], 2)
            pool.affine_select(out=m.ident[:, :], in_=m.ident[:, :], compare_op=ALU.not_equal, fill=1.0,
                               base=0, pattern=[[-1, P]], channel_multiplier=1).then_inc(s["c_ident"], 1)


def load_later(sp, m, a):
    s = m.sems
    half = lambda w: w.rearrange("(h q) n -> q h n", h=2)
    for dst, src in ((m.w_qkv0[:, :, :], half(a["L0_attn_W_qkv"])), (m.w_gp[:, :, :], half(a["L0_attn_W_gp"])),
                     (m.w_proj0[:, :, :], half(a["L0_attn_W_proj"])), (m.b_qk0[:, :], a["L0_attn_b_qkv_cols"]),
                     (m.alpha[:, :], row_to_all(a["L0_attn_alpha"], 1)),
                     (m.r_bv0[:, :], row_to_all(a["L0_attn_b_qkv"][2 * D:3 * D], D)),
                     (m.r_bproj0[:, :], row_to_all(a["L0_attn_b_proj"], D))):
        sp.dma_start(dst, src).then_inc(s["c_attn0"], 16)
        m.n_attn0 += 16
    sp.dma_start(m.pair_row[:, :], a["c_pair_row"]).then_inc(s["c_masks"], 16)
    sp.dma_start(m.pair_bar[:, :], a["c_pair_bar"]).then_inc(s["c_masks"], 16)
    for dst, src in ((m.iota[:, :], row_to_all(a["c_iota"], 2 * P)), (m.upto[:, :], a["c_upto"]),
                     (m.w_route[:, :, 0:R2], a["L0_ffn_W_fk"].rearrange("(h q) n -> q h n", h=2)),
                     (m.w_route[:, :, R2:2 * R2], a["L0_ffn_W_rk"].rearrange("(h q) n -> q h n", h=2)),
                     (m.b_route[0:R2, :], a["L0_ffn_b_fk"].rearrange("(q a) -> q a", a=1)),
                     (m.b_route[R2:2 * R2, :], a["L0_ffn_b_rk"].rearrange("(q a) -> q a", a=1)),
                     (m.emb[:, 0:R2], a["L0_ffn_emb_fk"]), (m.emb[:, R2:2 * R2], a["L0_ffn_emb_rk"])):
        sp.dma_start(dst, src).then_inc(s["c_ffn0"], 16)
        m.n_ffn0 += 16
    for dst, src in ((m.w_switch[:, :, :], a["L1_ffn_switch_w"].rearrange("(h q) n -> q h n", h=2)),
                     (m.r_switch[:, :], row_to_all(a["L1_ffn_switch_b"], EXPERTS)),
                     (m.b_up[:, :, :], a["L1_ffn_b1"]), (m.group_ones[:, :], a["c_group_ones"]),
                     (m.group_before[:, :], a["c_group_before"]),
                     (m.threshold[:, :], a["c_threshold"]), (m.slot_base[:, :], a["c_slot_base"]),
                     (m.own_row[:, :], a["c_own_row"])):
        sp.dma_start(dst, src).then_inc(s["c_moe"], 16)
        m.n_moe += 16
    for dst, src in ((m.w_qkv1[:, :, :], half(a["L1_attn_qkv_w"])), (m.w_proj1[:, :, :], half(a["L1_attn_proj_w"])),
                     (m.b_qk1[:, :], a["L1_attn_qkv_b"][:, 0:4]), (m.b_v1[:, :], a["L1_attn_qkv_b"][:, 4:6]),
                     (m.r_bproj1[:, :], row_to_all(a["L1_attn_proj_b"], D)),
                     (m.score_scale[:, :], row_to_all(a["L1_attn_temperature"], 1)),
                     (m.head_mask[:, :], a["c_head_mask"])):
        sp.dma_start(dst, src).then_inc(s["c_attn1"], 16)
        m.n_attn1 += 16

    sp.wait_ge(s["c_ident"], 2)
    for g in range(TURNS):
        sp.wait_ge(s["c_x"][g], 16 if g < TURNS - 1 else 48)
    sp.wait_ge(s["c_rows"], 48)
    for dram, n in ((m.fk_in, D), (m.rk_in, NEURONS)):
        sp.dma_start(dram.rearrange("(t q) d -> q t d", q=P),
                     m.zeros[:, 0:n].unsqueeze(1).broadcast_to([P, SLOT_TILES, n])).then_inc(s["c_fill"], 16)
    sp.dma_start(m.moe_in[0:MOE_SLOTS, :].rearrange("(t q) d -> q t d", q=P),
                 m.zeros[:, 0:D].unsqueeze(1).broadcast_to([P, MOE_SLOTS // P, D])).then_inc(s["c_fill_moe"], 16)


def tiles(t0, n=1):
    return bass.ds(t0, n)


def one(ap):
    return ap.rearrange("q a n -> q (a n)")


def rstd_of_variance(pool, m, mv, rstd, now, n, sem, before):
    pool.tensor_scalar(rstd[:, now], mv[:, now, 1], EPS, None, ALU.add).then_inc(sem, 1)
    pool.wait_ge(sem, before + 1)
    pool.tensor_tensor(rstd[:, now], rstd[:, now], m.minus_half[:, 0:n], ALU.pow).then_inc(sem, 1)
    pool.wait_ge(sem, before + 2)


def row_statistics(dve, m, mv, g, rows_ready, part, aggregated, stats, passed):
    bn = m.bn[:, 64:64 + GROUP * 6].rearrange("q (j n) -> q j n", j=GROUP)
    dve.wait_ge(*rows_ready).then_inc(passed, 1)
    for j in range(GROUP):
        ins = dve.bn_stats(bn[:, j, :], m.h[:, tiles(g * GROUP + j), :])
    ins.then_inc(part, 1)
    dve.wait_ge(part, g + 1).then_inc(passed, 1)
    for j in range(GROUP):
        ins = dve.bn_aggr(m.mv_group[:, j, :], bn[:, j, :])
    ins.then_inc(aggregated, 1)
    dve.wait_ge(aggregated, g + 1)
    dve.tensor_copy(mv[:, tiles(g * GROUP, GROUP), :], m.mv_group[:, :, :]).then_inc(stats, 1)
    dve.wait_ge(stats, g + 1)


def patch_tokens(nc, p, m, a):
    s = m.sems
    folded, bias_ready, stats_part, stats_ready, rstd_step, shift_ready, xn_ready, turned, xt_ready, y_ready, \
        y_biased, y_part, y_stats, aggregated, y_aggregated, passed, rstd2_step = [p.sem("tok_" + n) for n in (
            "folded", "bias_ready", "stats_part", "stats_ready", "rstd_step", "shift_ready", "xn_ready", "turned",
            "xt_ready", "y_ready", "y_biased", "y_part", "y_stats", "aggregated", "y_aggregated", "passed", "rstd2_step")]
    AHEAD = 3
    xt = m.xt_patches
    bn = m.bn[:, 0:GROUP * 12].rearrange("q (j n) -> q j n", j=GROUP)

    def xt_ps(j, lo, hi):
        bank = m.bank[2 * (j % 2) + lo // 4]
        return bank[:, (lo % 4) * P:(lo % 4 + hi - lo) * P]

    def y_ps(j):
        return m.bank[4 + j % 4][:, 0:D]

    with nc.Block() as block:

        @block.sync
        def _(sp):
            load_later(sp, m, a)

        @block.vector
        def _(dve):
            def patch_stats(g):
                for j in range(GROUP):
                    for h in range(2):
                        ins = dve.bn_stats(bn[:, j, 6 * h:6 * h + 6],
                                           m.x_all[:, tiles(g * GROUP + j), h * 384:(h + 1) * 384])
                ins.then_inc(stats_part, 1)
                dve.wait_ge(stats_part, g + 1).then_inc(passed, 1)
                for j in range(GROUP):
                    ins = dve.bn_aggr(m.mv_group[:, j, :], bn[:, j, :])
                ins.then_inc(aggregated, 1)
                dve.wait_ge(aggregated, g + 1)
                dve.tensor_copy(m.mv[:, tiles(g * GROUP, GROUP), :], m.mv_group[:, :, :]).then_inc(stats_ready, 1)
                dve.wait_ge(stats_ready, g + 1).then_inc(passed, 1)

            def token_rows(g):
                for j in range(GROUP):
                    dve.wait_ge(y_ready, g * GROUP + j + 1)
                    dve.tensor_tensor(one(m.h[:, tiles(g * GROUP + j), :]), y_ps(j), m.r_btok[:, :],
                                      ALU.add).then_inc(y_biased, 1)
                row_statistics(dve, m, m.mv2, g, (y_biased, g * GROUP + GROUP), y_part, y_aggregated, y_stats, passed)

            dve.wait_ge(s["c_x"][0], 16)
            patch_stats(0)

            dve.wait_ge(s["c_tok"], 48)
            dve.wait_ge(s["c_rows"], 48)
            dve.wait_ge(bias_ready, 1)
            dve.tensor_tensor(m.r_btok[:, :], m.r_btok[:, :], m.bank[7][:, 0:D], ALU.add)
            for c in range(PCH):
                ins = dve.tensor_scalar(m.w_tok[:, c, :], m.w_tok[:, c, :], m.g1[:, c:c + 1], None, ALU.mult)
            ins.then_inc(folded, 1)

            for g in range(1, AHEAD):
                dve.wait_ge(s["c_x"][g], 16)
                patch_stats(g)
            for g in range(AHEAD, TURNS):
                dve.wait_ge(s["c_x"][g], 16 if g < TURNS - 1 else 48)
            with dve.Fori(0, TURNS - AHEAD) as g:
                token_rows(g)
                patch_stats(g + AHEAD)
            for g in range(TURNS - AHEAD, TURNS):
                token_rows(g)

        @block.gpsimd
        def _(pool):
            def patches(g):
                now = slice(g * GROUP, (g + 1) * GROUP)
                pool.wait_ge(stats_ready, g + 1)
                rstd_of_variance(pool, m, m.mv, m.rstd, now, GROUP, rstd_step, 2 * g)
                pool.tensor_tensor(m.shift[:, now], m.mv[:, now, 0], m.rstd[:, now], ALU.mult).then_inc(shift_ready, 1)
                pool.wait_ge(shift_ready, 2 * g + 1)
                pool.tensor_scalar(m.shift[:, now], m.shift[:, now], -1.0, None, ALU.mult).then_inc(shift_ready, 1)

            for g in range(AHEAD):
                patches(g)
            for g in range(TURNS):
                pool.wait_ge(y_stats, g + 1)
                rstd_of_variance(pool, m, m.mv2, m.rstd2, slice(g * GROUP, (g + 1) * GROUP), GROUP, rstd2_step, 2 * g)
                if g + AHEAD < TURNS:
                    patches(g + AHEAD)

        @block.scalar
        def _(act):
            def normalise(g, j):
                act.wait_ge(shift_ready, 2 * g + 2)
                act.activation(m.xn_patches[:, j, :], one(m.x_all[:, tiles(g * GROUP + j), :]), ACT.Identity, bias=m.shift[:, tiles(g * GROUP + j)],
                               scale=m.rstd[:, tiles(g * GROUP + j)]).then_inc(xn_ready, 1)

            def lift(g, j, before):
                act.wait_ge(turned, g * GROUP + j + 1)
                if before is not None:
                    act.wait_ge(y_ready, before + j + 1)
                act.activation(xt[:, j, 0:4 * P], xt_ps(j, 0, 4), ACT.Copy)
                act.activation(xt[:, j, 4 * P:6 * P], xt_ps(j, 4, 6), ACT.Copy).then_inc(xt_ready, 1)

            for j in range(GROUP):
                normalise(0, j)
            for j in range(GROUP):
                lift(0, j, None)
                normalise(1, j)
            with act.Fori(0, TURNS - 2) as g:
                for j in range(GROUP):
                    lift(g + 1, j, g * GROUP)
                    normalise(g + 2, j)
            for j in range(GROUP):
                lift(TURNS - 1, j, (TURNS - 2) * GROUP)

        @block.tensor
        def _(pe):
            pe.wait_ge(s["c_tok"], 48)
            for c in range(PCH):
                mm = pe.matmul(m.bank[7][:, 0:D], m.b1[:, c:c + 1].broadcast_to([P, P]), m.w_tok[:, c, :],
                               start=(c == 0), stop=(c == PCH - 1))
            mm.then_inc(bias_ready, 1)

            def turn(g, j):
                pe.wait_ge(xn_ready, g * GROUP + j + 1)
                pe.wait_ge(xt_ready, g * GROUP + (j - 1 if j >= 2 else 0))
                for c in range(PCH):
                    mm = pe.transpose(xt_ps(j, c, c + 1), m.xn_patches[:, j, c * P:(c + 1) * P],
                                      m.ident[:, :])
                mm.then_inc(turned, 1)

            def project(g, j):
                pe.wait_ge(xt_ready, g * GROUP + j + 1)
                pe.wait_ge(y_biased, g * GROUP + j // 4)
                for c in range(PCH):
                    mm = pe.matmul(y_ps(j), xt[:, j, c * P:(c + 1) * P], m.w_tok[:, c, :],
                                   start=(c == 0), stop=(c == PCH - 1))
                mm.then_inc(y_ready, 1)

            pe.wait_ge(s["c_ident"], 3)
            pe.wait_ge(folded, 1)
            turn(0, 0)
            with pe.Fori(0, TURNS - 1) as g:
                for j in range(GROUP):
                    turn(g + (j + 1) // GROUP, (j + 1) % GROUP)
                    project(g, j)
            for j in range(GROUP):
                if j + 1 < GROUP:
                    turn(TURNS - 1, j + 1)
                project(TURNS - 1, j)


class Embeddings:

    def __init__(self, p, m):
        self.m = m
        self.step, self.pstep, self.turned = [p.sem("emb_" + n) for n in ("step", "pstep", "turned")]
        self.norm = m.mv_group[:, 0, :]

    def normalise(self, dve):
        m, norm = self.m, self.norm
        halves = [slice(r * R2, (r + 1) * R2) for r in range(2)]
        dve.wait_ge(m.sems["c_ffn0"], m.n_ffn0)
        for r, half in enumerate(halves):
            ins = dve.tensor_tensor_reduce(m.bn[:, half], m.emb[:, half], m.emb[:, half], 1.0, 0.0, ALU.mult, ALU.add,
                                           norm[:, r:r + 1])
        ins.then_inc(self.step, 1)
        dve.wait_ge(self.pstep, 2)
        dve.reciprocal(norm, norm).then_inc(self.step, 1)
        dve.wait_ge(self.step, 2)
        for r, half in enumerate(halves):
            ins = dve.tensor_scalar(m.emb[:, half], m.emb[:, half], norm[:, r:r + 1], None, ALU.mult)
        ins.then_inc(self.step, 1)
        dve.wait_ge(self.turned, 1)
        dve.tensor_copy(m.emb_t[:, :], m.bank[4][:, 0:P])

    def norms(self, pool):
        m, norm = self.m, self.norm
        pool.wait_ge(self.step, 1)
        pool.tensor_tensor(norm, norm, m.plus_half[:, 0:2], ALU.pow).then_inc(self.pstep, 1)
        pool.wait_ge(self.pstep, 1)
        pool.tensor_scalar(norm, norm, 1e-8, None, ALU.add).then_inc(self.pstep, 1)

    def turn(self, pe):
        pe.wait_ge(self.step, 3)
        pe.transpose(self.m.bank[4][:, 0:P], self.m.emb[:, :], self.m.ident[:, :]).then_inc(self.turned, 1)


def token_norm(nc, p, m):
    centred, scaled, shifted, part, aggregated, stats, passed = [p.sem("tn_" + n) for n in (
        "centred", "scaled", "shifted", "part", "aggregated", "stats", "passed")]
    ln = LayerNorm(p, m, "n0", stats)
    qk = Projection(p, m, "qk0", m.w_qkv0, m.b_qk0, (m.sems["c_attn0"], m.n_attn0), ln.lifted)
    emb = Embeddings(p, m)

    with nc.Block() as block:

        @block.gpsimd
        def _(pool):
            qk.clear_gaps(pool)
            for g in range(TURNS):
                ln.rstd(pool, g)
            emb.norms(pool)

        @block.vector
        def _(dve):
            gamma = m.r_g2[:, :].unsqueeze(1).broadcast_to([P, GROUP, D])
            beta = m.r_b2[:, :].unsqueeze(1).broadcast_to([P, GROUP, D])

            def group(g):
                rows = m.h[:, tiles(g * GROUP, GROUP), :]
                for j in range(GROUP):
                    t = tiles(g * GROUP + j)
                    ins = dve.tensor_scalar(one(m.h[:, t, :]), one(m.h[:, t, :]), one(m.mv2[:, t, 0:1]),
                                            m.rstd2[:, t], ALU.subtract, ALU.mult)
                ins.then_inc(centred, 1)
                dve.wait_ge(centred, g + 1)
                dve.tensor_tensor(rows, rows, gamma, ALU.mult).then_inc(scaled, 1)
                dve.wait_ge(scaled, g + 1)
                dve.tensor_tensor(rows, rows, beta, ALU.add).then_inc(shifted, 1)
                row_statistics(dve, m, m.mv, g, (shifted, g + 1), part, aggregated, stats, passed)

            by_groups(dve, group, lambda g: ln.rows(dve, g))
            emb.normalise(dve)

        @block.tensor
        def _(pe):
            for g in range(TURNS):
                ln.turn(pe, g)
                qk.project(pe, g)
            emb.turn(pe)

        @block.scalar
        def _(act):
            for g in range(TURNS):
                ln.lift(act, g)
                qk.take(act, g)


class LayerNorm:

    def __init__(self, p, m, name, stats, banks=(5, 6, 7)):
        self.m, self.stats, self.banks = m, stats, banks
        self.rstd_step, self.xn_ready, self.turned, self.lifted = [p.sem(f"{name}_{n}") for n in (
            "rstd_step", "xn_ready", "turned", "lifted")]

    def rstd(self, pool, g):
        pool.wait_ge(self.stats, g + 1)
        rstd_of_variance(pool, self.m, self.m.mv, self.m.rstd, slice(g * GROUP, (g + 1) * GROUP), GROUP,
                         self.rstd_step, 2 * g)

    def rows(self, dve, g):
        m = self.m
        dve.wait_ge(self.rstd_step, 2 * g + 2)
        for j in range(GROUP):
            now = tiles(g * GROUP + j)
            dve.tensor_scalar(one(m.xn[:, now, :]), one(m.h[:, now, :]), one(m.mv[:, now, 0:1]), m.rstd[:, now],
                              ALU.subtract, ALU.mult).then_inc(self.xn_ready, 1)

    def turn(self, pe, g):
        m, n = self.m, len(self.banks)
        for t in range(g * GROUP, (g + 1) * GROUP):
            pe.wait_ge(self.xn_ready, t + 1)
            if t >= n:
                pe.wait_ge(self.lifted, t - n + 1)
            for c in range(2):
                mm = pe.transpose(m.bank[self.banks[t % n]][0:DH, c * P:(c + 1) * P], m.xn[:, t, c * DH:(c + 1) * DH],
                                  m.ident[:, :])
            mm.then_inc(self.turned, 1)

    def lift(self, act, g):
        m = self.m
        for t in range(g * GROUP, (g + 1) * GROUP):
            act.wait_ge(self.turned, t + 1)
            act.activation(m.xt[:, :, t * P:(t + 1) * P],
                           m.bank[self.banks[t % len(self.banks)]][0:DH, 0:2 * P].rearrange("q (c n) -> q c n", c=2),
                           ACT.Copy).then_inc(self.lifted, 1)


def by_groups(eng, make, rows):
    make(0)
    with eng.Fori(0, TURNS - 1) as g:
        make(g + 1)
        rows(g)
    rows(TURNS - 1)


class Projection:

    PER = 8
    N = PER * SEQ

    def __init__(self, p, m, name, w, bias, loaded, lifted, late=()):
        self.late = late
        self.m, self.w, self.bias, self.loaded, self.lifted = m, w, bias, loaded, lifted
        self.ready, self.out = [p.sem(f"{name}_{n}") for n in ("ready", "out")]

    def clear_gaps(self, eng):
        for x in (self.m.qt, self.m.kt, self.m.xs):
            eng.memset(x[:, :, :].rearrange("q h (i k) -> q h i k", k=SLOT)[:, :, :, SEQ:SLOT], 0.0)

    def turns(self, g):
        done = lambda g: min(IMAGES // self.PER, g * GROUP * P // self.N)
        return range(done(g), done(g + 1))

    def project(self, pe, g):
        m = self.m
        if g == 0:
            pe.wait_ge(*self.loaded)
        pe.wait_ge(self.lifted, (g + 1) * GROUP)
        for c in self.turns(g):
            if c in self.late:
                continue
            for o in range(4):
                if c:
                    pe.wait_ge(self.out, 4 * (c - 1) + o + 1)
                for h in range(2):
                    mm = pe.matmul(m.bank[o][0:DH, 0:self.N], self.w[:, h, o * DH:(o + 1) * DH],
                                   m.xt[:, h, c * self.N:(c + 1) * self.N], start=(h == 0), stop=(h == 1))
                mm.then_inc(self.ready, 1)

    def take(self, act, g):
        m = self.m
        if g == 0:
            act.wait_ge(*self.loaded)
        act.wait_ge(self.lifted, (g + 1) * GROUP)
        for c in self.turns(g):
            columns = slice((c * self.PER + 1) * SLOT, ((c + 1) * self.PER + 1) * SLOT)
            by_image = lambda x, h: x[:, h, columns].rearrange("q (i k) -> q i k", k=SLOT)[:, :, 0:SEQ]
            for h in range(2):
                act.activation(by_image(m.xs, h), m.xt[:, h, c * self.N:(c + 1) * self.N]
                               .rearrange("q (i k) -> q i k", k=SEQ), ACT.Copy)
            for o in range(4) if c not in self.late else ():
                act.wait_ge(self.ready, 4 * c + o + 1)
                act.activation(by_image(m.qt if o < 2 else m.kt, o % 2),
                               m.bank[o][0:DH, 0:self.N].rearrange("q (i k) -> q i k", k=SEQ),
                               ACT.Identity, bias=self.bias[:, o:o + 1]).then_inc(self.out, 1)


class LateProjection:

    TURNS = range((TURNS - 1) * GROUP * P // Projection.N - 1, IMAGES // Projection.PER)
    STEPS = 4 * len(TURNS)
    FIRST_PAIR = TURNS[0] * Projection.PER // 2

    def __init__(self, p, m, bank):
        self.m, self.bank = m, bank[0:DH, 0:Projection.N]
        self.ready, self.out = [p.sem("late_" + n) for n in ("ready", "out")]

    def product(self, pe, step):
        m, c, o = self.m, self.TURNS[step // 4], step % 4
        for h in range(2):
            mm = pe.matmul(self.bank, m.w_qkv1[:, h, o * DH:(o + 1) * DH],
                           m.xt[:, h, c * Projection.N:(c + 1) * Projection.N], start=(h == 0), stop=(h == 1))
        mm.then_inc(self.ready, 1)

    def take(self, act, turn, o):
        m = self.m
        at = o * COLS + (self.TURNS[turn] * Projection.PER + 1) * SLOT
        act.wait_ge(self.ready, o + (4 * turn + 1))
        act.activation(m.qk[:, bass.ds(at, Projection.PER * SLOT)].rearrange("q (i k) -> q i k", k=SLOT)[:, :, 0:SEQ],
                       self.bank.rearrange("q (i k) -> q i k", k=SEQ),
                       ACT.Identity, bias=m.b_qk1[:, bass.ds(o, 1)]).then_inc(self.out, 1)


def pair_columns(x, h, i):
    return x[:, h, (2 * i + 1) * SLOT:(2 * i + 3) * SLOT]


def group_attention(nc, p, m):
    s = m.sems
    names = ("scores_ready", "row_max", "shift_ready", "v_out", "group_exp", "score_exp", "group_sum", "group_weights",
             "groups_turned", "groups_out", "group_ready", "mixed", "sum_inverse", "weights_ready", "weights_turned",
             "weights_out", "heads_ready", "heads_out", "gate", "v_ready")
    (scores_ready, row_max, shift_ready, v_out, group_exp, score_exp, group_sum, group_weights, groups_turned,
     groups_out, group_ready, mixed, sum_inverse, weights_ready, weights_turned, weights_out, heads_ready,
     heads_out, gate, v_ready) = [p.sem("a0_" + n) for n in names]
    SCALE = float(D) ** -0.5
    with ExitStack() as mem:
        sb = lambda n, shape: mem.enter_context(nc.sbuf_tensor("a0_" + n, shape, F32))
        v = sb("v", [P, 2, D])
        probs = sb("probs", [P, 2, P])
        weights = sb("weights", [P, P])
        weights_t = sb("weights_t", [P, P])
        mix = sb("mix", [P, P])
        ge = sb("ge", [P, 2, SEQ])
        gw = sb("gw", [P, 2, SEQ])
        gw_t = sb("gw_t", [SEQ, P])
        peak = sb("peak", [P, 2, 2])
        shift = sb("shift", [P, 2, 2])
        total = sb("total", [P, 2, 2])
        inverse = sb("inverse", [P, 2, 2])
        a_col = sb("a_col", [P, 3])
        S, GL, V, GT, G, WT, O = [m.bank[0], m.bank[1]], m.bank[2], m.bank[3], m.bank[4], m.bank[5], m.bank[6], m.bank[7]

        with nc.Block() as block:

            @block.tensor
            def _(pe):
                def scores(i):
                    if i >= 2:
                        pe.wait_ge(score_exp, i - 1)
                    if i >= 1:
                        pe.wait_ge(group_exp, i)
                    for h in range(2):
                        pe.matmul(S[i % 2][:, 0:P], pair_columns(m.qt, h, i), pair_columns(m.kt, h, i),
                                  start=(h == 0), stop=False)
                    pe.matmul(S[i % 2][:, 0:P], m.pair_row[:, :], m.pair_bar[:, :], start=False, stop=True)
                    for h in range(2):
                        mm = pe.matmul(GL[:, 0:SEQ], pair_columns(m.qt, h, i), m.w_gp[:, h, :], start=(h == 0), stop=(h == 1))
                    mm.then_inc(scores_ready, 1)

                def values(i):
                    if i:
                        pe.wait_ge(v_out, i)
                    for h in range(2):
                        mm = pe.matmul(V[:, 0:D], pair_columns(m.xs, h, i), m.w_qkv0[:, h, 2 * D:3 * D],
                                       start=(h == 0), stop=(h == 1))
                    mm.then_inc(v_ready, 1)

                def turn_groups(i):
                    pe.wait_ge(group_weights, i + 1)
                    if i:
                        pe.wait_ge(groups_out, i)
                    pe.transpose(GT[0:SEQ, 0:P], gw[:, i % 2, :], m.ident[:, :]).then_inc(groups_turned, 1)

                def group(i):
                    pe.wait_ge(groups_out, i + 1)
                    if i:
                        pe.wait_ge(mixed, i)
                    pe.matmul(G[:, 0:P], gw_t[:, :], gw_t[:, :], start=True, stop=True).then_inc(group_ready, 1)

                def turn_weights(i):
                    pe.wait_ge(weights_ready, i + 1)
                    if i:
                        pe.wait_ge(weights_out, i)
                    pe.transpose(WT[:, 0:P], weights[:, :], m.ident[:, :]).then_inc(weights_turned, 1)

                def heads(i):
                    pe.wait_ge(weights_out, i + 1)
                    if i:
                        pe.wait_ge(heads_out, i)
                    for h in range(2):
                        mm = pe.matmul(O[0:DH, h * P:(h + 1) * P], v[:, i % 2, h * DH:(h + 1) * DH], weights_t[:, :],
                                       start=True, stop=True)
                    mm.then_inc(heads_ready, 1)

                pe.wait_ge(s["c_attn0"], m.n_attn0)
                pe.wait_ge(s["c_masks"], 32)
                scores(0)
                values(0)
                turn_groups(0)
                for i in range(PAIRS):
                    group(i)
                    if i + 1 < PAIRS:
                        scores(i + 1)
                    turn_weights(i)
                    if i + 1 < PAIRS:
                        values(i + 1)
                        turn_groups(i + 1)
                    heads(i)

            def over_pairs(eng, before, body, ahead):
                before()
                with eng.Fori(0, PAIRS // 2 - 1) as g:
                    for u in range(2):
                        body(2 * g + u, u, lambda: ahead(2 * g + u + 1, 1 - u))
                body(PAIRS - 2, 0, lambda: ahead(PAIRS - 1, 1))
                body(PAIRS - 1, 1, lambda: None)

            @block.vector
            def _(dve):
                dve.wait_ge(gate, 1)
                dve.tensor_scalar(a_col[:, 1:2], a_col[:, 0:1], 1.0, None, ALU.add).then_inc(gate, 1)
                dve.wait_ge(gate, 2)
                dve.reciprocal(a_col[:, 0:1], a_col[:, 1:2]).then_inc(gate, 1)
                dve.wait_ge(gate, 3)
                dve.tensor_scalar(a_col[:, 1:2], a_col[:, 0:1], -1.0, 1.0, ALU.mult, ALU.add).then_inc(gate, 1)
                dve.wait_ge(gate, 4)

                def maxima(i, u, first=False):
                    dve.wait_ge(scores_ready, i + 1)
                    dve.reduce_max(peak[:, u, 0:1], S[u][:, 0:P], AX.X)
                    dve.reduce_max(peak[:, u, 1:2], GL[:, 0:SEQ], AX.X).then_inc(row_max, 1)
                    dve.wait_ge(row_max, i + 1)
                    dve.tensor_scalar(shift[:, u, 0:1], peak[:, u, 0:1], -SCALE, None, ALU.mult)
                    dve.tensor_scalar(shift[:, u, 1:2], peak[:, u, 1:2], -1.0, None, ALU.mult).then_inc(shift_ready, 1)
                    dve.wait_ge(group_exp, i + 1)
                    dve.reciprocal(inverse[:, u, 1:2], total[:, u, 1:2]).then_inc(group_sum, 1)
                    dve.wait_ge(group_sum, i + 1)
                    dve.tensor_scalar(gw[:, u, :], ge[:, u, :], inverse[:, u, 1:2], None, ALU.mult).then_inc(group_weights, 1)
                    dve.wait_ge(v_ready, i + 1)
                    if not first:
                        dve.wait_ge(heads_ready, i - 1)
                    dve.tensor_tensor(v[:, u, :], V[:, 0:D], m.r_bv0[:, :], ALU.add).then_inc(v_out, 1)

                def mix_in(i, u, ahead):
                    dve.wait_ge(group_ready, i + 1)
                    dve.tensor_scalar(mix[:, :], G[:, 0:P], a_col[:, 1:2], a_col[:, 0:1], ALU.mult, ALU.add)\
                        .then_inc(mixed, 1)
                    dve.wait_ge(score_exp, i + 1)
                    dve.reciprocal(inverse[:, u, 0:1], total[:, u, 0:1]).then_inc(sum_inverse, 1)
                    dve.wait_ge(sum_inverse, i + 1)
                    dve.wait_ge(mixed, i + 1)
                    dve.wait_ge(weights_turned, i)
                    dve.scalar_tensor_tensor(weights[:, :], mix[:, :], inverse[:, u, 0:1], probs[:, u, :], ALU.mult,
                                             ALU.mult).then_inc(weights_ready, 1)
                    ahead()

                over_pairs(dve, lambda: maxima(0, 0, True), mix_in, maxima)

            @block.scalar
            def _(act):
                act.wait_ge(s["c_attn0"], m.n_attn0)
                act.activation(a_col[:, 0:1], m.alpha[:, :], ACT.Exp, scale=-1.0).then_inc(gate, 1)

                def exps(i, u):
                    act.wait_ge(shift_ready, i + 1)
                    act.activation(ge[:, u, :], GL[:, 0:SEQ], ACT.Exp, bias=shift[:, u, 1:2],
                                   accum_out=total[:, u, 1:2]).then_inc(group_exp, 1)
                    act.activation(probs[:, u, :], S[u][:, 0:P], ACT.Exp, bias=shift[:, u, 0:1], scale=SCALE,
                                   accum_out=total[:, u, 0:1]).then_inc(score_exp, 1)

                def lift_groups(i, u):
                    act.wait_ge(groups_turned, i + 1)
                    act.wait_ge(group_ready, i)
                    act.activation(gw_t[:, :], GT[0:SEQ, 0:P], ACT.Copy).then_inc(groups_out, 1)

                def body(i, u, ahead):
                    act.wait_ge(weights_turned, i + 1)
                    act.wait_ge(heads_ready, i)
                    act.activation(weights_t[:, :], WT[:, 0:P], ACT.Copy).then_inc(weights_out, 1)
                    ahead()
                    for x in pending:
                        lift_groups(*x)
                    pending.clear()
                    act.wait_ge(heads_ready, i + 1)
                    src = O[0:DH, 0:2 * P].rearrange("q (h a k) -> q h a k", h=2, a=2)
                    dst = m.at[:, :, bass.ds(i * 2 * SEQ, 2 * SEQ)].rearrange("q h (a k) -> q h a k", a=2)
                    for h in range(2):
                        ins = act.activation(dst[:, h], src[:, h, :, 0:SEQ], ACT.Copy)
                    ins.then_inc(heads_out, 1)

                def ahead(i, u):
                    exps(i, u)
                    pending.append((i, u))

                pending = []

                def both(i, u, nxt):
                    body(i, u, nxt)

                def before():
                    exps(0, 0)
                    lift_groups(0, 0)

                over_pairs(act, before, both, ahead)


def output_projection(nc, p, m, name, w, r_bias, w_next=None):
    ready, with_bias, added, part, aggregated, stats, passed = [p.sem(f"{name}_{n}") for n in (
        "ready", "with_bias", "added", "part", "aggregated", "stats", "passed")]
    ln = LayerNorm(p, m, name, stats, (5, 6, 7) if w_next is None else (5, 6))

    with nc.Block() as block:

        @block.tensor
        def _(pe):
            def project(g):
                for t in range(g * GROUP, (g + 1) * GROUP):
                    if t >= GROUP:
                        pe.wait_ge(added, t - GROUP + 1)
                    for h in range(2):
                        mm = pe.matmul(m.bank[t % GROUP][:, 0:D], m.at[:, h, t * P:(t + 1) * P], w[:, h, :],
                                       start=(h == 0), stop=(h == 1))
                    mm.then_inc(ready, 1)

            if w_next is not None:
                pe.wait_ge(m.sems["c_moe"], m.n_moe)
            project(0)
            project(1)
            for g in range(TURNS):
                if g + 2 < TURNS:
                    project(g + 2)
                ln.turn(pe, g)
                if w_next is not None:
                    pe.wait_ge(ln.lifted, (g + 1) * GROUP)
                    for t in range(g * GROUP, (g + 1) * GROUP):
                        for h in range(2):
                            pe.matmul(m.bank[7][:, t * EXPERTS:(t + 1) * EXPERTS], m.xt[:, h, t * P:(t + 1) * P],
                                      w_next[:, h, :], start=(h == 0), stop=(h == 1))

        @block.gpsimd
        def _(pool):
            with pool.Fori(0, TURNS) as g:
                rows = m.h[:, tiles(g * GROUP, GROUP), :]
                pool.tensor_tensor(rows, rows, r_bias[:, :].unsqueeze(1).broadcast_to([P, GROUP, D]), ALU.add)\
                    .then_inc(with_bias, 1)
            for g in range(TURNS):
                ln.rstd(pool, g)

        @block.scalar
        def _(act):
            for g in range(TURNS):
                ln.lift(act, g)

        @block.vector
        def _(dve):
            def group(g):
                dve.wait_ge(with_bias, g + 1)
                for j in range(GROUP):
                    dve.wait_ge(ready, g * GROUP + j + 1)
                    row = one(m.h[:, tiles(g * GROUP + j), :])
                    dve.tensor_tensor(row, row, m.bank[j][:, 0:D], ALU.add).then_inc(added, 1)
                row_statistics(dve, m, m.mv, g, (added, g * GROUP + GROUP), part, aggregated, stats, passed)

            by_groups(dve, group, lambda g: ln.rows(dve, g))


def over_tiles(eng, tile):
    with eng.Fori(0, TILES // 2) as g:
        for b in range(2):
            tile(g, b)
    tile(TILES // 2, 0)


def route(nc, p, m):
    (z_ready, z_out, logits_ready, top, index, shifted, exp_done, mark, four_set, hot, hot_turned, hot_out, less, e4, dsum,
     denom, inverse, passed) = [p.sem("route_" + n) for n in (
         "z_ready", "z_out", "logits_ready", "top", "index", "shifted", "exp_done", "mark", "four_set", "hot",
         "hot_turned", "hot_out", "less", "e4", "dsum", "denom", "inverse", "passed")]
    N = PADDED // 8
    with ExitStack() as mem:
        sb = lambda n, shape, dt=F32: mem.enter_context(nc.sbuf_tensor("route_" + n, shape, dt))
        top8 = sb("top8", [P, 2, 2, 8])
        index8 = sb("index8", [P, 2, 2, 8], U32)
        scratch = sb("scratch", [P, 2, 2, P])
        shift = sb("shift", [P, TILES, 2])
        total = sb("total", [P, TILES, 2])
        sum4 = sb("sum4", [P, TILES, 2])
        onehot = sb("onehot", [P, 2, 2, P])
        marked = sb("marked", [P, 2, P])
        four = sb("four", [P, 2, 2, 8])
        zt = m.zt

        with nc.Block() as block:

            @block.tensor
            def _(pe):
                with pe.Fori(0, 4) as c:
                    for b in range(2):
                        pe.wait_ge(z_out, 2 * c)
                        for h in range(2):
                            mm = pe.matmul(m.bank[b][:, 0:N], m.w_route[:, h, :], m.xt[:, h, bass.ds((2 * c + b) * N, N)],
                                           start=(h == 0), stop=(h == 1))
                        mm.then_inc(z_ready, 1)
                pe.wait_ge(z_out, 8)

                def turn(t):
                    for r in range(2):
                        pe.wait_ge(hot, 2 * t + r + 1)
                        if t >= 2:
                            pe.wait_ge(hot_out, 2 * (t - 2) + r + 1)
                        pe.transpose(m.bank[4 + 2 * r + t % 2][:, 0:P], onehot[:, t % 2, r, :], m.ident[:, :])\
                            .then_inc(hot_turned, 1)
                for t in range(TILES):
                    for r in range(2):
                        if t >= 2:
                            pe.wait_ge(exp_done, 2 * (t - 2) + r + 1)
                        q = slice(r * R2, (r + 1) * R2)
                        pe.matmul(m.bank[2 * (t % 2) + r][:, 0:P], zt[q, t * P:(t + 1) * P], m.emb_t[q, :],
                                  start=True, stop=True).then_inc(logits_ready, 1)
                    if t:
                        turn(t - 1)
                turn(TILES - 1)

            @block.scalar
            def _(act):
                with act.Fori(0, 4) as c:
                    for b in range(2):
                        act.wait_ge(z_ready, 2 * c + b + 1)
                        act.activation(zt[:, bass.ds((2 * c + b) * N, N)], m.bank[b][:, 0:N], ACT.Identity,
                                       bias=m.b_route[:, :]).then_inc(z_out, 1)

                def tile(g, b):
                    t = 2 * g + b
                    for r in range(2):
                        act.wait_ge(shifted, t + 1)
                        act.wait_ge(exp_done, 4 * g)
                        act.activation(scratch[:, b, r, :], m.bank[2 * b + r][:, 0:P], ACT.Exp,
                                       bias=one(shift[:, tiles(t), r:r + 1]),
                                       accum_out=one(total[:, tiles(t), r:r + 1])).then_inc(exp_done, 1)
                    for r in range(2):
                        act.wait_ge(hot_turned, 2 * t + r + 1)
                        act.activation(m.chosen[r][:, bass.ds(t * P, P)], m.bank[4 + 2 * r + b][:, 0:P],
                                       ACT.Copy).then_inc(hot_out, 1)

                over_tiles(act, tile)
                act.wait_ge(less, TILES)
                act.activation(m.w4[:, :, :, :], m.w4[:, :, :, :], ACT.Exp).then_inc(e4, 1)

            @block.vector
            def _(dve):
                dve.memset(four[:, :, :, :], LOWEST).then_inc(four_set, 1)
                dve.wait_ge(four_set, 1)

                def tile(g, b):
                    t = 2 * g + b
                    for r in range(2):
                        dve.wait_ge(logits_ready, 2 * t + r + 1).then_inc(passed, 1)
                        ins = dve.max(top8[:, b, r, :], m.bank[2 * b + r][:, 0:P])
                    ins.then_inc(top, 1)
                    dve.wait_ge(top, t + 1).then_inc(passed, 1)
                    for r in range(2):
                        ins = dve.max_index(index8[:, b, r, :], top8[:, b, r, :], m.bank[2 * b + r][:, 0:P])
                    ins.then_inc(index, 1)
                    dve.tensor_copy(four[:, b, :, 0:4], top8[:, b, :, 0:4]).then_inc(four_set, 1)
                    dve.tensor_tensor(m.w4[:, tiles(t), :, :].rearrange("q a r k -> q (a r) k"), top8[:, b, :, 0:4],
                                      top8[:, b, :, 0:1].broadcast_to([P, 2, 4]), ALU.subtract).then_inc(less, 1)
                    dve.wait_ge(four_set, t + 2).then_inc(passed, 1)
                    for r in range(2):
                        ins = dve.match_replace(marked[:, r, :], four[:, b, r, :], m.bank[2 * b + r][:, 0:P], HIGHEST)
                    ins.then_inc(mark, 1)
                    dve.tensor_scalar(one(shift[:, tiles(t), :]), top8[:, b, :, 0], -1.0, None, ALU.mult).then_inc(shifted, 1)
                    dve.wait_ge(index, t + 1)
                    dve.tensor_copy(m.index4[:, tiles(t), :, :].rearrange("q a r k -> q (a r) k"),
                                    index8[:, b, :, 0:4])
                    dve.wait_ge(mark, t + 1)
                    dve.wait_ge(hot_turned, 4 * g)
                    for r in range(2):
                        ins = dve.tensor_scalar(onehot[:, b, r, :], marked[:, r, :], HIGHEST, None, ALU.is_equal)\
                            .then_inc(hot, 1)

                over_tiles(dve, tile)

                dve.wait_ge(e4, 1)
                dve.reduce_sum(sum4[:, :, :], m.w4[:, :, :, :], AX.X).then_inc(dsum, 1)
                dve.wait_ge(dsum, 1)
                dve.scalar_tensor_tensor(sum4[:, :, :], total[:, :, :], 1e-8, sum4[:, :, :], ALU.mult,
                                         ALU.add).then_inc(denom, 1)
                dve.wait_ge(denom, 1)
                dve.reciprocal(sum4[:, :, :], sum4[:, :, :]).then_inc(inverse, 1)
                dve.wait_ge(inverse, 1)
                dve.tensor_tensor(m.w4[:, :, :, :], m.w4[:, :, :, :],
                                  sum4[:, :, :].unsqueeze(3).broadcast_to([P, TILES, 2, 4]), ALU.mult)


class ProjectionBias:

    def __init__(self, p, m):
        self.m = m
        self.ready, self.scaled = [p.sem("pb_" + n) for n in ("ready", "scaled")]

    def product(self, pe):
        m = self.m
        pe.wait_ge(m.sems["c_attn1"], m.n_attn1)
        for h in range(2):
            mm = pe.matmul(m.bank[7][:, 0:D], m.b_v1[:, h:h + 1].broadcast_to([DH, P]), m.w_proj1[:, h, :],
                           start=(h == 0), stop=(h == 1))
        mm.then_inc(self.ready, 1)

    def add(self, dve):
        m = self.m
        dve.wait_ge(m.sems["c_attn1"], m.n_attn1)
        dve.tensor_scalar(m.score_scale[:, :], m.score_scale[:, :], 0.01, None, ALU.max).then_inc(self.scaled, 1)
        dve.wait_ge(self.scaled, 1)
        dve.reciprocal(m.score_scale[:, :], m.score_scale[:, :]).then_inc(self.scaled, 1)
        dve.wait_ge(self.scaled, 2)
        dve.tensor_scalar(m.score_scale[:, :], m.score_scale[:, :], float(HEAD) ** -0.5, None, ALU.mult)
        dve.wait_ge(self.ready, 1)
        dve.tensor_tensor(m.r_bproj1[:, :], m.r_bproj1[:, :], m.bank[7][:, 0:D], ALU.add)


def assign_slots(nc, p, m, filled):
    names = ("counted", "masked", "step", "incl_ready", "begun_ready", "owner_ready", "turned", "zmax", "slots_out", "passed")
    counted, masked, step, incl_ready, begun_ready, owner_ready, turned, zmax, slots_out, passed = \
        [p.sem("slots_" + n) for n in names]
    sent, = p.software["scatter0_sent"]
    bias = ProjectionBias(p, m)
    with ExitStack() as mem:
        sb = lambda n, shape, dt=F32: mem.enter_context(nc.sbuf_tensor("slots_" + n, shape, dt))
        cum = m.cum
        tiles_f = sb("tiles_f", [P, 2])
        tiles_i = sb("tiles_i", [P, 2], I32)
        incl = sb("incl", [P, 2])
        base = sb("base", [P, 2])
        begun = sb("begun", [P, 2, SLOT_TILES])
        z8 = sb("z8", [P, GROUP, 8])
        rank = sb("rank", [P, TILES * 2, 4])
        pairs4 = sb("pairs4", [P, TILES * 2, 4, 4])
        w_new = sb("w_new", [P, TILES * 2, 4])

        with nc.Block() as block:

            @block.vector
            def _(dve):
                n = [0]

                def then(ins):
                    ins.then_inc(step, 1)
                    n[0] += 1
                    dve.wait_ge(step, n[0])

                for r in range(2):
                    col = slice(r, r + 1)
                    then(dve.tensor_tensor_scan(cum[r][:, :], m.chosen[r][:, :], m.chosen[r][:, :], 0.0, ALU.add, ALU.max))
                    then(dve.tensor_scalar(tiles_f[:, col], cum[r][:, PADDED - 1:PADDED], float(P - 1), None, ALU.add))
                    then(dve.tensor_copy(tiles_i[:, col], tiles_f[:, col]))
                    then(dve.tensor_scalar(tiles_i[:, col], tiles_i[:, col], P.bit_length() - 1, None, ALU.arith_shift_right))
                    dve.tensor_copy(tiles_f[:, col], tiles_i[:, col]).then_inc(counted, 1)
                    dve.wait_ge(incl_ready, r + 1)
                    then(dve.tensor_copy(incl[:, col], m.bank[0][:, 0:1]))
                    then(dve.tensor_tensor(base[:, col], incl[:, col], tiles_f[:, col], ALU.subtract))
                    then(dve.tensor_scalar(base[:, col], base[:, col], float(P), None, ALU.mult))
                    dve.scalar_tensor_tensor(cum[r][:, :], cum[r][:, :], base[:, col], m.chosen[r][:, :], ALU.add,
                                             ALU.mult).then_inc(masked, 1)
                    dve.tensor_scalar(begun[:, r, :], m.iota[:, 0:SLOT_TILES], incl[:, col], None, ALU.is_ge)\
                        .then_inc(begun_ready, 1)
                    dve.wait_ge(owner_ready, r + 1)
                    dve.tensor_scalar(m.owner[0:1, r * SLOT_TILES:(r + 1) * SLOT_TILES], m.bank[1][0:1, 0:SLOT_TILES],
                                      float(P - 1), None, ALU.min)

                    with dve.Fori(0, TURNS) as g:
                        for j in range(GROUP):
                            dve.wait_ge(turned, g * GROUP + (r * TILES + j + 1)).then_inc(passed, 1)
                            dve.max(z8[:, j, :], m.bank[2 + j][:, 0:P]).then_inc(zmax, 1)
                        dve.wait_ge(zmax, g * GROUP + (r * TILES + GROUP))
                        now = m.slots[:, tiles(g * GROUP, GROUP), r, :]
                        dve.tensor_scalar(now, z8[:, :, 0:4], -1.0, None, ALU.add).then_inc(slots_out, 1)
                        dve.wait_ge(slots_out, g + (r * TURNS + 1))

                idx = m.index4[:, :, :, :].rearrange("q t r k -> q (t r) k")
                w = m.w4[:, :, :, :].rearrange("q t r k -> q (t r) k")
                G4 = [P, TILES * 2, 4, 4]
                then(dve.tensor_tensor(pairs4[:, :, :, :], idx.unsqueeze(2).broadcast_to(G4),
                                       idx.unsqueeze(3).broadcast_to(G4), ALU.is_gt))
                then(dve.reduce_sum(rank[:, :, :], pairs4[:, :, :, :], AX.X))
                at = m.iota[:, 0:4].unsqueeze(1).unsqueeze(3).broadcast_to(G4)
                then(dve.tensor_tensor(pairs4[:, :, :, :], rank[:, :, :].unsqueeze(2).broadcast_to(G4), at, ALU.is_equal))
                then(dve.tensor_tensor(pairs4[:, :, :, :], pairs4[:, :, :, :], w.unsqueeze(2).broadcast_to(G4), ALU.mult))
                then(dve.reduce_sum(w_new[:, :, :], pairs4[:, :, :, :], AX.X))
                dve.tensor_copy(w, w_new[:, :, :])
                bias.add(dve)

            @block.gpsimd
            def _(pool):
                pool.wait_ge(*filled)
                for t in range(TILES):
                    if t % GROUP == 0:
                        pool.wait_ge(slots_out, t // GROUP + 1)
                    for k in range(4):
                        pool.indirect_dma_start(out=m.fk_in, out_offset=bass.IndirectOffsetOnAxis(
                            ap=m.slots[:, t, 0, k:k + 1], axis=0), in_=m.xn[:, t, :], in_offset=None).then_inc(sent, 16)
                pool.wait_ge(sent, 16 * 4 * TILES)

            @block.tensor
            def _(pe):
                for r in range(2):
                    pe.wait_ge(counted, r + 1)
                    pe.matmul(m.bank[0][:, 0:1], m.upto[:, :], tiles_f[:, r:r + 1], start=True, stop=True)\
                        .then_inc(incl_ready, 1)
                    pe.wait_ge(begun_ready, r + 1)
                    pe.matmul(m.bank[1][0:1, 0:SLOT_TILES], m.ones[:, 0:1], begun[:, r, :], start=True, stop=True)\
                        .then_inc(owner_ready, 1)
                    pe.wait_ge(masked, r + 1)
                    for t in range(TILES):
                        n = r * TILES + t
                        if n >= GROUP:
                            pe.wait_ge(zmax, n - GROUP + 1)
                        pe.transpose(m.bank[2 + t % GROUP][:, 0:P], cum[r][:, t * P:(t + 1) * P], m.ident[:, :])\
                            .then_inc(turned, 1)
                bias.product(pe)


def neuron_tiles(nc, p, m, r, slots_in, weights, slots_out, kh, kp, n):
    x_ready = [p.sem(f"nt{r}_x_ready{i}") for i in range(X_CHUNKS)]
    w_ready = [p.sem(f"nt{r}_w_ready{i}") for i in range(NT_RING)]
    turned, xt_out, o_ready, o_out = [p.sem(f"nt{r}_" + n) for n in ("turned", "xt_out", "o_ready", "o_out")]
    stored = p.software[f"nt{r}_stored"]
    K = kh * kp
    TURN = NT_RING
    PER = TURN // X_CHUNKS
    LOOPS = SLOT_TILES // TURN
    area = m.after_hidden()
    x = area(P, TURN * K).rearrange("q (t n) -> q t n", t=TURN)
    w = area(kp, TURN * kh * n).rearrange("q (t h n) -> q t h n", t=TURN, h=kh)
    xt = area(kp, TURN * kh * P).rearrange("q (t n) -> q t n", t=TURN)
    o = area(P, TURN * n).rearrange("q (t n) -> q t n", t=TURN)
    chunk = lambda dram, g, c: dram[bass.ds((g * TURN + c * PER) * P, PER * P), :].rearrange("(t q) d -> q t d", q=P)

    def turns(eng, turn):
        turn(0, None)
        with eng.Fori(0, LOOPS - 1) as g:
            turn(g + 1, g * TURN)

    with nc.Block() as block:

        @block.sync
        def _(sp):
            def turn(g, before):
                _, owners = nc.values_load_multi_w_load_instructions(
                    m.owner[0:1, bass.ds(r * SLOT_TILES + g * TURN, TURN)], engines=[mybir.EngineType.SP],
                    min_val=0, max_val=P - 1, skip_runtime_bounds_check_because="assign_slots clips owners")
                for j in range(TURN):
                    if before is not None:
                        sp.wait_ge(o_ready, before + j + 1)
                    sp.dma_start(w[:, j, :, :].rearrange("q h n -> q (h n)"),
                                 weights[bass.ds(owners[j], 1), :, :].rearrange("e q n -> q (e n)"))\
                        .then_inc(w_ready[j], 16)

            turns(sp, turn)

        @block.gpsimd
        def _(pool):
            with pool.Fori(0, LOOPS) as g:
                for c in range(X_CHUNKS):
                    pool.wait_ge(o_out, g * TURN + (c + 1) * PER)
                    pool.dma_start(chunk(slots_out, g, c), o[:, c * PER:(c + 1) * PER, :]).then_inc(stored[c], 16)
            for c in range(X_CHUNKS):
                pool.wait_ge(stored[c], 16 * LOOPS)

        @block.tensor
        def _(pe):
            AHEAD = 3

            def turn(g, j, first=False):
                pe.wait_ge(x_ready[j // PER], 16 * g + 16)
                if not first:
                    pe.wait_ge(xt_out, g * TURN + j - 3)
                for h in range(kh):
                    mm = pe.transpose(m.bank[j % 4][0:kp, h * P:(h + 1) * P], x[:, j, h * kp:(h + 1) * kp], m.ident[:, :])
                mm.then_inc(turned, 1)

            def product(g, j, first=False):
                pe.wait_ge(xt_out, g * TURN + j + 1)
                pe.wait_ge(w_ready[j], 16 * g + 16)
                if not first:
                    pe.wait_ge(o_out, g * TURN + j - 3)
                for h in range(kh):
                    mm = pe.matmul(m.bank[4 + j % 4][:, 0:n], xt[:, j, h * P:(h + 1) * P], w[:, j, h, :],
                                   start=(h == 0), stop=(h == kh - 1))
                mm.then_inc(o_ready, 1)

            for j in range(AHEAD):
                turn(0, j, True)
            for j in range(TURN):
                t = j + AHEAD
                turn(t // TURN, t % TURN, t < 4)
                product(0, j, j < 4)
            with pe.Fori(0, LOOPS - 2) as g:
                for j in range(TURN):
                    turn(g + (1 + (j + AHEAD) // TURN), (j + AHEAD) % TURN)
                    product(g + 1, j)
            for j in range(TURN):
                if j + AHEAD < TURN:
                    turn(LOOPS - 1, j + AHEAD)
                product(LOOPS - 1, j)

        @block.scalar
        def _(act):
            def load(g, c):
                act.dma_start(x[:, c * PER:(c + 1) * PER, :], chunk(slots_in, g, c)).then_inc(x_ready[c], 16)

            def turn(g, before, last=False):
                for j in range(TURN):
                    act.wait_ge(turned, g * TURN + j + 1)
                    if before is not None:
                        act.wait_ge(o_ready, before + j + 1)
                    act.activation(xt[:, j, :], m.bank[j % 4][0:kp, 0:kh * P], ACT.Copy).then_inc(xt_out, 1)
                    if (j + 1) % PER == 0 and not last:
                        load(g + 1, j // PER)

            for c in range(X_CHUNKS):
                load(0, c)
            turn(0, None)
            with act.Fori(0, LOOPS - 2) as g:
                turn(g + 1, g * TURN)
            turn(LOOPS - 1, (LOOPS - 2) * TURN, last=True)

        @block.vector
        def _(dve):
            def turn(g, before):
                for j in range(TURN):
                    if j % PER == 0 and before is not None:
                        dve.wait_ge(stored[j // PER], 16 * g)
                    dve.wait_ge(o_ready, g * TURN + j + 1)
                    dve.tensor_copy(o[:, j, :], m.bank[4 + j % 4][:, 0:n]).then_inc(o_out, 1)

            turns(dve, turn)


def combine(nc, p, m, r, slots_out, n, dst, scatter_to=None, filled=None):
    gathered = p.software[f"comb{r}_gathered"]
    sent, = p.software[f"comb{r}_sent"]
    step, summed, part, aggregated, stats, passed = [p.sem(f"comb{r}_" + n) for n in (
        "step", "summed", "part", "aggregated", "stats", "passed")]
    LAG = 3
    MIDDLE = 2
    last = scatter_to is None
    ln = LayerNorm(p, m, "n2", stats) if last else None
    qk = Projection(p, m, "qk1", m.w_qkv1, m.b_qk1, (m.sems["c_attn1"], m.n_attn1), ln.lifted,
                    late=LateProjection.TURNS) if last else None

    with nc.sbuf_tensor(f"comb{r}_rows", [P, GROUP, 4, n], F32) as rows, nc.Block() as block:

        @block.gpsimd
        def _(pool):

            def scatter(t):
                pool.wait_ge(summed, t + 1)
                for k in range(4):
                    pool.indirect_dma_start(out=scatter_to, out_offset=bass.IndirectOffsetOnAxis(
                        ap=m.slots[:, t, 1, k:k + 1], axis=0), in_=dst[:, t, :], in_offset=None).then_inc(sent, 16)

            if scatter_to is not None:
                pool.wait_ge(filled[0], filled[1])
            for t in range(TILES):
                if t >= GROUP:
                    pool.wait_ge(summed, t - GROUP + 1)
                for k in range(4):
                    pool.indirect_dma_start(out=rows[:, t % GROUP, k, :], out_offset=None, in_=slots_out,
                                            in_offset=bass.IndirectOffsetOnAxis(ap=m.slots[:, t, r, k:k + 1], axis=0))\
                        .then_inc(gathered[t % GROUP], 16)
                if scatter_to is not None and t >= LAG:
                    scatter(t - LAG)
                if ln and t >= GROUP and t % GROUP == MIDDLE:
                    ln.rstd(pool, t // GROUP - 1)
            if scatter_to is not None:
                for t in range(TILES - LAG, TILES):
                    scatter(t)
                pool.wait_ge(sent, 16 * 4 * TILES)
            if ln:
                ln.rstd(pool, TURNS - 1)

        @block.vector
        def _(dve):
            def group(g, normalise=None):
                for j in range(GROUP):
                    t = g * GROUP + j
                    out = one(dst[:, tiles(t), :])
                    dve.wait_ge(gathered[j], 64 * g + 64)
                    for k in range(4):
                        w = m.w4[:, tiles(t), r, k:k + 1].rearrange("q a k -> q (a k)")
                        if k == 0 and scatter_to is not None:
                            ins = dve.tensor_scalar(out, rows[:, j, k, :], w, None, ALU.mult)
                        else:
                            ins = dve.scalar_tensor_tensor(out, rows[:, j, k, :], w, out, ALU.mult, ALU.add)
                        if k < 3:
                            ins.then_inc(step, 1)
                            dve.wait_ge(step, 3 * t + k + 1)
                        else:
                            ins.then_inc(summed, 1)
                    if normalise and j == MIDDLE:
                        normalise()
                if ln:
                    row_statistics(dve, m, m.mv, g, (summed, g * GROUP + GROUP), part, aggregated, stats, passed)

            if ln:
                qk.clear_gaps(dve)
                group(0)
                with dve.Fori(0, TURNS - 1) as g:
                    group(g + 1, lambda: ln.rows(dve, g))
                ln.rows(dve, TURNS - 1)
            else:
                with dve.Fori(0, TURNS) as g:
                    group(g)

        if ln:

            @block.tensor
            def _(pe):
                for g in range(TURNS):
                    ln.turn(pe, g)
                    qk.project(pe, g)

            @block.scalar
            def _(act):
                for g in range(TURNS):
                    ln.lift(act, g)
                    qk.take(act, g)


def sparse_attention(nc, p, m):
    s = m.sems
    names = ("k_blocks", "scores_ready", "top1", "rest1", "top2", "rest2", "top3", "shift_ready", "mask_ready",
             "exp_ready", "kept_ready", "v_ready", "v_blocks", "probs_turned", "probs_out", "heads_ready", "inverse",
             "heads_scaled", "heads_turned", "heads_out", "cleared", "v_cleared", "scores_out", "passed")
    (k_blocks, scores_ready, top1, rest1, top2, rest2, top3, shift_ready, mask_ready, exp_ready, kept_ready, v_ready,
     v_blocks, probs_turned, probs_out, heads_ready, inverse_ready, heads_scaled, heads_turned, heads_out,
     cleared, v_cleared, scores_out, passed) = [p.sem("a1_" + n) for n in names]
    NH, HB = HEADS, HEADS // 2
    VC = 2 * HEAD + 2
    KEYS = HB * SEQ
    xn = m.xn[:, :, :].rearrange("q t d -> q (t d)")
    at = [0]

    def area(parts, n):
        at[0] += n
        assert at[0] <= TILES * D
        return xn[0:parts, at[0] - n:at[0]]

    with ExitStack() as mem:
        sb = lambda n, shape, dt=F32: mem.enter_context(nc.sbuf_tensor("a1_" + n, shape, dt))
        kb = sb("kb", [DH, 2, 2, 2, KEYS])
        work = area(P, NH * SEQ).rearrange("q (h k) -> q h k", h=NH)
        ex = [area(P, NH * SEQ).rearrange("q (h k) -> q h k", h=NH) for _ in range(2)]
        sc = [area(P, NH * SEQ).rearrange("q (h k) -> q h k", h=NH) for _ in range(2)]
        mask = [area(P, KEYS).bitcast(mybir.dt.bfloat16).rearrange("q (h k) -> q h k", h=NH) for _ in range(2)]
        kept = [area(P, NH * SLOT).rearrange("q (h k) -> q h k", h=NH), sb("kept", [P, NH, SLOT])]
        pt = m.spare[:, 0:HB * P].rearrange("q (j n) -> q j n", j=HB)
        vb = sb("vb", [P, 2, 2, HB, VC])
        top_a, top_b, top_c = [area(P, NH * 8).rearrange("q (h k) -> q h k", h=NH) for _ in range(3)]
        shift = sb("shift", [P, 2, NH])
        inverse = area(P, NH)
        o = area(P, D)
        S = [(m.bank[0], m.bank[1]), (m.bank[2], m.bank[3])]
        PT, V, O = (m.bank[4], m.bank[5]), m.bank[6], m.bank[7]
        late = LateProjection(p, m, PT[1])
        assert 2 + late.STEPS + 3 < late.FIRST_PAIR

        def score(u, h):
            return sc[u][:, h, :]

        with nc.Block() as block:

            @block.tensor
            def _(pe):
                def columns(x, c, i, b):
                    return x[:, c, (2 * i + 1 + b) * SLOT:(2 * i + 2 + b) * SLOT]

                def scores(i):
                    pe.wait_ge(k_blocks, i + 1)
                    if i >= 2:
                        pe.wait_ge(scores_out, i - 1)
                    for c in range(2):
                        for b in range(2):
                            mm = pe.matmul(S[i % 2][c][b * SLOT:(b + 1) * SLOT, 0:KEYS], columns(m.qt, c, i, b),
                                           kb[:, i % 2, b, c, :], start=True, stop=True)
                    mm.then_inc(scores_ready, 1)

                def values(i):
                    if i:
                        pe.wait_ge(v_blocks, i)
                    wv = m.w_qkv1[:, :, 2 * D:3 * D]
                    for c in range(2):
                        pe.matmul(V[:, 0:D], pair_columns(m.xs, c, i), wv[:, c, :], start=(c == 0), stop=(c == 1))
                    for b in range(2):
                        q = slice((1 - b) * SLOT, (2 - b) * SLOT)
                        for c in range(2):
                            mm = pe.matmul(V[q, D:2 * D], columns(m.xs, c, i, b), wv[:, c, :], start=(c == 0), stop=(c == 1))
                    mm.then_inc(v_ready, 1)

                def turn_probs(i):
                    pe.wait_ge(kept_ready, i + 1)
                    if i:
                        pe.wait_ge(probs_out, i)
                    if 2 <= i < 2 + late.STEPS:
                        pe.wait_ge(late.out, i - 1)
                    for j in range(HB):
                        mm = pe.transpose(PT[j // 4][:, (j % 4) * P:(j % 4 + 1) * P],
                                          kept[i % 2][:, 2 * j:2 * j + 2, :].rearrange("q h k -> q (h k)"), m.ident[:, :])
                    mm.then_inc(probs_turned, 1)

                def heads(i):
                    pe.wait_ge(probs_out, i + 1)
                    pe.wait_ge(v_blocks, i + 1)
                    if i:
                        pe.wait_ge(heads_out, i)
                    for j in range(HB):
                        for b in range(2):
                            q = slice(b * SLOT, (b + 1) * SLOT)
                            mm = pe.matmul(O[q, j * VC:(j + 1) * VC], pt[:, j, q], vb[:, i % 2, b, j, :], start=True, stop=True)
                    mm.then_inc(heads_ready, 1)

                def turn_heads(i):
                    pe.wait_ge(heads_scaled, i + 1)
                    for c in range(2):
                        mm = pe.transpose(O[0:DH, c * P:(c + 1) * P], o[:, c * DH:(c + 1) * DH], m.ident[:, :])
                    mm.then_inc(heads_turned, 1)

                scores(0)
                for i in range(PAIRS + 2):
                    if 1 <= i <= PAIRS:
                        turn_probs(i - 1)
                    if i >= 2:
                        turn_heads(i - 2)
                    if i + 1 < PAIRS:
                        scores(i + 1)
                    if 1 <= i <= PAIRS:
                        heads(i - 1)
                    if i < PAIRS:
                        values(i)
                    if 2 <= i < 2 + late.STEPS:
                        late.product(pe, i - 2)

            @block.gpsimd
            def _(pool):
                def blocks(i, u, first=False):
                    if not first:
                        pool.wait_ge(scores_ready, i - 1)
                    for b in range(2):
                        for c in range(2):
                            k = m.kt[:, c, bass.ds((2 * i + 1 + b) * SLOT, SEQ)]
                            ins = pool.tensor_tensor(kb[:, u, b, c, :].rearrange("q (h k) -> q h k", h=HB),
                                                     k.unsqueeze(1).broadcast_to([DH, HB, SEQ]),
                                                     m.head_mask[:, :].unsqueeze(2).broadcast_to([DH, HB, SEQ]), ALU.mult)
                    ins.then_inc(k_blocks, 1)

                def keep(i, u, first=False):
                    pool.wait_ge(mask_ready, i + 1)
                    pool.wait_ge(exp_ready, i + 1)
                    if not first:
                        pool.wait_ge(probs_turned, i - 1)
                    pool.tensor_tensor(kept[u][:, :, 0:SEQ], ex[u], mask[u], ALU.mult).then_inc(kept_ready, 1)

                blocks(0, 0, True)
                blocks(1, 1, True)
                for x in kept:
                    pool.memset(x[:, :, :], 0.0).then_inc(cleared, 1)
                pool.wait_ge(cleared, 2)
                for i in range(2):
                    blocks(i + 2, i)
                    keep(i, i, True)
                first_late = late.FIRST_PAIR // 2 - 2
                for turns in ((0, first_late), (first_late, PAIRS // 2 - 2)):
                    if turns[0]:
                        pool.wait_ge(late.out, late.STEPS)
                    with pool.Fori(*turns) as g:
                        for u in range(2):
                            i = 2 * g + 2 + u
                            blocks(i + 2, u)
                            keep(i, u)
                keep(PAIRS - 2, 0)
                keep(PAIRS - 1, 1)

            @block.vector
            def _(dve):
                def select(i, u):
                    half = [range(n * HB, (n + 1) * HB) for n in range(2)]

                    def largest(top, x, n, done):
                        for h in half[n]:
                            ins = dve.max(top[:, h, :], x(h))
                        ins.then_inc(done, 1)

                    def without(top, x, n, done):
                        for h in half[n]:
                            ins = dve.match_replace(work[:, h, :], top[:, h, :], x(h), LOWEST)
                        ins.then_inc(done, 1)

                    given = lambda h: score(u, h)
                    rest = lambda h: work[:, h, :]
                    dve.wait_ge(scores_out, i + 1).then_inc(passed, 1)
                    largest(top_a, given, 0, top1)
                    largest(top_a, given, 1, top1)
                    dve.wait_ge(top1, 2 * i + 1).then_inc(passed, 1)
                    without(top_a, given, 0, rest1)
                    dve.wait_ge(top1, 2 * i + 2)
                    dve.tensor_scalar(shift[:, u, :], top_a[:, :, 0], m.score_scale[:, 0:1], -1.0, ALU.mult,
                                      ALU.mult).then_inc(shift_ready, 1)
                    without(top_a, given, 1, rest1)
                    for n in range(2):
                        dve.wait_ge(rest1, 2 * i + n + 1).then_inc(passed, 1)
                        largest(top_b, rest, n, top2)
                    for n in range(2):
                        dve.wait_ge(top2, 2 * i + n + 1).then_inc(passed, 1)
                        without(top_b, rest, n, rest2)
                    for n in range(2):
                        dve.wait_ge(rest2, 2 * i + n + 1).then_inc(passed, 1)
                        largest(top_c, rest, n, top3)
                    dve.wait_ge(top3, 2 * i + 2)
                    if not (isinstance(i, int) and i == 0):
                        dve.wait_ge(kept_ready, i - 1)
                    dve.tensor_tensor(mask[u], sc[u], top_c[:, :, 7:8].broadcast_to([P, NH, SEQ]), ALU.is_ge)\
                        .then_inc(mask_ready, 1)

                def scale(i):
                    dve.wait_ge(heads_ready, i + 1)
                    got = O[:, 0:HB * VC].rearrange("q (j c) -> q j c", j=HB)
                    dve.reciprocal(inverse[:, :].rearrange("q (j e) -> q j e", e=2), got[:, :, 2 * HEAD:VC])\
                        .then_inc(inverse_ready, 1)
                    dve.wait_ge(inverse_ready, i + 1)
                    dve.wait_ge(heads_turned, i)
                    inv = inverse[:, :].rearrange("q (j e) -> q j e", e=2)
                    out = o[:, :].rearrange("q (j e d) -> q j e d", j=HB, e=2)
                    for e in range(2):
                        ins = dve.tensor_tensor(out[:, :, e, :], got[:, :, e * HEAD:(e + 1) * HEAD],
                                                inv[:, :, e:e + 1].broadcast_to([P, HB, HEAD]), ALU.mult)
                    ins.then_inc(heads_scaled, 1)

                select(0, 0)
                with dve.Fori(0, PAIRS // 2 - 1) as g:
                    for k in range(2):
                        i = 2 * g + 1 + k
                        select(i, 1 - k)
                        scale(i - 1)
                select(PAIRS - 1, 1)
                scale(PAIRS - 2)
                scale(PAIRS - 1)

            @block.scalar
            def _(act):
                act.activation(vb[:, :, :, :, :].rearrange("q a b j c -> q (a b j c)"),
                               m.zeros[:, 0:1].broadcast_to([P, 4 * HB * VC]), ACT.Copy).then_inc(v_cleared, 1)
                act.wait_ge(v_cleared, 1)
                flat = vb[:, :, :, :, :].rearrange("q a b j c -> q (a b j) c")
                for e in range(2):
                    q = slice(e * SLOT, (e + 1) * SLOT)
                    act.activation(flat[q, :, 2 * HEAD + e], m.ones[q, 0:1].broadcast_to([SLOT, 4 * HB]), ACT.Copy)

                def lift_scores(i, u):
                    act.wait_ge(scores_ready, i + 1)
                    for c in range(2):
                        ins = act.activation(sc[u][:, c * HB:(c + 1) * HB, :],
                                             S[u][c][:, 0:KEYS].rearrange("q (h k) -> q h k", h=HB), ACT.Copy)
                    ins.then_inc(scores_out, 1)

                def exps(i, u):
                    act.wait_ge(shift_ready, i + 1)
                    if not (isinstance(i, int) and i == 0):
                        act.wait_ge(kept_ready, i - 1)
                    for h in range(NH):
                        ins = act.activation(ex[u][:, h, :], score(u, h), ACT.Exp, bias=shift[:, u, h:h + 1],
                                             scale=m.score_scale[:, 0:1])
                    ins.then_inc(exp_ready, 1)

                def spread_values(i, u):
                    act.wait_ge(v_ready, i + 1)
                    if not (isinstance(i, int) and i == 0):
                        act.wait_ge(heads_ready, i - 1)
                    for e in range(2):
                        for b in range(2):
                            q = slice(e * SLOT, (e + 1) * SLOT)
                            src = V[q, (e != b) * D:(e != b) * D + D].rearrange("q (j e d) -> q j e d", j=HB, e=2)
                            ins = act.activation(vb[q, u, b, :, e * HEAD:(e + 1) * HEAD], src[:, :, e, :], ACT.Copy)
                    ins.then_inc(v_blocks, 1)

                def lift_probs(i):
                    act.wait_ge(probs_turned, i + 1)
                    act.wait_ge(heads_ready, i)
                    act.activation(pt[:, 0:4, :], PT[0][:, :].rearrange("q (j n) -> q j n", j=4), ACT.Copy)
                    act.activation(pt[:, 4:6, :], PT[1][:, 0:2 * P].rearrange("q (j n) -> q j n", j=2), ACT.Copy)\
                        .then_inc(probs_out, 1)

                def lift_heads(i):
                    act.wait_ge(heads_turned, i + 1)
                    src = O[0:DH, 0:2 * P].rearrange("q (h a k) -> q h a k", h=2, a=2)
                    dst = m.at[:, :, bass.ds(i * 2 * SEQ, 2 * SEQ)].rearrange("q h (a k) -> q h a k", a=2)
                    for h in range(2):
                        ins = act.activation(dst[:, h], src[:, h, :, 0:SEQ], ACT.Copy)
                    ins.then_inc(heads_out, 1)

                def pair(i, u, lag=2, last=False):
                    if lag >= 1:
                        lift_probs(i - 1)
                    if lag >= 2:
                        lift_heads(i - 2)
                    exps(i, u)
                    if not last:
                        lift_scores(i + 1, 1 - u)
                    spread_values(i, u)

                lift_scores(0, 0)
                pair(0, 0, lag=0)
                pair(1, 1, lag=1)
                for turn in range(len(late.TURNS)):
                    with act.Fori(0, 2) as g:
                        for k in range(2):
                            pair(2 * g + (4 * turn + 2 + k), k)
                            late.take(act, turn, 2 * g + k)
                with act.Fori(late.STEPS // 2, PAIRS // 2 - 2) as g:
                    for k in range(2):
                        pair(2 * g + 2 + k, k)
                pair(PAIRS - 2, 0)
                pair(PAIRS - 1, 1, last=True)
                lift_probs(PAIRS - 1)
                lift_heads(PAIRS - 2)
                lift_heads(PAIRS - 1)


def route_experts(nc, p, m):
    s = m.sems
    names = ("step", "less", "exp_ready", "spread", "turned", "rows_out", "enough", "over_ready",
             "valued", "back_turned", "counted", "before_ready")
    step, less, exp_ready, spread, turned, rows_out, enough, over_ready, valued, back_turned, \
        counted, before_ready = [p.sem("moe_" + n) for n in names]
    at = [0]

    def area(n):
        at[0] += n
        assert at[0] <= 6 * COLS
        return m.arena[:, at[0] - n:at[0]]

    E = EXPERTS
    C = P // E
    by_expert = lambda x: x.rearrange("q (t e) -> q t e", e=E)
    logits, probs, first = [by_expert(area(TILES * E)) for _ in range(3)]
    equal_all = by_expert(area(2 * C * E))
    equal = equal_all[:, 0:TILES, :]
    halves_q = area(2 * P).rearrange("q (u e c) -> q u e c", u=2, e=E)
    low, total, route = [area(TILES) for _ in range(3)]
    spread_q = area(TILES * P).rearrange("q (t e c) -> q t e c", t=TILES, e=E)
    rows, above_all = [area(PADDED) for _ in range(2)]
    halves, above, level, run = [area(2 * P) for _ in range(4)]
    lo, thr, count, over, room, level_at, part, before = [area(1) for _ in range(8)]
    value_all = area(2 * C)
    value = value_all[:, 0:TILES]
    BANKS = -(-TILES // 4)
    T8 = [P, TILES, E]

    with nc.Block() as block:

        @block.tensor
        def _(pe):
            pe.wait_ge(spread, 1)
            for t in range(TILES):
                mm = pe.transpose(m.bank[t // 4][:, (t % 4) * P:(t % 4 + 1) * P],
                                  spread_q[:, t, :, :].rearrange("q e c -> q (e c)"), m.ident[:, :])
                mm.then_inc(turned, 1)
            pe.wait_ge(rows_out, 1)
            for u in range(2):
                mm = pe.transpose(m.bank[0][:, u * P:(u + 1) * P], halves_q[:, u, :, :].rearrange("q e c -> q (e c)"),
                                  m.ident[:, :])
            mm.then_inc(turned, 1)
            for n in range(ROUNDS):
                pe.wait_ge(enough, n + 1)
                pe.matmul(m.bank[7][:, 0:1], m.group_ones[:, :], over, start=True, stop=True).then_inc(over_ready, 1)
            for n, weights in enumerate((m.group_ones, m.group_before, m.group_before)):
                pe.wait_ge(counted, n + 1)
                pe.matmul(m.bank[7][:, 0:1], weights[:, :], count, start=True, stop=True).then_inc(before_ready, 1)
            pe.wait_ge(valued, 1)
            for u in range(2):
                mm = pe.transpose(m.bank[0][:, u * P:(u + 1) * P], level[:, u * P:(u + 1) * P], m.ident[:, :])
            mm.then_inc(back_turned, 1)

        @block.scalar
        def _(act):
            act.wait_ge(less, 1)
            act.activation(probs, probs, ACT.Exp).then_inc(exp_ready, 1)
            for b in range(BANKS):
                n = min(4, TILES - 4 * b) * P
                act.wait_ge(turned, min(4 * b + 4, TILES))
                act.activation(rows[:, 4 * b * P:4 * b * P + n], m.bank[b][:, 0:n], ACT.Copy).then_inc(rows_out, 1)
            act.wait_ge(turned, TILES + 1)
            act.activation(halves, m.bank[0][:, 0:2 * P], ACT.Copy).then_inc(rows_out, 1)

        @block.vector
        def _(dve):
            n = [0]

            def then(ins):
                ins.then_inc(step, 1)
                n[0] += 1
                dve.wait_ge(step, n[0])

            dve.wait_ge(s["c_moe"], m.n_moe)
            then(dve.tensor_tensor(logits, m.bank[7][:, 0:TILES * E].rearrange("q (t e) -> q t e", e=E),
                                   m.r_switch[:, :].unsqueeze(1).broadcast_to(T8), ALU.add))
            then(dve.reduce_max(low, logits, AX.X))
            dve.tensor_tensor(probs, logits, low.unsqueeze(2).broadcast_to(T8), ALU.subtract).then_inc(less, 1)
            dve.wait_ge(exp_ready, 1)
            then(dve.reduce_sum(total, probs, AX.X))
            then(dve.reciprocal(total, total))
            then(dve.tensor_tensor(probs, probs, total.unsqueeze(2).broadcast_to(T8), ALU.mult))
            then(dve.reduce_max(m.prob_max[:, :], probs, AX.X))
            best = m.prob_max[:, :].unsqueeze(2).broadcast_to(T8)
            expert = m.iota[:, 0:E].unsqueeze(1).broadcast_to(T8)
            then(dve.tensor_tensor(equal, probs, best, ALU.is_lt))
            dve.memset(equal_all[:, TILES:2 * C, :], 0.0)
            then(dve.scalar_tensor_tensor(first, equal, float(E), expert, ALU.mult, ALU.add))
            then(dve.tensor_reduce(route, first, AX.X, ALU.min))
            then(dve.tensor_tensor(equal, expert, route.unsqueeze(2).broadcast_to(T8), ALU.is_equal))
            then(dve.tensor_tensor(equal, equal, best, ALU.mult))
            then(dve.memset(equal_all[LAST:P, TILES - 1, :], 0.0))
            dve.tensor_copy(halves_q, equal_all.rearrange("q (c u) e -> q u e c", u=2))
            dve.tensor_copy(spread_q.rearrange("q t e c -> q (t e) c"),
                            equal.rearrange("q t e -> q (t e)").unsqueeze(2).broadcast_to([P, TILES * E, C]))\
                .then_inc(spread, 1)

            dve.wait_ge(rows_out, BANKS + 1)
            now = slice(0, TOKENS)
            then(dve.memset(lo, 0.0))
            width = 2.0
            for r in range(ROUNDS):
                width /= C
                then(dve.scalar_tensor_tensor(thr, m.threshold[:, 0:1], width, lo, ALU.mult, ALU.add))
                then(dve.tensor_scalar(above_all[:, now], rows[:, now], thr, None, ALU.is_ge, ALU.add, accum_out=count))
                dve.tensor_scalar(over, count, float(CAPACITY), None, ALU.is_ge).then_inc(enough, 1)
                dve.wait_ge(over_ready, r + 1)
                then(dve.tensor_scalar(part, m.bank[7][:, 0:1], -1.0, width, ALU.add, ALU.mult))
                then(dve.tensor_tensor(lo, lo, part, ALU.add))
            then(dve.tensor_scalar(level_at, lo, 0.0, None, ALU.is_equal))
            then(dve.tensor_tensor(level_at, lo, level_at, ALU.subtract))
            dve.tensor_scalar(above, halves, lo, None, ALU.is_gt, ALU.add, accum_out=count).then_inc(counted, 1)
            dve.wait_ge(before_ready, 1)
            then(dve.tensor_scalar(room, m.bank[7][:, 0:1], -1.0, float(CAPACITY), ALU.mult, ALU.add))
            dve.tensor_scalar(level, halves, level_at, None, ALU.is_equal, ALU.add, accum_out=count).then_inc(counted, 1)
            dve.wait_ge(counted, 2)
            then(dve.tensor_tensor_scan(run, level, level, 0.0, ALU.add, ALU.max))
            dve.wait_ge(before_ready, 2)
            then(dve.tensor_tensor(room, room, m.bank[7][:, 0:1], ALU.subtract))
            then(dve.scalar_tensor_tensor(level, run, room, level, ALU.is_le, ALU.mult))
            then(dve.tensor_tensor(above, above, level, ALU.add))
            dve.reduce_sum(count, above, AX.X).then_inc(counted, 1)
            then(dve.tensor_tensor_scan(run, above, above, 0.0, ALU.add, ALU.max))
            dve.wait_ge(before_ready, 3)
            then(dve.tensor_tensor(before, m.slot_base[:, 0:1], m.bank[7][:, 0:1], ALU.add))
            dve.scalar_tensor_tensor(level, run, before, above, ALU.add, ALU.mult).then_inc(valued, 1)
            dve.wait_ge(back_turned, 1)
            then(dve.reduce_max(value_all.rearrange("q (c u) -> q u c", u=2),
                                m.bank[0][:, 0:2 * P].rearrange("q (u e c) -> q u c e", u=2, e=E), AX.X))
            then(dve.tensor_scalar(route, value, 0.0, None, ALU.is_equal))
            then(dve.tensor_tensor(low, value, route, ALU.add))
            then(dve.tensor_scalar(m.moe_row[:, :], low, -1.0, None, ALU.add))
            then(dve.tensor_tensor(low, route, m.own_row[:, :], ALU.mult))
            then(dve.tensor_tensor(value, value, low, ALU.add))
            then(dve.tensor_scalar(m.moe_slot[:, :], value, -1.0, None, ALU.add))
            then(dve.tensor_tensor(m.scale_xn[:, :], m.prob_max[:, :], route, ALU.mult))
            dve.tensor_tensor(m.scale_out[:, :], m.prob_max[:, :], m.scale_xn[:, :], ALU.subtract)


def scatter_to_experts(nc, p, m):
    sent, = p.software["moe_sent"]
    with nc.Block() as block:

        @block.gpsimd
        def _(pool):
            pool.wait_ge(m.sems["c_fill_moe"], 16)
            for t in range(TILES):
                pool.indirect_dma_start(out=m.moe_in, out_offset=bass.IndirectOffsetOnAxis(
                    ap=m.moe_slot[:, t:t + 1], axis=0), in_=m.xn[:, t, :], in_offset=None).then_inc(sent, 16)
            pool.wait_ge(sent, 16 * TILES)


def experts(nc, p, m, a):
    s = m.sems
    x_ready, w_ready = [[p.sem(f"ex_{n}{u}") for u in range(2)] for n in ("x_ready", "w_ready")]
    stored = p.software["ex_stored"]
    bias_ready = p.sem("ex_bias_ready")
    turned, xt_out, h_ready, h_out, o_ready, o_out = [p.sem("ex_" + n) for n in (
        "turned", "xt_out", "h_ready", "h_out", "o_ready", "o_out")]
    at = [0]

    def area(parts, n):
        at[0] += n
        assert at[0] <= 6 * COLS
        return m.arena[0:parts, at[0] - n:at[0]]

    ST = EXPERT_SLOTS // P
    FC = HIDDEN // P
    x = area(P, 2 * ST * D).rearrange("q (u t d) -> q u t d", u=2, t=ST)
    xt = area(DH, 2 * 2 * EXPERT_SLOTS).rearrange("q (u h n) -> q u h n", u=2, h=2)
    w1 = area(DH, 2 * 2 * HIDDEN).rearrange("q (u h n) -> q u h n", u=2, h=2)
    w2 = area(P, 2 * FC * D).rearrange("q (u f n) -> q u f n", u=2, f=FC)
    hid = area(P, FC * EXPERT_SLOTS).rearrange("q (f n) -> q f n", f=FC)
    o = area(P, 2 * ST * D).rearrange("q (u t d) -> q u t d", u=2, t=ST)
    r_down = area(P, EXPERTS * D)
    w1_dram = a["L1_ffn_w1"].rearrange("e (h q) n -> q e h n", h=2)
    w2_dram = a["L1_ffn_w2"].rearrange("e (f q) n -> q e f n", q=P)
    slots = lambda dram, e: dram[bass.ds(e * EXPERT_SLOTS, EXPERT_SLOTS), :].rearrange("(t q) d -> q t d", q=P)

    def weights_of(dram, e):
        return dram[:, bass.ds(e, 1), :, :].rearrange("q e h n -> q (e h) n")

    with nc.Block() as block:

        @block.sync
        def _(sp):
            def load(e, u, before):
                if before is not None:
                    sp.wait_ge(turned, (before + 1) * ST)
                sp.dma_start(x[:, u, :, :], slots(m.moe_in, e)).then_inc(x_ready[u], 16)
                if before is not None:
                    sp.wait_ge(h_ready, (before + 1) * FC)
                sp.dma_start(w1[:, u, :, :], weights_of(w1_dram, e)).then_inc(w_ready[u], 16)
                if before is not None:
                    sp.wait_ge(o_ready, (before + 1) * ST)
                sp.dma_start(w2[:, u, :, :], weights_of(w2_dram, e)).then_inc(w_ready[u], 16)

            for e in range(2):
                load(e, e, None)
            sp.dma_start(r_down, row_to_all(a["L1_ffn_b2"].rearrange("e d -> (e d)"), EXPERTS * D)).then_inc(bias_ready, 16)
            with sp.Fori(0, EXPERTS // 2 - 1) as g:
                for u in range(2):
                    load(2 * g + (2 + u), u, 2 * g + u)

        @block.gpsimd
        def _(pool):
            with pool.Fori(0, EXPERTS // 2) as g:
                for u in range(2):
                    pool.wait_ge(o_out, ST * (2 * g + u + 1))
                    pool.dma_start(slots(m.moe_out, 2 * g + u), o[:, u, :, :]).then_inc(stored[u], 16)
            for u in range(2):
                pool.wait_ge(stored[u], 16 * (EXPERTS // 2))

        @block.tensor
        def _(pe):
            def turn(g, u):
                e = 2 * g + u
                pe.wait_ge(x_ready[u], 16 * g + 16)
                for t in range(ST):
                    pe.wait_ge(xt_out, ST * e)
                    for h in range(2):
                        mm = pe.transpose(m.bank[h][0:DH, t * P:(t + 1) * P], x[:, u, t, h * DH:(h + 1) * DH], m.ident[:, :])
                    mm.then_inc(turned, 1)

            def up(g, u):
                e = 2 * g + u
                pe.wait_ge(xt_out, ST * (e + 1))
                pe.wait_ge(w_ready[u], 32 * g + 32)
                for f in range(FC):
                    pe.wait_ge(h_out, FC * e + (f - 1 if f >= 2 else 0))
                    for h in range(2):
                        mm = pe.matmul(m.bank[2 + f % 2][:, :], w1[:, u, h, f * P:(f + 1) * P], xt[:, u, h, :],
                                       start=(h == 0), stop=(h == 1))
                    mm.then_inc(h_ready, 1)

            def down(g, u):
                e = 2 * g + u
                pe.wait_ge(h_out, FC * (e + 1))
                pe.wait_ge(o_out, ST * e)
                for t in range(ST):
                    for f in range(FC):
                        mm = pe.matmul(m.bank[4 + t][:, 0:D], hid[:, f, t * P:(t + 1) * P], w2[:, u, f, :],
                                       start=(f == 0), stop=(f == FC - 1))
                    mm.then_inc(o_ready, 1)

            turn(0, 0)
            with pe.Fori(0, EXPERTS // 2 - 1) as g:
                for u in range(2):
                    up(g, u)
                    turn(g + u, 1 - u)
                    down(g, u)
            up(EXPERTS // 2 - 1, 0)
            turn(EXPERTS // 2 - 1, 1)
            down(EXPERTS // 2 - 1, 0)
            up(EXPERTS // 2 - 1, 1)
            down(EXPERTS // 2 - 1, 1)

        @block.scalar
        def _(act):
            with act.Fori(0, EXPERTS // 2) as g:
                for u in range(2):
                    e = 2 * g + u
                    act.wait_ge(o_ready, ST * e)
                    for f in range(FC):
                        act.wait_ge(h_ready, FC * e + f + 1)
                        act.activation(hid[:, f, :], m.bank[2 + f % 2][:, :], ACT.Gelu,
                                       bias=m.b_up[:, bass.ds(e, 1), f]).then_inc(h_out, 1)

        @block.vector
        def _(dve):
            def lift_x(e, u):
                dve.wait_ge(turned, ST * (e + 1))
                for h in range(2):
                    ins = dve.tensor_copy(xt[:, u, h, :], m.bank[h][0:DH, :])
                ins.then_inc(xt_out, ST)

            def rows(g, u):
                dve.wait_ge(stored[u], 16 * g)
                for t in range(ST):
                    dve.wait_ge(o_ready, ST * (2 * g + u) + t + 1)
                    dve.tensor_tensor(o[:, u, t, :], m.bank[4 + t][:, 0:D], r_down[:, bass.ds((2 * g + u) * D, D)],
                                      ALU.add).then_inc(o_out, 1)

            lift_x(0, 0)
            dve.wait_ge(bias_ready, 16)
            with dve.Fori(0, EXPERTS // 2 - 1) as g:
                for u in range(2):
                    lift_x(2 * g + u + 1, 1 - u)
                    rows(g, u)
            lift_x(EXPERTS - 1, 1)
            rows(EXPERTS // 2 - 1, 0)
            rows(EXPERTS // 2 - 1, 1)


def finish(nc, p, m, out):
    gathered = p.software["fin_gathered"]
    first, second = [p.sem("fin_" + n) for n in ("first", "second")]
    stored = m.sems["out_stored"]
    rows = m.arena[:, 0:GROUP * D].rearrange("q (j d) -> q j d", j=GROUP)
    with nc.Block() as block:

        @block.gpsimd
        def _(pool):
            for t in range(TILES):
                if t >= GROUP:
                    pool.wait_ge(second, t - GROUP + 1)
                pool.indirect_dma_start(out=rows[:, t % GROUP, :], out_offset=None, in_=m.moe_out,
                                        in_offset=bass.IndirectOffsetOnAxis(ap=m.moe_row[:, t:t + 1], axis=0))\
                    .then_inc(gathered[t % GROUP], 16)

        @block.vector
        def _(dve):
            with dve.Fori(0, TURNS) as g:
                for j in range(GROUP):
                    t = g * GROUP + j
                    h = one(m.h[:, tiles(t), :])
                    dve.scalar_tensor_tensor(h, one(m.xn[:, tiles(t), :]), m.scale_xn[:, tiles(t)], h, ALU.mult,
                                             ALU.add).then_inc(first, 1)
                for j in range(GROUP):
                    t = g * GROUP + j
                    h = one(m.h[:, tiles(t), :])
                    dve.wait_ge(gathered[j], 16 * g + 16)
                    dve.wait_ge(first, g * GROUP + GROUP)
                    dve.scalar_tensor_tensor(h, rows[:, j, :], m.scale_out[:, tiles(t)], h, ALU.mult,
                                             ALU.add).then_inc(second, 1)

        @block.sync
        def _(sp):
            with sp.Fori(0, TURNS - 1) as g:
                sp.wait_ge(second, g * GROUP + GROUP)
                sp.dma_start(out[bass.ds(g * GROUP * P, GROUP * P), :].rearrange("(j q) d -> q j d", q=P),
                             m.h[:, tiles(g * GROUP, GROUP), :]).then_inc(stored, 16)
            sp.wait_ge(second, TILES)
            t0 = (TURNS - 1) * GROUP
            sp.dma_start(out[t0 * P:(TILES - 1) * P, :].rearrange("(j q) d -> q j d", q=P),
                         m.h[:, t0:TILES - 1, :]).then_inc(stored, 16)
            sp.dma_start(out[(TILES - 1) * P:TOKENS, :], m.h[0:LAST, TILES - 1, :]).then_inc(stored, 16)
            sp.wait_ge(stored, 16 * (TURNS + 1))


class Memory:

    def after_hidden(self):
        at = [PADDED]

        def area(parts, n):
            at[0] += n
            assert at[0] <= 6 * COLS
            return self.arena[0:parts, at[0] - n:at[0]]
        return area



def build(nc, a, out):
    with ExitStack() as ctx:
        p = Program(nc, ctx)
        m = Memory()
        m.sems = {}
        m.bank = [p.bank(f"bank{i}") for i in range(8)]
        m.h = p.sb("h", [P, TILES, D])
        m.xn = p.sb("xn", [P, TILES, D])
        m.xn_patches = m.xn[:, :, :].rearrange("q t d -> q (t d)")[:, 0:GROUP * PATCH].rearrange("q (j d) -> q j d", j=GROUP)
        m.xt = p.sb("xt", [DH, 2, PADDED])
        m.arena = p.sb("arena", [P, 6 * COLS])
        m.x_all = m.arena[:, 0:TILES * PATCH].rearrange("q (t d) -> q t d", t=TILES)
        m.mv = p.sb("mv", [P, TILES, 2])
        m.mv2 = p.sb("mv2", [P, TILES, 2])
        m.rstd = p.sb("rstd", [P, TILES])
        m.rstd2 = p.sb("rstd2", [P, TILES])
        m.shift = p.sb("shift", [P, TILES])
        m.bn = p.sb("bn", [P, 128])
        m.mv_group = p.sb("mv_group", [P, GROUP, 2])
        m.minus_half = p.sb("minus_half", [P, TILES])
        m.ident = p.sb("ident", [P, P])
        m.g1 = p.sb("g1", [P, PCH])
        m.b1 = p.sb("b1", [P, PCH])
        m.r_btok = p.sb("r_btok", [P, D])
        m.r_g2 = p.sb("r_g2", [P, D])
        m.r_b2 = p.sb("r_b2", [P, D])
        m.n_attn0 = 0
        m.qt, m.kt, m.xs = [m.arena[0:DH, i * 2 * COLS:(i + 1) * 2 * COLS].rearrange("q (h n) -> q h n", h=2)
                            for i in range(3)]
        m.qk = m.arena[0:DH, 0:4 * COLS]
        m.at = m.xt
        m.pair_row = p.sb("pair_row", [2, P])
        m.pair_bar = p.sb("pair_bar", [2, P])
        m.spare = p.sb("spare", [P, 6 * D])
        m.w_qkv0 = m.spare[0:DH, :].rearrange("q (h n) -> q h n", h=2)
        m.w_gp = p.sb("w_gp", [DH, 2, SEQ])
        m.w_proj0 = p.sb("w_proj0", [DH, 2, D])
        m.b_qk0 = p.sb("b_qk0", [DH, 4])
        m.alpha = p.sb("alpha", [P, 1])
        m.r_bv0 = p.sb("r_bv0", [P, D])
        m.r_bproj0 = p.sb("r_bproj0", [P, D])
        m.n_moe = 0
        m.w_switch = p.sb("w_switch", [DH, 2, EXPERTS])
        m.r_switch = p.sb("r_switch", [P, EXPERTS])
        m.b_up = p.sb("b_up", [P, EXPERTS, HIDDEN // P])
        m.group_ones = p.sb("group_ones", [P, P])
        m.group_before = p.sb("group_before", [P, P])
        m.threshold, m.slot_base = [p.sb(n, [P, 1]) for n in ("threshold", "slot_base")]
        m.own_row = p.sb('own_row', [P, TILES])
        m.prob_max, m.scale_xn, m.scale_out = [p.sb(n, [P, TILES]) for n in ("prob_max", "scale_xn", "scale_out")]
        m.moe_slot = p.sb("moe_slot", [P, TILES], U32)
        m.moe_row = p.sb("moe_row", [P, TILES], U32)
        m.moe_in = nc.dram_tensor("moe_in", [MOE_SLOTS + 1 + PADDED, D], F32).ap()
        m.moe_out = nc.dram_tensor("moe_out", [MOE_SLOTS, D], F32).ap()
        m.n_attn1 = 0
        m.w_qkv1 = p.sb("w_qkv1", [DH, 2, 3 * D])
        m.w_proj1 = p.sb("w_proj1", [DH, 2, D])
        m.b_qk1 = p.sb("b_qk1", [DH, 4])
        m.b_v1 = p.sb("b_v1", [DH, 2])
        m.r_bproj1 = p.sb("r_bproj1", [P, D])
        m.score_scale = p.sb("score_scale", [P, 1])
        m.head_mask = p.sb("head_mask", [DH, HEADS // 2])
        m.n_ffn0 = 0
        m.plus_half = p.sb("plus_half", [P, 2])
        m.ones = p.sb("ones", [P, 2])
        m.zeros = p.sb("zeros", [P, D])
        m.iota = p.sb("iota", [P, 2 * P])
        m.upto = p.sb("upto", [P, P])
        m.w_route = p.sb("w_route", [DH, 2, 2 * R2])
        m.b_route = p.sb("b_route", [2 * R2, 1])
        m.emb = p.sb("emb", [P, 2 * R2])
        m.emb_t = p.sb("emb_t", [2 * R2, NEURONS])
        m.w4 = p.sb("w4", [P, TILES, 2, 4])
        m.index4 = p.sb("index4", [P, TILES, 2, 4])
        m.slots = p.sb("slots", [P, TILES, 2, 4], U32)
        m.owner = p.sb("owner", [1, 2 * SLOT_TILES], I32)
        m.zt = m.arena[:, 0:PADDED]
        m.chosen = [m.arena[:, (1 + r) * PADDED:(2 + r) * PADDED] for r in range(2)]
        m.cum = [m.arena[:, (3 + r) * PADDED:(4 + r) * PADDED] for r in range(2)]
        m.hidden = m.arena[:, 0:PADDED].rearrange("q (t n) -> q t n", t=TILES)
        m.fk_in = nc.dram_tensor("fk_in", [SLOT_TILES * P, D], F32).ap()
        m.fk_out = nc.dram_tensor("fk_out", [SLOT_TILES * P, NEURONS], F32).ap()
        m.rk_in = nc.dram_tensor("rk_in", [SLOT_TILES * P, NEURONS], F32).ap()
        m.rk_out = nc.dram_tensor("rk_out", [SLOT_TILES * P, D], F32).ap()
        n = TILES * PATCH
        m.xt_patches = m.arena[:, n:n + GROUP * PATCH].rearrange("q (j d) -> q j d", j=GROUP)
        n += GROUP * PATCH
        m.w_tok = m.arena[:, n:n + PCH * D].rearrange("q (c d) -> q c d", c=PCH)
        p.stage(load_constants, m, a)
        p.stage(patch_tokens, m, a)
        p.stage(token_norm, m)
        p.stage(group_attention, m)
        p.stage(output_projection, m, "proj0", m.w_proj0, m.r_bproj0)
        p.stage(route, m)
        filled = (m.sems["c_fill"], 32)
        p.stage(assign_slots, m, filled)
        p.stage(neuron_tiles, m, 0, m.fk_in, a["L0_ffn_f_know"], m.fk_out, 2, DH, NEURONS)
        p.stage(combine, m, 0, m.fk_out, NEURONS, m.hidden, m.rk_in, filled)
        p.stage(neuron_tiles, m, 1, m.rk_in, a["L0_ffn_r_know"], m.rk_out, 1, P, D)
        p.stage(combine, m, 1, m.rk_out, D, m.h)
        p.stage(sparse_attention, m)
        p.stage(output_projection, m, "proj1", m.w_proj1, m.r_bproj1, m.w_switch)
        p.stage(route_experts, m)
        p.stage(scatter_to_experts, m)
        p.stage(experts, m, a)
        p.stage(finish, m, out)


def _layouts(inputs):
    import numpy as np

    a = {n: np.ascontiguousarray(v) for n, v in inputs.items()}
    grid, side = 7, 16
    patches = a["x"].reshape(IMAGES, 3, grid, side, grid, side).transpose(0, 2, 4, 3, 5, 1)
    a["x"] = patches.reshape(TOKENS, PATCH)
    for n in ("L0_tok_ln1_g", "L0_tok_ln1_b"):
        a[n] = a[n].reshape(PCH, P).T
    a["L0_attn_b_qkv_cols"] = a["L0_attn_b_qkv"][:2 * D].reshape(4, DH).T
    a["L1_attn_qkv_w"], a["L1_attn_proj_w"] = a["L1_attn_qkv_w"].T, a["L1_attn_proj_w"].T
    a["L1_attn_qkv_b"] = a["L1_attn_qkv_b"].reshape(6, DH).T
    a["L0_ffn_f_know"] = a["L0_ffn_f_know"].reshape(NEURONS, 2, DH, NEURONS).transpose(0, 2, 1, 3).reshape(NEURONS, DH, 2 * NEURONS)
    a["L1_ffn_b1"] = a["L1_ffn_b1"].reshape(EXPERTS, HIDDEN // P, P).transpose(2, 0, 1)

    q = np.arange(P)
    columns = np.stack([q < SLOT, q >= SLOT])
    a["c_pair_row"] = columns.astype(np.float32)
    a["c_pair_bar"] = np.where(columns & (q % SLOT < SEQ), 0.0, -1e30).astype(np.float32)
    a["c_iota"] = np.arange(2 * P).astype(np.float32)
    a["c_upto"] = np.triu(np.ones((P, P), np.float32))
    a["c_head_mask"] = (np.arange(DH)[:, None] // HEAD == np.arange(HEADS // 2)).astype(np.float32)
    per_expert = P // EXPERTS
    a["c_group_ones"] = (q[:, None] // per_expert == q // per_expert).astype(np.float32)
    a["c_group_before"] = np.triu(a["c_group_ones"], 1)
    a["c_threshold"] = (q % per_expert).astype(np.float32)[:, None]
    a["c_slot_base"] = (q // per_expert * EXPERT_SLOTS).astype(np.float32)[:, None]
    a["c_own_row"] = (MOE_SLOTS + 1 + q[:, None] + P * np.arange(TILES)).astype(np.float32)
    return {n: np.ascontiguousarray(v) for n, v in a.items()}


def kernel(**inputs):
    import numpy as np
    import concourse.bacc as bacc
    from concourse.bass_utils import run_bass_kernel_spmd

    nc = bacc.Bacc("TRN2", target_bir_lowering=False, num_devices=1)
    arrays = _layouts(inputs)
    a = {n: nc.dram_tensor(n, v.shape, mybir.dt.from_np(v.dtype), kind="ExternalInput").ap() for n, v in arrays.items()}
    out = nc.dram_tensor("out", (TOKENS, D), F32, kind="ExternalOutput").ap()
    build(nc, a, out)
    r = run_bass_kernel_spmd(nc, [arrays], core_ids=[0])
    return r.results[0]["out"].reshape(IMAGES, SEQ, D)
```
